# Optimizing a Trainium2 kernel written in Bass

```python
import numpy as np
import jax
import jax.numpy as jnp

def _softmax(x, axis=-1):
    return jax.nn.softmax(x, axis=axis)

def _gelu(x):
    return jax.nn.gelu(x, approximate=True)

def _silu(x):
    return jax.nn.silu(x)

def _sigmoid(x):
    return jax.nn.sigmoid(x)

def _layernorm(x, axis=-1, eps=1e-05):
    m = jnp.mean(x, axis=axis, keepdims=True)
    v = jnp.var(x, axis=axis, keepdims=True)
    return (x - m) / jnp.sqrt(v + eps)

def _scatter_add(tgt, idx, src, axis=0):
    return tgt.at[idx].add(src)

def _segment_sum(src, seg, n):
    return jax.ops.segment_sum(src, seg, n)
kernel_name = 'mk_perceiver_d2_seqx_r8_cfcf96'

def setup_inputs(seed: int=0):
    np.random.seed(seed)
    _w = jnp.asarray

    def _rec_inputs():
        import jax
        import jax.numpy as jnp
        _rk = jax.random.key(seed)
        x = -0.0003929 + 0.9999 * jax.random.normal(jax.random.fold_in(_rk, 1), (2, 128, 256), jnp.float32)
        _lenS = 128 - jax.random.randint(jax.random.fold_in(_rk, 7), (2,), 0, max(1, 128 // 4) + 1, jnp.int32)
        _lenS2 = 2048 - jax.random.randint(jax.random.fold_in(_rk, 8), (2,), 0, max(1, 2048 // 4) + 1, jnp.int32)
        _ctx_1024P = jax.random.normal(jax.random.fold_in(_rk, 11), (2, 16, 128), jnp.float32)
        _ctx_1024c = jax.random.dirichlet(jax.random.fold_in(_rk, 511), 0.3 * jnp.ones((16,), jnp.float32), (2, 2048))
        _ctx_1024t = jnp.einsum('bsk,bkd->bsd', _ctx_1024c, _ctx_1024P)
        _ctx_1024t = _ctx_1024t * jax.lax.rsqrt(jnp.mean(jnp.square(_ctx_1024t)) + 1e-12) * 0.953939
        ctx_1024 = 0.000227908 + 0.99994 * (_ctx_1024t + 0.3 * jax.random.normal(jax.random.fold_in(_rk, 611), (2, 2048, 128), jnp.float32))
        return (x, ctx_1024)
    x, ctx_1024 = _rec_inputs()

    def _L0_xattn_setup():
        import jax, jax.numpy as jnp
        import numpy as np
        EPS = 1e-05

        def rmsnorm(x, g, eps=EPS):
            var = jnp.mean(jnp.square(x), axis=-1, keepdims=True)
            return x * jax.lax.rsqrt(var + eps) * g
        key = jax.random.key(seed)
        ks = jax.random.split(key, 8)
        B, Sq, Skv = (2, 512, 64)
        dim, cdim, H, D = (256, 128, 16, 128)
        inner = H * D
        s = lambda f: 1.0 / np.sqrt(f)
        return {'hidden_states': jax.random.normal(ks[0], (B, Sq, dim), jnp.float32), 'encoder_hidden_states': jax.random.normal(ks[1], (B, Skv, cdim), jnp.float32), 'Wq': jax.random.normal(ks[2], (dim, inner), jnp.float32) * s(dim), 'Wk': jax.random.normal(ks[3], (cdim, inner), jnp.float32) * s(cdim), 'Wv': jax.random.normal(ks[4], (cdim, inner), jnp.float32) * s(cdim), 'Wo': jax.random.normal(ks[5], (inner, dim), jnp.float32) * s(inner), 'gq': jnp.ones((D,), jnp.float32), 'gk': jnp.ones((D,), jnp.float32)}
    _L0_xattn_all = _L0_xattn_setup()
    _L0_xattn_in = {k: v for k, v in _L0_xattn_all.items() if k in ('Wq', 'Wk', 'Wv', 'Wo', 'gq', 'gk')}
    del _L0_xattn_all

    def _L0_attn_setup():
        import jax, jax.numpy as jnp
        import numpy as np
        import math
        N_HEADS = 16
        D_EMBED = 256
        D_HEAD = D_EMBED // N_HEADS
        BATCH = 2
        SEQ = 256
        CAUSAL = True
        key = jax.random.key(seed)
        k_x, k_wi, k_wo = jax.random.split(key, 3)
        scale = 1.0 / math.sqrt(D_EMBED)
        return {'x': jax.random.normal(k_x, (BATCH, SEQ, D_EMBED), dtype=jnp.float32), 'w_in': jax.random.normal(k_wi, (D_EMBED, 3 * D_EMBED), dtype=jnp.float32) * scale, 'b_in': jnp.zeros((3 * D_EMBED,), dtype=jnp.float32), 'w_out': jax.random.normal(k_wo, (D_EMBED, D_EMBED), dtype=jnp.float32) * scale, 'b_out': jnp.zeros((D_EMBED,), dtype=jnp.float32)}
    _L0_attn_all = _L0_attn_setup()
    _L0_attn_in = {k: v for k, v in _L0_attn_all.items() if k in ('w_in', 'b_in', 'w_out', 'b_out')}
    del _L0_attn_all

    def _L0_ffn_setup():
        import jax, jax.numpy as jnp
        import numpy as np
        EPS = 1e-05

        def rms_norm(x):
            return x * jax.lax.rsqrt(jnp.mean(x * x, axis=-1, keepdims=True) + EPS)

        def act_quant(x):
            scale = 127.0 / jnp.clip(jnp.max(jnp.abs(x), axis=-1, keepdims=True), 1e-05)
            q = jnp.clip(jnp.round(x * scale), -128.0, 127.0) / scale
            return x + jax.lax.stop_gradient(q - x)

        def weight_quant(w):
            scale = 1.0 / jnp.clip(jnp.mean(jnp.abs(w)), 1e-05)
            q = jnp.clip(jnp.round(w * scale), -1.0, 1.0) / scale
            return w + jax.lax.stop_gradient(q - w)

        def bitlinear158(x, w, b):
            xq = act_quant(rms_norm(x))
            wq = weight_quant(w)
            return jnp.einsum('bsd,od->bso', xq, wq) + b

        def layer_norm(x, g, b):
            mu = jnp.mean(x, axis=-1, keepdims=True)
            var = jnp.mean((x - mu) ** 2, axis=-1, keepdims=True)
            return (x - mu) * jax.lax.rsqrt(var + EPS) * g + b
        key = jax.random.key(seed)
        ks = jax.random.split(key, 3)
        d, inner = (256, 1024)
        x = jax.random.normal(ks[0], (4, 256, d), dtype=jnp.float32)
        w1 = jax.random.normal(ks[1], (inner, d), dtype=jnp.float32) * 0.02
        b1 = jnp.zeros((inner,), jnp.float32)
        ln_g = jnp.ones((inner,), jnp.float32)
        ln_b = jnp.zeros((inner,), jnp.float32)
        w2 = jax.random.normal(ks[2], (d, inner), dtype=jnp.float32) * 0.02
        b2 = jnp.zeros((d,), jnp.float32)
        return {'x': x, 'w1': w1, 'b1': b1, 'ln_g': ln_g, 'ln_b': ln_b, 'w2': w2, 'b2': b2}
    _L0_ffn_all = _L0_ffn_setup()
    _L0_ffn_in = {k: v for k, v in _L0_ffn_all.items() if k in ('w1', 'b1', 'ln_g', 'ln_b', 'w2', 'b2')}
    del _L0_ffn_all

    def _L1_xattn_setup():
        import jax, jax.numpy as jnp
        import numpy as np
        B, S1, S2, DCA = (2, 256, 128, 16)
        QDIM, KDIM, H = (256, 128, 16)
        HD = QDIM // H
        SCALE = HD ** (-0.5)
        EPS = 1e-06
        DCA_WEIGHT = 1.0

        def _ln(t, w, b):
            m = jnp.mean(t, axis=-1, keepdims=True)
            v = jnp.var(t, axis=-1, keepdims=True)
            return (t - m) * jax.lax.rsqrt(v + EPS) * w + b

        def _attn(q, k, v):
            s = jnp.einsum('bhqd,bhkd->bhqk', q, k) * SCALE
            p = jax.nn.softmax(s, axis=-1)
            return jnp.einsum('bhqk,bhkd->bhqd', p, v)
        key = jax.random.key(seed)
        ks = jax.random.split(key, 8)
        w = lambda k, shape: jax.random.normal(k, shape, jnp.float32) * 0.02
        return {'x': jax.random.normal(ks[0], (B, S1, QDIM), jnp.float32), 'y': jax.random.normal(ks[1], (B, S2 + DCA, KDIM), jnp.float32), 'Wq': w(ks[2], (QDIM, QDIM)), 'bq': jnp.zeros((QDIM,), jnp.float32), 'Wk': w(ks[3], (KDIM, QDIM)), 'bk': jnp.zeros((QDIM,), jnp.float32), 'Wv': w(ks[4], (KDIM, QDIM)), 'bv': jnp.zeros((QDIM,), jnp.float32), 'Wkv_dca': w(ks[5], (KDIM, 2 * QDIM)), 'bkv_dca': jnp.zeros((2 * QDIM,), jnp.float32), 'qn_w': jnp.ones((HD,), jnp.float32), 'qn_b': jnp.zeros((HD,), jnp.float32), 'kn_w': jnp.ones((HD,), jnp.float32), 'kn_b': jnp.zeros((HD,), jnp.float32), 'kn_dca_w': jnp.ones((HD,), jnp.float32), 'kn_dca_b': jnp.zeros((HD,), jnp.float32), 'Wo': w(ks[6], (QDIM, QDIM)), 'bo': jnp.zeros((QDIM,), jnp.float32)}
    _L1_xattn_all = _L1_xattn_setup()
    _L1_xattn_in = {k: v for k, v in _L1_xattn_all.items() if k in ('Wq', 'bq', 'Wk', 'bk', 'Wv', 'bv', 'Wkv_dca', 'bkv_dca', 'qn_w', 'qn_b', 'kn_w', 'kn_b', 'kn_dca_w', 'kn_dca_b', 'Wo', 'bo')}
    del _L1_xattn_all

    def _L1_attn_setup():
        import jax, jax.numpy as jnp
        import numpy as np
        HIDDEN = 256
        KEY = 256
        EPS = 1e-05
        key = jax.random.key(seed)
        k1, k2, k3 = jax.random.split(key, 3)
        B, S = (4, 256)
        x = jax.random.normal(k1, (B, S, HIDDEN), dtype=jnp.float32)
        bq = 1.0 / np.sqrt(HIDDEN)
        qkv = jax.random.uniform(k2, (HIDDEN, KEY * 3), minval=-bq, maxval=bq, dtype=jnp.float32)
        bo = 1.0 / np.sqrt(KEY)
        o_proj = jax.random.uniform(k3, (KEY, HIDDEN), minval=-bo, maxval=bo, dtype=jnp.float32)
        gamma = jnp.ones((HIDDEN,), dtype=jnp.float32)
        beta = jnp.zeros((HIDDEN,), dtype=jnp.float32)
        return {'x': x, 'qkv': qkv, 'o_proj': o_proj, 'gamma': gamma, 'beta': beta}
    _L1_attn_all = _L1_attn_setup()
    _L1_attn_in = {k: v for k, v in _L1_attn_all.items() if k in ('qkv', 'o_proj', 'gamma', 'beta')}
    del _L1_attn_all

    def _L1_ffn_setup():
        import jax, jax.numpy as jnp
        import numpy as np
        TOP_K = 4
        NUM_EXPERTS = 16
        key = jax.random.key(seed)
        ks = jax.random.split(key, 6)
        B, S, H, I, E = (2, 128, 256, 224, NUM_EXPERTS)
        return {'x': jax.random.normal(ks[0], (B, S, H), dtype=jnp.float32), 'router_w': jax.random.normal(ks[1], (E, H), dtype=jnp.float32) * 0.02, 'expert_bias': jnp.zeros((E,), dtype=jnp.float32), 'gate_proj': jax.random.normal(ks[2], (E, H, I), dtype=jnp.float32) * 0.02, 'up_proj': jax.random.normal(ks[3], (E, H, I), dtype=jnp.float32) * 0.02, 'down_proj': jax.random.normal(ks[4], (E, I, H), dtype=jnp.float32) * 0.02}
    _L1_ffn_all = _L1_ffn_setup()
    _L1_ffn_in = {k: v for k, v in _L1_ffn_all.items() if k in ('router_w', 'expert_bias', 'gate_proj', 'up_proj', 'down_proj')}
    del _L1_ffn_all
    return {'x': x, 'ctx_1024': ctx_1024, 'L0_xattn_Wq': _L0_xattn_in['Wq'], 'L0_xattn_Wk': _L0_xattn_in['Wk'], 'L0_xattn_Wv': _L0_xattn_in['Wv'], 'L0_xattn_Wo': _L0_xattn_in['Wo'], 'L0_xattn_gq': _L0_xattn_in['gq'], 'L0_xattn_gk': _L0_xattn_in['gk'], 'L0_attn_w_in': _L0_attn_in['w_in'], 'L0_attn_b_in': _L0_attn_in['b_in'], 'L0_attn_w_out': _L0_attn_in['w_out'], 'L0_attn_b_out': _L0_attn_in['b_out'], 'L0_ffn_w1': _L0_ffn_in['w1'], 'L0_ffn_b1': _L0_ffn_in['b1'], 'L0_ffn_ln_g': _L0_ffn_in['ln_g'], 'L0_ffn_ln_b': _L0_ffn_in['ln_b'], 'L0_ffn_w2': _L0_ffn_in['w2'], 'L0_ffn_b2': _L0_ffn_in['b2'], 'L1_xattn_Wq': _L1_xattn_in['Wq'], 'L1_xattn_bq': _L1_xattn_in['bq'], 'L1_xattn_Wk': _L1_xattn_in['Wk'], 'L1_xattn_bk': _L1_xattn_in['bk'], 'L1_xattn_Wv': _L1_xattn_in['Wv'], 'L1_xattn_bv': _L1_xattn_in['bv'], 'L1_xattn_Wkv_dca': _L1_xattn_in['Wkv_dca'], 'L1_xattn_bkv_dca': _L1_xattn_in['bkv_dca'], 'L1_xattn_qn_w': _L1_xattn_in['qn_w'], 'L1_xattn_qn_b': _L1_xattn_in['qn_b'], 'L1_xattn_kn_w': _L1_xattn_in['kn_w'], 'L1_xattn_kn_b': _L1_xattn_in['kn_b'], 'L1_xattn_kn_dca_w': _L1_xattn_in['kn_dca_w'], 'L1_xattn_kn_dca_b': _L1_xattn_in['kn_dca_b'], 'L1_xattn_Wo': _L1_xattn_in['Wo'], 'L1_xattn_bo': _L1_xattn_in['bo'], 'L1_attn_qkv': _L1_attn_in['qkv'], 'L1_attn_o_proj': _L1_attn_in['o_proj'], 'L1_attn_gamma': _L1_attn_in['gamma'], 'L1_attn_beta': _L1_attn_in['beta'], 'L1_ffn_router_w': _L1_ffn_in['router_w'], 'L1_ffn_expert_bias': _L1_ffn_in['expert_bias'], 'L1_ffn_gate_proj': _L1_ffn_in['gate_proj'], 'L1_ffn_up_proj': _L1_ffn_in['up_proj'], 'L1_ffn_down_proj': _L1_ffn_in['down_proj']}

def reference(x, ctx_1024, L0_xattn_Wq, L0_xattn_Wk, L0_xattn_Wv, L0_xattn_Wo, L0_xattn_gq, L0_xattn_gk, L0_attn_w_in, L0_attn_b_in, L0_attn_w_out, L0_attn_b_out, L0_ffn_w1, L0_ffn_b1, L0_ffn_ln_g, L0_ffn_ln_b, L0_ffn_w2, L0_ffn_b2, L1_xattn_Wq, L1_xattn_bq, L1_xattn_Wk, L1_xattn_bk, L1_xattn_Wv, L1_xattn_bv, L1_xattn_Wkv_dca, L1_xattn_bkv_dca, L1_xattn_qn_w, L1_xattn_qn_b, L1_xattn_kn_w, L1_xattn_kn_b, L1_xattn_kn_dca_w, L1_xattn_kn_dca_b, L1_xattn_Wo, L1_xattn_bo, L1_attn_qkv, L1_attn_o_proj, L1_attn_gamma, L1_attn_beta, L1_ffn_router_w, L1_ffn_expert_bias, L1_ffn_gate_proj, L1_ffn_up_proj, L1_ffn_down_proj):
    import jax
    import jax.numpy as jnp

    def _L0_xattn_ref(hidden_states, encoder_hidden_states, Wq, Wk, Wv, Wo, gq, gk):
        import jax, jax.numpy as jnp
        import numpy as np
        EPS = 1e-05

        def rmsnorm(x, g, eps=EPS):
            var = jnp.mean(jnp.square(x), axis=-1, keepdims=True)
            return x * jax.lax.rsqrt(var + eps) * g
        B, Sq, _ = hidden_states.shape
        Skv = encoder_hidden_states.shape[1]
        D = gq.shape[0]
        H = Wq.shape[1] // D
        scale = 1.0 / np.sqrt(D)
        q = (hidden_states @ Wq).reshape(B, Sq, H, D)
        k = (encoder_hidden_states @ Wk).reshape(B, Skv, H, D)
        v = (encoder_hidden_states @ Wv).reshape(B, Skv, H, D)
        q = rmsnorm(q, gq)
        k = rmsnorm(k, gk)
        scores = jnp.einsum('bqhd,bkhd->bhqk', q, k) * scale
        attn = jax.nn.softmax(scores, axis=-1)
        out = jnp.einsum('bhqk,bkhd->bqhd', attn, v)
        out = out.reshape(B, Sq, H * D)
        return out @ Wo

    def _L0_attn_ref(x, w_in, b_in, w_out, b_out):
        import jax, jax.numpy as jnp
        import numpy as np
        import math
        N_HEADS = 16
        D_EMBED = 256
        D_HEAD = D_EMBED // N_HEADS
        BATCH = 2
        SEQ = 256
        CAUSAL = True
        B, S, D = x.shape
        qkv = x @ w_in + b_in
        q, k, v = jnp.split(qkv, 3, axis=-1)
        q = q.reshape(B, S, N_HEADS, D_HEAD)
        k = k.reshape(B, S, N_HEADS, D_HEAD)
        v = v.reshape(B, S, N_HEADS, D_HEAD)
        scores = jnp.einsum('bqhd,bkhd->bhqk', q, k)
        if CAUSAL:
            causal = jnp.tril(jnp.ones((S, S), dtype=bool))
            scores = jnp.where(causal, scores, -jnp.inf)
        scores = scores * (1.0 / math.sqrt(D_HEAD))
        probs = jax.nn.softmax(scores, axis=-1)
        out = jnp.einsum('bhqk,bkhd->bqhd', probs, v)
        out = out.reshape(B, S, D)
        return out @ w_out + b_out

    def _L0_ffn_ref(x, w1, b1, ln_g, ln_b, w2, b2):
        import jax, jax.numpy as jnp
        import numpy as np
        EPS = 1e-05

        def rms_norm(x):
            return x * jax.lax.rsqrt(jnp.mean(x * x, axis=-1, keepdims=True) + EPS)

        def act_quant(x):
            scale = 127.0 / jnp.clip(jnp.max(jnp.abs(x), axis=-1, keepdims=True), 1e-05)
            q = jnp.clip(jnp.round(x * scale), -128.0, 127.0) / scale
            return x + jax.lax.stop_gradient(q - x)

        def weight_quant(w):
            scale = 1.0 / jnp.clip(jnp.mean(jnp.abs(w)), 1e-05)
            q = jnp.clip(jnp.round(w * scale), -1.0, 1.0) / scale
            return w + jax.lax.stop_gradient(q - w)

        def bitlinear158(x, w, b):
            xq = act_quant(rms_norm(x))
            wq = weight_quant(w)
            return jnp.einsum('bsd,od->bso', xq, wq) + b

        def layer_norm(x, g, b):
            mu = jnp.mean(x, axis=-1, keepdims=True)
            var = jnp.mean((x - mu) ** 2, axis=-1, keepdims=True)
            return (x - mu) * jax.lax.rsqrt(var + EPS) * g + b
        h = jax.nn.silu(bitlinear158(x, w1, b1))
        h = jax.nn.gelu(h, approximate=False)
        h = layer_norm(h, ln_g, ln_b)
        return bitlinear158(h, w2, b2)

    def _L1_xattn_ref(x, y, Wq, bq, Wk, bk, Wv, bv, Wkv_dca, bkv_dca, qn_w, qn_b, kn_w, kn_b, kn_dca_w, kn_dca_b, Wo, bo):
        import jax, jax.numpy as jnp
        import numpy as np
        B, S1, S2, DCA = (2, 256, 128, 16)
        QDIM, KDIM, H = (256, 128, 16)
        HD = QDIM // H
        SCALE = HD ** (-0.5)
        EPS = 1e-06
        DCA_WEIGHT = 1.0

        def _ln(t, w, b):
            m = jnp.mean(t, axis=-1, keepdims=True)
            v = jnp.var(t, axis=-1, keepdims=True)
            return (t - m) * jax.lax.rsqrt(v + EPS) * w + b

        def _attn(q, k, v):
            s = jnp.einsum('bhqd,bhkd->bhqk', q, k) * SCALE
            p = jax.nn.softmax(s, axis=-1)
            return jnp.einsum('bhqk,bhkd->bhqd', p, v)
        b, s1, _ = x.shape
        y_dca = y[:, -DCA:, :]
        y_main = y[:, :-DCA, :]
        kv_dca = (y_dca @ Wkv_dca + bkv_dca).reshape(b, DCA, 2, H, HD)
        k_dca = _ln(kv_dca[:, :, 0], kn_dca_w, kn_dca_b)
        v_dca = kv_dca[:, :, 1]
        s2 = y_main.shape[1]
        q = _ln((x @ Wq + bq).reshape(b, s1, H, HD), qn_w, qn_b)
        kv = jnp.concatenate([y_main @ Wk + bk, y_main @ Wv + bv], axis=-1)
        kv = kv.reshape(b, s2, H, 2 * HD)
        k = _ln(kv[..., :HD], kn_w, kn_b)
        v = kv[..., HD:]
        qT = q.transpose(0, 2, 1, 3)
        ctx = _attn(qT, k.transpose(0, 2, 1, 3), v.transpose(0, 2, 1, 3))
        ctx = ctx.transpose(0, 2, 1, 3).reshape(b, s1, QDIM)
        ctx_dca = _attn(qT, k_dca.transpose(0, 2, 1, 3), v_dca.transpose(0, 2, 1, 3))
        ctx_dca = ctx_dca.transpose(0, 2, 1, 3).reshape(b, s1, QDIM)
        ctx = ctx + DCA_WEIGHT * ctx_dca
        return ctx @ Wo + bo

    def _L1_attn_ref(x, qkv, o_proj, gamma, beta):
        import jax, jax.numpy as jnp
        import numpy as np
        HIDDEN = 256
        KEY = 256
        EPS = 1e-05
        residual = x
        mu = jnp.mean(x, axis=-1, keepdims=True)
        var = jnp.mean((x - mu) ** 2, axis=-1, keepdims=True)
        x_norm = (x - mu) / jnp.sqrt(var + EPS) * gamma + beta
        q = x_norm @ qkv[:, :KEY]
        k = x_norm @ qkv[:, KEY:2 * KEY]
        v = x_norm @ qkv[:, 2 * KEY:]
        scale = 1.0 / jnp.sqrt(jnp.float32(KEY))
        scores = jnp.einsum('bsk,btk->bst', q, k) * scale
        S_len = x.shape[1]
        causal = jnp.tril(jnp.ones((S_len, S_len), dtype=bool))
        scores = jnp.where(causal[None], scores, -jnp.inf)
        attn = jax.nn.softmax(scores, axis=-1)
        out = attn @ v
        out = out @ o_proj
        return out + residual

    def _L1_ffn_ref(x, router_w, expert_bias, gate_proj, up_proj, down_proj):
        import jax, jax.numpy as jnp
        import numpy as np
        TOP_K = 4
        NUM_EXPERTS = 16
        logits = jnp.einsum('bsh,eh->bse', x, router_w) + expert_bias
        scores = jax.nn.softmax(logits, axis=-1)
        top_w, top_idx = jax.lax.top_k(scores, TOP_K)
        top_w = top_w / jnp.sum(top_w, axis=-1, keepdims=True)
        g = jnp.einsum('bsh,khe->bske', x, gate_proj)
        u = jnp.einsum('bsh,khe->bske', x, up_proj)
        act = jax.nn.silu(g) * u
        out = jnp.einsum('bske,keh->bskh', act, down_proj)
        sel = jnp.take_along_axis(out, top_idx[..., None], axis=2)
        return jnp.sum(sel * top_w[..., None], axis=2)
    x = x + _L0_xattn_ref(_layernorm(x, axis=-1), ctx_1024, L0_xattn_Wq, L0_xattn_Wk, L0_xattn_Wv, L0_xattn_Wo, L0_xattn_gq, L0_xattn_gk)
    x = x + _L0_attn_ref(_layernorm(x, axis=-1), L0_attn_w_in, L0_attn_b_in, L0_attn_w_out, L0_attn_b_out)
    x = x + _L0_ffn_ref(_layernorm(x, axis=-1), L0_ffn_w1, L0_ffn_b1, L0_ffn_ln_g, L0_ffn_ln_b, L0_ffn_w2, L0_ffn_b2)
    x = x + _L1_xattn_ref(_layernorm(x, axis=-1), ctx_1024, L1_xattn_Wq, L1_xattn_bq, L1_xattn_Wk, L1_xattn_bk, L1_xattn_Wv, L1_xattn_bv, L1_xattn_Wkv_dca, L1_xattn_bkv_dca, L1_xattn_qn_w, L1_xattn_qn_b, L1_xattn_kn_w, L1_xattn_kn_b, L1_xattn_kn_dca_w, L1_xattn_kn_dca_b, L1_xattn_Wo, L1_xattn_bo)
    x = x + _L1_attn_ref(_layernorm(x, axis=-1), L1_attn_qkv, L1_attn_o_proj, L1_attn_gamma, L1_attn_beta)
    x = x + _L1_ffn_ref(_layernorm(x, axis=-1), L1_ffn_router_w, L1_ffn_expert_bias, L1_ffn_gate_proj, L1_ffn_up_proj, L1_ffn_down_proj)
    return x

_drawn_inputs = setup_inputs


def setup_inputs(seed=0):
    import zlib

    import numpy as np

    out = dict(_drawn_inputs(seed))
    spreads = {'L0_xattn_gq': (1.0, 0.2),
     'L0_xattn_gk': (1.0, 0.2),
     'L0_attn_b_in': (0.0, 0.1),
     'L0_attn_b_out': (0.0, 0.1),
     'L0_ffn_b1': (0.0, 0.1),
     'L0_ffn_ln_g': (1.0, 0.2),
     'L0_ffn_ln_b': (0.0, 0.1),
     'L0_ffn_b2': (0.0, 0.1),
     'L1_xattn_bq': (0.0, 0.8),
     'L1_xattn_bk': (0.0, 0.46),
     'L1_xattn_bv': (0.0, 0.491),
     'L1_xattn_bkv_dca': (0.0, 0.31),
     'L1_xattn_qn_w': (1.0, 0.6),
     'L1_xattn_qn_b': (0.0, 0.8),
     'L1_xattn_kn_w': (1.0, 0.6),
     'L1_xattn_kn_b': (0.0, 0.8),
     'L1_xattn_kn_dca_w': (1.0, 0.6),
     'L1_xattn_kn_dca_b': (0.0, 0.8),
     'L1_xattn_bo': (0.0, 0.1),
     'L1_attn_gamma': (1.0, 0.6),
     'L1_attn_beta': (0.0, 0.576),
     'L1_ffn_expert_bias': (0.0, 0.8)}
    factors = {'L1_xattn_Wq': 3.495,
     'L1_xattn_Wk': 2.744,
     'L1_xattn_Wv': 2.974,
     'L1_ffn_router_w': 8.0,
     'L1_ffn_gate_proj': 8.0,
     'L1_ffn_up_proj': 8.0,
     'L1_ffn_down_proj': 8.0}
    for name, (base, spread) in spreads.items():
        noise = np.random.default_rng([zlib.crc32(name.encode()), seed]).standard_normal(out[name].shape)
        drawn = base * np.exp(spread * noise) if base else spread * noise
        out[name] = jnp.asarray(drawn.astype(out[name].dtype))
    for name, factor in factors.items():
        out[name] = (out[name] * factor).astype(out[name].dtype)
    return out
```

```python
from contextlib import ExitStack

import numpy as np
import concourse.bass as bass
from concourse import mybir

F32 = mybir.dt.float32
F32R = mybir.dt.float32r
BF16 = mybir.dt.bfloat16
ALU = mybir.AluOpType
ACT = mybir.ActivationFunctionType
AX = mybir.AxisListType

P = 128
EPS = 1e-5


def build(nc, a, out, upto=6):
    B, S, D = a["x"].shape
    KV = a["ctx_1024"].shape[1]
    C = a["ctx_1024"].shape[2]
    H = 16
    HD0 = a["L0_xattn_gq"].shape[0]
    NC = KV // P
    KC = D // P
    G = 4
    NG = H // G
    assert S == P and C == P and HD0 == P

    ctx = ExitStack()
    with ctx:
        def sb(name, shape, dt=F32):
            return ctx.enter_context(nc.sbuf_tensor(name, shape, dt))

        def sem(name):
            return ctx.enter_context(nc.semaphore(name))

        ps = ctx.enter_context(nc.psum_tensor("ps", [P, 8, 512], F32))

        ident = sb("ident", [P, P])
        ones = sb("ones", [P, P])
        neg_half = sb("neg_half", [P, 32])
        x_sb = sb("x_sb", [P, B, D])
        stats = sb("stats", [P, B, 6])
        meanvar = sb("meanvar", [P, B, 2])
        veps = sb("veps", [P, B])
        rstd = sb("rstd", [P, B])
        xn = sb("xn", [P, B, D])
        xnT = sb("xnT", [P, KC, B * S])
        ctx_nat = sb("ctx_nat", [P, B * NC, C + 2])
        KB = 1024
        ARENA = 168 * KB
        arena_start = nc.sbuf_base
        arena = sb("arena", [P, ARENA // 4])
        base = -(-arena_start // 32) * 32

        def at(name, offset, shape, dt=F32):
            size = int(np.prod(shape[1:])) * mybir.dt.size(dt)
            assert offset + size <= ARENA
            return nc.alloc_sbuf_tensor_at(name, shape, dt, offset=base + offset)

        ctxT_hi = at("ctxT_hi", 0, [P, B * NC, P], F32R)
        ctxT_lo = at("ctxT_lo", 16 * KB, [P, B * NC, P], F32R)
        wk_hi = at("wk_hi", 32 * KB, [P, H * HD0], F32R)
        wk_lo = at("wk_lo", 40 * KB, [P, H * HD0], F32R)
        wk = at("wk", 48 * KB, [P, H * HD0])
        s_sb = at("s_sb", 48 * KB, [P, 2, 2, 512])
        wkT = at("wkT", 56 * KB, [P, H, C])
        p_sb = at("p_sb", 56 * KB, [P, 2, 2, 512])
        q3_hi = at("q3_hi", 64 * KB, [P, B, H, S], F32R)
        q3_lo = at("q3_lo", 80 * KB, [P, B, H, S], F32R)
        wq = at("wq", 96 * KB, [P, KC, H * HD0])
        wv = at("wv", 112 * KB, [P, H, HD0])
        wo = at("wo", 120 * KB, [P, H, D])
        qn = at("qn", 136 * KB, [P, B, H, HD0])
        qT = at("qT", 152 * KB, [P, H, B * S])
        gains = sb("gains", [P, 2])
        gqk = sb("gqk", [P, 1])
        sq = sb("sq", [P, 2, 512])
        q_ss = sb("q_ss", [P, B, H])
        q_rstd = sb("q_rstd", [P, B, H])
        k_ss = sb("k_ss", [P, B * NC, H])
        k_rstd = sb("k_rstd", [P, B * NC, H])
        shift = sb("shift", [P, 1])
        o_den = sb("o_den", [P, B * NG, G])
        o_n = qn
        oT = qT
        aT = wq[:, :, :].rearrange("p k (h s) -> p (k h) s", s=B * S)

        HD = D // H
        w_in = at("w_in", 0, [P, KC, 3 * D])
        w_out = at("w_out", 6 * KB, [P, KC, D])
        bqk = sb("bqk", [P, 2 * KC])
        b_in_row = at("b_in_row", 16 * KB, [1, 3 * D])
        b_out_row = at("b_out_row", 19 * KB, [1, D])
        head_mask = sb("head_mask", [P, 8])
        causal = at("causal", 28 * KB, [P, S])
        sa_s = at("sa_s", 152 * KB, [P, B, H, S])
        sa_qT = at("sa_qT", 120 * KB, [P, KC, B * S])
        sa_kT = at("sa_kT", 122 * KB, [P, KC, B * S])
        sa_km = at("sa_km", 124 * KB, [P, 2, 8, S])
        sa_v = at("sa_v", 132 * KB, [P, B, H, HD + 2])
        sa_o = at("sa_o", 135 * KB, [P, B, D])
        sa_oT = at("sa_oT", 137 * KB, [P, KC, B * S])
        sa_pT = at("sa_pT", 48 * KB, [P, B, H, S])
        sa_max = sb("sa_max", [P, B, H])
        sa_den = sb("sa_den", [P, B, H])
        FI = a["L0_ffn_w1"].shape[0]
        FC = FI // P
        w1 = at("w1", 32 * KB, [P, FC, D])
        w2 = at("w2", 40 * KB, [P, KC, FI])
        w1qT = at("w1qT", 139 * KB, [P, KC, FI], BF16)
        w2qT = at("w2qT", 143 * KB, [P, FC, D], BF16)
        b1_all = at("b1_all", 8 * KB, [P, FI])
        lng_all = at("lng_all", 12 * KB, [P, FI])
        lnb_all = at("lnb_all", 24 * KB, [P, FI])
        b2_all = at("b2_all", 20 * KB, [P, D])
        w_abs = sb("w_abs", [P, 2])
        w_mean = sb("w_mean", [P, 2])
        w_scale = sb("w_scale", [P, 2])
        ff_ss = sb("ff_ss", [P, 2, B])
        ff_r = sb("ff_r", [P, 2, B])
        ff_max = sb("ff_max", [P, 2, B])
        ff_s = sb("ff_s", [P, 2, B])
        ff_dq = sb("ff_dq", [P, 2, B])
        ff_q1 = at("ff_q1", 128 * KB, [P, B, D])
        ff_sq = at("ff_sq", 152 * KB, [P, B, FI])
        ff_qT1 = at("ff_qT1", 130 * KB, [P, KC, B * S], BF16)
        ff_h = at("ff_h", 48 * KB, [P, B, FI])
        ff_h2 = at("ff_h2", 56 * KB, [P, B, FI])
        ff_qT2 = at("ff_qT2", 124 * KB, [P, FC, B * S], BF16)
        ff_stats = sb("ff_stats", [P, B, 2, 6])
        ff_mv = sb("ff_mv", [P, B, 2])
        ff_rstd = sb("ff_rstd", [P, B])

        DCA = 16
        assert DCA == NC
        PAIRS = H // 2
        W = 64
        NU = NC // 2
        EPS2 = 1e-6
        SC = float(HD) ** -0.5
        xb_cT = at("xb_cT", 0, [P, NC, P])
        xb_kn = at("xb_kn", 0, [P, NC, 2, W], F32R)
        xb_kv = at("xb_kv", 8 * KB, [P, NC, H, 2 * HD + 1])
        xb_p = at("xb_p", 42 * KB, [P, 2, 4, S])
        xb_qn = at("xb_qn", 46 * KB, [P, H, W], F32R)
        xb_qT1 = at("xb_qT1", 50 * KB, [P, PAIRS, S], F32R)
        xb_qT2 = at("xb_qT2", 54 * KB, [P, 2, 2 * S], F32R)
        xb_kt = at("xb_kt", 56 * KB, [P, NC, 2, HD])
        xb_oh = at("xb_oh", 56 * KB, [P, 4 * S])
        xb_kT = at("xb_kT", 152 * KB, [P, 2, NC, P], F32R)
        xb_wkv = at("xb_wkv", 120 * KB, [P, 2 * D])
        xb_bkv = at("xb_bkv", 122 * KB, [P, 2 * D])
        xb_wq = at("xb_wq", 124 * KB, [P, KC, D])
        xb_wo = at("xb_wo", 126 * KB, [P, KC, D])
        xb_wd = at("xb_wd", 128 * KB, [P, 2 * D])
        xb_bd = at("xb_bd", 130 * KB, [P, 2 * D])
        xb_bq = at("xb_bq", 132 * KB, [P, D])
        xb_q = at("xb_q", 133 * KB, [P, B, D])
        xb_qk = at("xb_qk", 135 * KB, [P, B, D])
        xb_t = at("xb_t", 137 * KB, [P, B, D])
        xb_qfT = at("xb_qfT", 139 * KB, [P, KC, B * S])
        xb_kd = at("xb_kd", 141 * KB, [P, B, 2 * D])
        xb_kdm = at("xb_kdm", 145 * KB, [P, B, 2 * D])
        xb_kdT = at("xb_kdT", 149 * KB, [P, B, KC, P])
        xb_wo_row = at("xb_wo_row", 151 * KB, [1, D])
        xb_yd = sb("xb_yd", [DCA, B, C])
        xb_ydT = sb("xb_ydT", [P, B, 8, DCA])
        xb_pd = at("xb_pd", 58 * KB, [P, B, D])
        xb_pdT = at("xb_pdT", 60 * KB, [P, KC, B * S])
        xb_o = at("xb_o", 62 * KB, [P, B, D])
        eps2 = sb("eps2", [P, 1])
        xb_vec = sb("xb_vec", [P, 6, HD])
        xb_ss = sb("xb_ss", [P, NC, H])
        xb_rk = sb("xb_rk", [P, NC, H])
        xb_s32 = sb("xb_s32", [P, 4, B * H])
        xb_d32 = sb("xb_d32", [P, 4, B * H])
        xb_qb = sb("xb_qb", [P, B * H])
        xb_pm = sb("xb_pm", [P, 2, 8])
        xb_m = sb("xb_m", [P, 2, 2])
        xb_den = sb("xb_den", [P, B, H])

        sb_w = at("sb_w", 0, [P, KC, 3 * D])
        sb_wo = at("sb_wo", 6 * KB, [P, KC, D])
        sb_g = at("sb_g", 8 * KB, [P, 2, D])
        sb_h = at("sb_h", 10 * KB, [P, B, D])
        sb_hT = at("sb_hT", 12 * KB, [P, KC, B * S])
        sb_qT = at("sb_qT", 14 * KB, [P, KC, B * S])
        sb_kT = at("sb_kT", 16 * KB, [P, KC, B * S])
        sb_v = at("sb_v", 18 * KB, [P, B, D])
        sb_s = at("sb_s", 20 * KB, [P, B, S])
        sb_pT = at("sb_pT", 21 * KB, [P, B, S])
        sb_oT = at("sb_oT", 22 * KB, [P, KC, B * S])
        causal2 = at("causal2", 24 * KB, [P, S])
        sb_mv = sb("sb_mv", [P, B, 2])
        sb_rstd = sb("sb_rstd", [P, B])
        sb_m = sb("sb_m", [P, 3, B])
        E = a["L1_ffn_router_w"].shape[0]
        TOP = 4
        EI = a["L1_ffn_gate_proj"].shape[2]
        IC = 2
        IP = EI // IC
        mo_gate = at("mo_gate", 64 * KB, [P, E, KC, EI])
        mo_up = at("mo_up", 92 * KB, [P, E, KC, EI])
        mo_down = at("mo_down", 120 * KB, [IP, E, IC, D])
        mo_r = at("mo_r", 26 * KB, [E, D])
        mo_rT = at("mo_rT", 27 * KB, [P, KC, E])
        mo_bias = at("mo_bias", 28 * KB, [P, E])
        mo_s = at("mo_s", 29 * KB, [P, B, E])
        mo_gt = at("mo_gt", 30 * KB, [P, B, E, E])
        mo_eq = at("mo_eq", 32 * KB, [P, B, E, E])
        mo_rank = at("mo_rank", 34 * KB, [P, B, E])
        mo_first = at("mo_first", 35 * KB, [P, E, E])
        mo_m = sb("mo_m", [P, 3, B])
        mo_sg = at("mo_sg", 38 * KB, [IP, 2, IC, B * S])
        mo_a = at("mo_a", 42 * KB, [IP, 2, IC, B * S])

        names = ["x_loaded", "ctx_loaded", "wk_loaded", "wq_loaded", "wv_loaded", "wo_loaded", "gains_loaded", "sb_psum", "sb_act", "sb_dve", "mo_psum", "mo_act", "xb_last_psum", "xb_last_act", "out_done",
                 "const_made", "pool_chain", "ident_ready", "dve_chain", "ln_var", "ln_rstd", "xn_ready", "xT_psum", "xnT_ready",
                 "ctxT_psum", "ctxT_hi_done", "ctxT_lo_done", "wk_split", "wkT_psum", "wkT_done", "q_psum", "q_squared", "q_ss_done",
                 "q_rstd_done", "qn_done", "qT_psum", "qT_done", "gqk_done", "q3_psum", "q3_hi_done", "q3_lo_done",
                 "k_psum", "k_squared", "k_ss_done", "k_rstd_done", "s_psum", "s_scaled", "p_done", "pv_chunk", "o_psum", "o_done",
                 "oT_psum", "oT_done", "aT_psum", "aT_done", "y_psum", "x_updated",
                 "sa_w_loaded", "mask_ready", "sa_q_psum", "sa_qkT", "sa_v_psum", "sa_v_done", "sa_km_done", "sa_s_psum", "sa_s_masked", "sa_centred",
                 "sa_p_done", "sa_pT_psum", "sa_pT_done", "sa_o_psum", "sa_o_done", "sa_oT_psum", "sa_oT_done",
                 "ffw_loaded", "ffb_loaded", "wabs_done", "wabs_psum", "wq_quant", "wqT_psum", "wqT_done",
                 "ff_ss_done", "ff_r_done", "ff_q_done", "ff_qT_psum", "ff_qT_done", "ff_h_psum", "ff_h_done", "ff_silu", "ff_gelu",
                 "ff_lnvar", "ff_lnrstd",
                 "xb_w_loaded", "xb_wkv_loaded", "xb_centred", "xb_cT_psum", "xb_cT_done", "xb_kv_psum", "xb_kv_done", "xb_k_sq", "xb_k_ss",
                 "xb_k_sqrt", "xb_kr_done", "xb_kt_done", "xb_khi", "xb_klo", "xb_kT_psum", "xb_kT_done", "xb_q_psum", "xb_q_ss", "xb_q_sqrt",
                 "xb_q_done", "xb_qn_done", "xb_q1_psum", "xb_q1_done", "xb_row_done", "xb_q2_psum", "xb_q2_done", "xb_m_psum", "xb_m_done",
                 "xb_s_psum", "xb_p_done", "xb_pv_done", "xb_o_psum", "xb_kd_ss", "xb_oh_done", "xb_ohT_psum", "xb_kdm_done", "xb_sd_centred", "xb_pd_done", "xb_od_done", "xb_o_done", "xb_oT_psum", "xb_oT_done",
                 "sb_w_loaded", "sb_masks", "sb_var", "sb_rstd_done", "mo_w_loaded", "mo_down_loaded", "mo_r_loaded", "mo_centred",
                 "mo_gu_psum", "mo_silu", "mo_a_done", "mo_y_psum", "mo_y_done"]
        M = {n: sem(n) for n in names}

        block = ctx.enter_context(nc.Block())
        LNS = upto

        @block.sync
        def _(sp):
            sp.dma_start(x_sb[:, :, :], a["x"].rearrange("b s d -> s b d")).then_inc(M["x_loaded"], 16)
            for b in range(B):
                sp.dma_start(ctx_nat[:, b * NC:(b + 1) * NC, 0:C],
                             a["ctx_1024"][b].rearrange("(p c) d -> p c d", c=NC)).then_inc(M["ctx_loaded"], 16)
            sp.dma_start(wk[:, :], a["L0_xattn_Wk"]).then_inc(M["wk_loaded"], 16)
            sp.dma_start(wq[:, :, :], a["L0_xattn_Wq"].rearrange("(k p) n -> p k n", p=P)).then_inc(M["wq_loaded"], 16)
            sp.dma_start(gains[:, 0:1], a["L0_xattn_gq"].rearrange("(p o) -> p o", o=1)).then_inc(M["gains_loaded"], 16)
            sp.dma_start(gains[:, 1:2], a["L0_xattn_gk"].rearrange("(p o) -> p o", o=1)).then_inc(M["gains_loaded"], 16)
            sp.dma_start(wv[:, :, :], a["L0_xattn_Wv"].rearrange("p (h d) -> p h d", h=H)).then_inc(M["wv_loaded"], 16)
            sp.dma_start(wo[:, :, :], a["L0_xattn_Wo"].rearrange("(h p) n -> p h n", p=P)).then_inc(M["wo_loaded"], 16)
            sp.wait_ge(M["k_psum"], B * NC * NG)
            sp.dma_start(w1[:, :, :], a["L0_ffn_w1"].rearrange("(o p) d -> p o d", p=P)).then_inc(M["ffw_loaded"], 16)
            sp.dma_start(w2[:, :, :], a["L0_ffn_w2"].rearrange("(o p) d -> p o d", p=P)).then_inc(M["ffw_loaded"], 16)
            sp.wait_ge(M["o_psum"], NG)
            sp.dma_start(w_in[:, :, :], a["L0_attn_w_in"].rearrange("(k p) n -> p k n", p=P)).then_inc(M["sa_w_loaded"], 16)
            sp.dma_start(w_out[:, :, :], a["L0_attn_w_out"].rearrange("(k p) n -> p k n", p=P)).then_inc(M["sa_w_loaded"], 16)
            for j in range(2 * KC):
                sp.dma_start(bqk[:, j:j + 1], a["L0_attn_b_in"][j * P:(j + 1) * P].rearrange("(p o) -> p o", o=1)).then_inc(M["sa_w_loaded"], 16)
            sp.dma_start(b_in_row[:, :], a["L0_attn_b_in"].rearrange("(o n) -> o n", o=1)).then_inc(M["sa_w_loaded"], 16)
            sp.dma_start(b_out_row[:, :], a["L0_attn_b_out"].rearrange("(o n) -> o n", o=1)).then_inc(M["sa_w_loaded"], 16)
            sp.wait_ge(M["o_psum"], B * NG)
            for t, name in ((b1_all, "L0_ffn_b1"), (lng_all, "L0_ffn_ln_g"), (lnb_all, "L0_ffn_ln_b"), (b2_all, "L0_ffn_b2")):
                sp.dma_start(t[:, :], a[name].rearrange("(o n) -> o n", o=1).to_broadcast([P, a[name].shape[0]])).then_inc(M["ffb_loaded"], 16)
            if upto >= 6:
                sp.wait_ge(M["y_psum"], B)
                for t, name in ((mo_gate, "L1_ffn_gate_proj"), (mo_up, "L1_ffn_up_proj")):
                    for e in range(0, E, 4):
                        for kc in range(KC):
                            sp.dma_start(t[:, e:e + 4, kc, :], a[name][e:e + 4, kc * P:(kc + 1) * P, :].rearrange("e p i -> p e i")).then_inc(M["mo_w_loaded"], 16)
            if upto >= 4:
                sp.wait_ge(M["x_updated"], 3 * B)
                wkv = M["xb_wkv_loaded"]
                sp.dma_start(xb_wkv[:, 0:D], a["L1_xattn_Wk"]).then_inc(wkv, 16)
                sp.dma_start(xb_wkv[:, D:2 * D], a["L1_xattn_Wv"]).then_inc(wkv, 16)
                everywhere = ((xb_bkv[:, 0:D], "L1_xattn_bk"), (xb_bkv[:, D:2 * D], "L1_xattn_bv"))
                for dst, name in everywhere:
                    sp.dma_start(dst, a[name].rearrange("(o n) -> o n", o=1).to_broadcast([P, D])).then_inc(wkv, 16)
                xw = M["xb_w_loaded"]
                sp.dma_start(xb_wq[:, :, :], a["L1_xattn_Wq"].rearrange("(k p) n -> p k n", p=P)).then_inc(xw, 16)
                sp.dma_start(xb_wo[:, :, :], a["L1_xattn_Wo"].rearrange("(k p) n -> p k n", p=P)).then_inc(xw, 16)
                sp.dma_start(xb_wd[:, :], a["L1_xattn_Wkv_dca"]).then_inc(xw, 16)
                sp.dma_start(xb_bd[:, :], a["L1_xattn_bkv_dca"].rearrange("(o n) -> o n", o=1).to_broadcast([P, 2 * D])).then_inc(xw, 16)
                sp.dma_start(xb_bq[:, :], a["L1_xattn_bq"].rearrange("(o n) -> o n", o=1).to_broadcast([P, D])).then_inc(xw, 16)
                sp.dma_start(xb_wo_row[:, :], a["L1_xattn_bo"].rearrange("(o n) -> o n", o=1)).then_inc(xw, 16)
                sp.dma_start(xb_yd[:, :, :], a["ctx_1024"][:, KV - DCA:KV, :].rearrange("b k c -> k b c")).then_inc(xw, 16)
                for j, name in enumerate(("qn_w", "qn_b", "kn_w", "kn_b", "kn_dca_w", "kn_dca_b")):
                    sp.dma_start(xb_vec[:, j, :], a["L1_xattn_" + name].rearrange("(o n) -> o n", o=1).to_broadcast([P, HD])).then_inc(xw, 16)
            if upto >= 5:
                sp.wait_ge(M["xb_o_psum"], B)
                lw = M["sb_w_loaded"]
                sp.dma_start(sb_w[:, :, :], a["L1_attn_qkv"].rearrange("(k p) n -> p k n", p=P)).then_inc(lw, 16)
                sp.dma_start(sb_wo[:, :, :], a["L1_attn_o_proj"].rearrange("(k p) n -> p k n", p=P)).then_inc(lw, 16)
                sp.dma_start(sb_g[:, 0, :], a["L1_attn_gamma"].rearrange("(o n) -> o n", o=1).to_broadcast([P, D])).then_inc(lw, 16)
                sp.dma_start(sb_g[:, 1, :], a["L1_attn_beta"].rearrange("(o n) -> o n", o=1).to_broadcast([P, D])).then_inc(lw, 16)
            if upto >= 6:
                sp.dma_start(mo_r[:, :], a["L1_ffn_router_w"]).then_inc(M["mo_r_loaded"], 16)
                sp.dma_start(mo_bias[:, :], a["L1_ffn_expert_bias"].rearrange("(o n) -> o n", o=1).to_broadcast([P, E])).then_inc(M["mo_r_loaded"], 16)
                sp.wait_ge(M["y_psum"], 4 * B)
                for e in range(0, E, 4):
                    for ic in range(IC):
                        sp.dma_start(mo_down[:, e:e + 4, ic, :], a["L1_ffn_down_proj"][e:e + 4, ic * IP:(ic + 1) * IP, :].rearrange("e p n -> p e n")).then_inc(M["mo_down_loaded"], 16)
            sp.wait_ge(M["x_updated"], B * upto)
            sp.dma_start(out.rearrange("b s d -> s b d"), x_sb[:, :, :]).then_inc(M["out_done"], 16)
            sp.wait_ge(M["out_done"], 16)

        @block.gpsimd
        def _(pool):
            links = [0]

            def chained(ins):
                links[0] += 1
                ins.then_inc(M["pool_chain"], 1)
                pool.wait_ge(M["pool_chain"], links[0])

            pool.memset(neg_half[:, :], -0.5).then_inc(M["const_made"], 1)
            pool.memset(ones[:, :], 1.0).then_inc(M["const_made"], 1)
            pool.memset(ctx_nat[:, :, C:C + 2], 1.0).then_inc(M["const_made"], 1)
            pool.memset(eps2[:, :], EPS2).then_inc(M["const_made"], 1)
            chained(pool.memset(ident[:, :], 0.0))
            pool.affine_select(out=ident[:, :], in_=ident[:, :], compare_op=ALU.not_equal, fill=1.0,
                               base=0, pattern=[[-1, P]], channel_multiplier=1).then_inc(M["ident_ready"], 1)
            pool.wait_ge(M["const_made"], 3)

            def ln_rstd(k):
                pool.wait_ge(M["ln_var"], B * (k + 1))
                chained(pool.tensor_scalar(veps[:, :], meanvar[:, :, 1], EPS, None, ALU.add))
                pool.tensor_tensor(rstd[:, :], veps[:, :], neg_half[:, 0:B], ALU.pow).then_inc(M["ln_rstd"], 1)

            ln_rstd(0)
            for b in range(B):
                pool.wait_ge(M["q_ss_done"], NG * (b + 1))
                chained(pool.tensor_scalar(q_ss[:, b, :], q_ss[:, b, :], 1.0 / HD0, EPS, ALU.mult, ALU.add))
                pool.tensor_tensor(q_rstd[:, b, :], q_ss[:, b, :], neg_half[:, 0:H], ALU.pow).then_inc(M["q_rstd_done"], 1)
            for b in range(B):
                pool.wait_ge(M["k_ss_done"], NG * NC * (b + 1))
                r = slice(b * NC, (b + 1) * NC)
                chained(pool.tensor_scalar(k_ss[:, r, :], k_ss[:, r, :], 1.0 / HD0, EPS, ALU.mult, ALU.add))
                pool.tensor_tensor(k_rstd[:, r, :], k_ss[:, r, :],
                                   neg_half[:, 0:1].unsqueeze(1).to_broadcast([P, NC, H]), ALU.pow).then_inc(M["k_rstd_done"], 1)


            pool.wait_ge(M["o_psum"], B * NG)
            chained(pool.memset(causal[:, :], 0.0))
            chained(pool.affine_select(out=causal[:, :], in_=causal[:, :], compare_op=ALU.is_ge, fill=-1e30,
                                       base=0, pattern=[[-1, S]], channel_multiplier=1))
            chained(pool.memset(head_mask[:, :], 1.0))
            chained(pool.affine_select(out=head_mask[:, :], in_=head_mask[:, :], compare_op=ALU.is_ge, fill=0.0,
                                       base=0, pattern=[[-HD, 8]], channel_multiplier=1))
            pool.affine_select(out=head_mask[:, :], in_=head_mask[:, :], compare_op=ALU.is_ge, fill=0.0,
                               base=HD - 1, pattern=[[HD, 8]], channel_multiplier=-1).then_inc(M["mask_ready"], 1)
            if upto < 2:
                return
            ln_rstd(1)
            if upto < 3:
                return
            ln_rstd(2)

            def rms(i, n):
                pool.wait_ge(M["ff_ss_done"], B * (i + 1))
                chained(pool.tensor_scalar(ff_ss[:, i, :], ff_ss[:, i, :], 1.0 / n, EPS, ALU.mult, ALU.add))
                pool.tensor_tensor(ff_r[:, i, :], ff_ss[:, i, :], neg_half[:, 0:B], ALU.pow).then_inc(M["ff_r_done"], 1)

            rms(0, D)
            pool.wait_ge(M["ff_lnvar"], B)
            chained(pool.tensor_scalar(ff_rstd[:, :], ff_mv[:, :, 1], EPS, None, ALU.add))
            pool.tensor_tensor(ff_rstd[:, :], ff_rstd[:, :], neg_half[:, 0:B], ALU.pow).then_inc(M["ff_lnrstd"], 1)
            rms(1, FI)
            if upto < 4:
                return
            ln_rstd(3)
            if upto < 5:
                return
            pool.wait_ge(M["xb_o_psum"], B)
            chained(pool.memset(causal2[:, :], 0.0))
            pool.affine_select(out=causal2[:, :], in_=causal2[:, :], compare_op=ALU.is_ge, fill=-1e30,
                               base=0, pattern=[[-1, S]], channel_multiplier=1).then_inc(M["sb_masks"], 1)
            chained(pool.memset(mo_first[:, :, :], 1.0))
            pool.affine_select(out=mo_first[:, :, :], in_=mo_first[:, :, :], compare_op=ALU.is_gt, fill=0.0,
                               base=0, pattern=[[1, E], [-1, E]], channel_multiplier=0).then_inc(M["sb_masks"], 1)
            ln_rstd(4)
            pool.wait_ge(M["sb_var"], B)
            chained(pool.tensor_scalar(sb_rstd[:, :], sb_mv[:, :, 1], EPS, None, ALU.add))
            pool.tensor_tensor(sb_rstd[:, :], sb_rstd[:, :], neg_half[:, 0:B], ALU.pow).then_inc(M["sb_rstd_done"], 1)
            if upto < 6:
                return
            ln_rstd(5)
        @block.scalar
        def _(act):
            def xnT_copy(k):
                act.wait_ge(M["xT_psum"], k + 1)
                act.activation(xnT[:, :, :], ps[:, 0, :], ACT.Copy).then_inc(M["xnT_ready"], 1)

            xnT_copy(0)
            for i in range(B * NG):
                act.wait_ge(M["q_psum"], i + 1)
                if i >= 2:
                    act.wait_ge(M["q_ss_done"], i - 1)
                act.activation(sq[:, i % 2, :], ps[:, (1 + i) % 8, :], ACT.Square).then_inc(M["q_squared"], 1)
            for j in range(B * NC // 4):
                act.wait_ge(M["ctxT_psum"], j + 1)
                act.activation(ctxT_hi[:, 4 * j:4 * j + 4, :], ps[:, j % 2, :], ACT.Copy).then_inc(M["ctxT_hi_done"], 1)
            for j in range(H // 4):
                act.wait_ge(M["wkT_psum"], j + 1)
                act.activation(wkT[:, 4 * j:4 * j + 4, :], ps[:, 2 + j % 2, :], ACT.Copy).then_inc(M["wkT_done"], 1)
            act.wait_ge(M["gqk_done"], 1)
            for j in range(H // 2):
                act.wait_ge(M["qT_psum"], j + 1)
                act.activation(qT[:, 2 * j:2 * j + 2, :], ps[:, 4 + j % 2, :], ACT.Copy, scale=gqk[:, 0:1]).then_inc(M["qT_done"], 1)
            for j in range(H // 2):
                act.wait_ge(M["q3_psum"], j + 1)
                act.activation(q3_hi[:, :, 2 * j:2 * j + 2, :].rearrange("p b h s -> p h b s"),
                               ps[:, 6 + j % 2, :].rearrange("p (h b s) -> p h b s", h=2, b=B),
                               ACT.Copy).then_inc(M["q3_hi_done"], 1)
            act.wait_ge(M["q_ss_done"], B * NG)
            for i in range(B * NC * NG):
                act.wait_ge(M["k_psum"], i + 1)
                if i >= 2:
                    act.wait_ge(M["k_ss_done"], i - 1)
                act.activation(sq[:, i % 2, :], ps[:, i % 4, :], ACT.Square).then_inc(M["k_squared"], 1)
            for i in range(B * NG * NC // 2):
                act.wait_ge(M["s_scaled"], i + 1)
                if i >= 2:
                    act.wait_ge(M["pv_chunk"], i - 1)
                act.activation(p_sb[:, i % 2, :, :], s_sb[:, i % 2, :, :], ACT.Exp, bias=shift[:, 0:1]).then_inc(M["p_done"], 1)
            for j in range(H // 2):
                act.wait_ge(M["oT_psum"], j + 1)
                act.activation(oT[:, 2 * j:2 * j + 2, :], ps[:, j % 2, :], ACT.Copy).then_inc(M["oT_done"], 1)
            for j in range(H // 2):
                act.wait_ge(M["aT_psum"], j + 1)
                act.activation(aT[:, 2 * j:2 * j + 2, :], ps[:, 2 + j % 2, :], ACT.Copy).then_inc(M["aT_done"], 1)
            if upto < 2:
                return
            xnT_copy(1)
            act.wait_ge(M["sa_w_loaded"], 128)
            act.wait_ge(M["sa_q_psum"], 1)
            for j in range(KC):
                act.activation(sa_qT[:, j, :], ps[:, 1, j * B * S:(j + 1) * B * S], ACT.Identity, bias=bqk[:, j:j + 1]).then_inc(M["sa_qkT"], 1)
            for j in range(KC):
                act.activation(sa_kT[:, j, :], ps[:, 2, j * B * S:(j + 1) * B * S], ACT.Identity, bias=bqk[:, KC + j:KC + j + 1]).then_inc(M["sa_qkT"], 1)
            act.wait_ge(M["sa_v_psum"], 1)
            act.activation(sa_v[:, :, :, 0:HD], ps[:, 3, :].rearrange("p (b h d) -> p b h d", b=B, h=H), ACT.Copy).then_inc(M["sa_v_done"], 1)
            for b in range(B):
                act.wait_ge(M["sa_centred"], b + 1)
                act.activation(sa_s[:, b, :, :], sa_s[:, b, :, :], ACT.Exp, scale=float(HD) ** -0.5).then_inc(M["sa_p_done"], 1)
            for b in range(B):
                for g in range(4):
                    act.wait_ge(M["sa_pT_psum"], b * 4 + g + 1)
                    act.activation(sa_pT[:, b, 4 * g:4 * g + 4, :], ps[:, 4 * (1 - b) + g, :], ACT.Copy).then_inc(M["sa_pT_done"], 1)
            for b in range(B):
                act.wait_ge(M["sa_oT_psum"], b + 1)
                act.activation(sa_oT[:, :, b * S:(b + 1) * S], ps[:, 4 * (1 - b) + 1, 0:D].rearrange("p (k s) -> p k s", k=KC),
                               ACT.Copy).then_inc(M["sa_oT_done"], 1)
            if upto < 3:
                return
            for i in range(8):
                act.wait_ge(M["wqT_psum"], i + 1)
                if i < 4:
                    dst = w1qT[:, i // 2, (i % 2) * 512:(i % 2) * 512 + 512]
                else:
                    dst = w2qT[:, 2 * (i - 4):2 * (i - 4) + 2, :]
                act.activation(dst, ps[:, 4 + i % 4, :], ACT.Copy).then_inc(M["wqT_done"], 1)
            xnT_like = ps[:, 0, :]
            act.wait_ge(M["ff_qT_psum"], 1)
            act.activation(ff_qT1[:, :, :], xnT_like, ACT.Copy).then_inc(M["ff_qT_done"], 1)
            for b in range(B):
                act.wait_ge(M["ff_h_done"], b + 1)
                act.activation(ff_h2[:, b, :], ff_h[:, b, :], ACT.Silu).then_inc(M["ff_silu"], 1)
            for b in range(B):
                act.wait_ge(M["ff_silu"], b + 1)
                act.activation(ff_h[:, b, :], ff_h2[:, b, :], ACT.Gelu).then_inc(M["ff_gelu"], 1)
            for b in range(B):
                for g in range(2):
                    act.wait_ge(M["ff_qT_psum"], 2 + 2 * b + g)
                    act.activation(ff_qT2[:, 4 * g:4 * g + 4, b * S:(b + 1) * S], ps[:, 4 + 2 * b + g, :], ACT.Copy).then_inc(M["ff_qT_done"], 1)
            if upto < 4:
                return

            def context_copy(b):
                for g in range(4):
                    act.wait_ge(M["xb_cT_psum"], 4 * b + g + 1)
                    act.activation(xb_cT[:, 4 * g:4 * g + 4, :], ps[:, 1 + g, :], ACT.Copy).then_inc(M["xb_cT_done"], 1)

            def k_squares(b):
                for t in range(NC // 2):
                    n = b * (NC // 2) + t
                    act.wait_ge(M["xb_kv_done"], b * NC + 2 * t + 2)
                    if n >= 2:
                        act.wait_ge(M["xb_k_ss"], n - 1)
                    act.activation(sq[:, n % 2, :].rearrange("p (c h d) -> p c h d", c=2, h=H), xb_kv[:, 2 * t:2 * t + 2, :, 0:HD],
                                   ACT.Square).then_inc(M["xb_k_sq"], 1)
                act.wait_ge(M["xb_k_ss"], (b + 1) * (NC // 2))
                act.activation(xb_rk[:, :, :], xb_ss[:, :, :], ACT.Sqrt, scale=1.0 / HD, bias=eps2[:, 0:1]).then_inc(M["xb_k_sqrt"], 1)

            def k_high(n):
                act.wait_ge(M["xb_kt_done"], n + 1)
                if n >= 1:
                    act.wait_ge(M["xb_kT_psum"], 4 * n)
                src = xb_kt[:, :, :, :].rearrange("p c h d -> p (c h) d").unsqueeze(2).to_broadcast([P, 2 * NC, 2, HD])
                dst = xb_kn[:, :, :, 0:4 * HD].rearrange("p c h (r t d) -> p (c h) r t d", r=2, t=2)[:, :, :, 0, :]
                act.activation(dst, src, ACT.Copy).then_inc(M["xb_khi"], 1)

            act.wait_ge(M["ff_gelu"], B)
            context_copy(0)
            k_squares(0)
            xnT_copy(2)
            act.wait_ge(M["xb_q_ss"], 1)
            act.activation(xb_s32[:, 2, :], xb_s32[:, 1, :], ACT.Sqrt, scale=1.0 / HD, bias=eps2[:, 0:1]).then_inc(M["xb_q_sqrt"], 1)
            act.wait_ge(M["xb_last_psum"], 1)
            act.activation(xb_ydT[:, :, :, :], ps[:, 5, 0:B * DCA].rearrange("p (b k) -> p b k", b=B).unsqueeze(2).to_broadcast([P, B, 8, DCA]),
                           ACT.Copy).then_inc(M["xb_last_act"], 1)
            act.wait_ge(M["xb_kd_ss"], 1)
            act.activation(xb_d32[:, 2, :], xb_d32[:, 1, :], ACT.Sqrt, scale=1.0 / HD, bias=eps2[:, 0:1]).then_inc(M["xb_last_act"], 1)
            act.wait_ge(M["xb_last_psum"], 4)
            act.activation(xb_kdT[:, :, :, :], ps[:, 5, :], ACT.Copy).then_inc(M["xb_last_act"], 1)
            act.activation(xb_qfT[:, :, :], ps[:, 6, :], ACT.Copy).then_inc(M["xb_last_act"], 1)
            act.wait_ge(M["xb_sd_centred"], 1)
            act.activation(xb_pd[:, :, :], xb_pd[:, :, :], ACT.Exp, scale=SC).then_inc(M["xb_last_act"], 1)
            act.wait_ge(M["xb_last_psum"], 6)
            act.activation(xb_pdT[:, :, :], ps[:, 6, :], ACT.Copy).then_inc(M["xb_last_act"], 1)

            def k_copy(n, g):
                act.wait_ge(M["xb_kT_psum"], 4 * n + g + 1)
                act.activation(xb_kT[:, n % 2, 4 * g:4 * g + 4, :], ps[:, 4 * (g % 2), :], ACT.Copy).then_inc(M["xb_kT_done"], 1)

            def q_copy(n):
                act.wait_ge(M["xb_q2_psum"], n + 1)
                act.activation(xb_qT2[0:W, n % 2, 0:S], ps[0:W, 0, 0:S], ACT.Copy)
                act.activation(xb_qT2[W:2 * W, n % 2, S:2 * S], ps[W:2 * W, 0, 0:S], ACT.Copy).then_inc(M["xb_q2_done"], 1)

            def probabilities(n, u):
                m = n * NU + u
                act.wait_ge(M["xb_s_psum"], m + 1)
                if m >= 2:
                    act.wait_ge(M["xb_pv_done"], m - 1)
                act.activation(xb_p[:, m % 2, :, :], ps[:, 5 + m % 2, :].rearrange("p (c s) -> p c s", c=4),
                               ACT.Exp).then_inc(M["xb_p_done"], 1)

            for b in range(B):
                if b == 1:
                    context_copy(1)
                    k_squares(1)
                for g in range(2):
                    act.wait_ge(M["xb_q1_psum"], 2 * b + g + 1)
                    act.activation(xb_qT1[:, 4 * g:4 * g + 4, :], ps[:, 1 + g, :], ACT.Copy).then_inc(M["xb_q1_done"], 1)
                k_high(b * PAIRS)
                for g in range(4):
                    k_copy(b * PAIRS, g)
                for i in range(PAIRS + 1):
                    n = b * PAIRS + i
                    for u in range(NU + 1):
                        if i >= 1 and u < NU:
                            probabilities(n - 1, u)
                        if i + 1 < PAIRS and u == 0:
                            k_high(n + 1)
                        if i + 1 < PAIRS and u in (2, 4, 6, 8):
                            k_copy(n + 1, u // 2 - 1)
                        if i < PAIRS and u == 7:
                            q_copy(n)
            for b in range(B):
                act.wait_ge(M["xb_oT_psum"], b + 1)
                act.activation(xb_qfT[:, :, b * S:(b + 1) * S],
                               ps[:, 1 + b, 0:D].rearrange("p (k s) -> p k s", k=KC), ACT.Copy).then_inc(M["xb_oT_done"], 1)
            if upto < 5:
                return

            act.wait_ge(M["sb_psum"], 1)
            act.activation(sb_hT[:, :, :], ps[:, 0, :], ACT.Copy).then_inc(M["sb_act"], 1)
            act.wait_ge(M["sb_psum"], 2)
            act.activation(sb_qT[:, :, :], ps[:, 1, :], ACT.Copy).then_inc(M["sb_act"], 1)
            act.activation(sb_kT[:, :, :], ps[:, 2, :], ACT.Copy).then_inc(M["sb_act"], 1)
            act.wait_ge(M["sb_psum"], 3)
            act.activation(sb_v[:, :, :], ps[:, 3, :], ACT.Copy).then_inc(M["sb_act"], 1)
            act.wait_ge(M["sb_dve"], 2)
            act.activation(sb_s[:, :, :], sb_s[:, :, :], ACT.Exp, scale=float(D) ** -0.5).then_inc(M["sb_act"], 1)
            act.wait_ge(M["sb_psum"], 5)
            act.activation(sb_pT[:, :, :], ps[:, 5, 0:B * S], ACT.Copy).then_inc(M["sb_act"], 1)
            act.wait_ge(M["sb_psum"], 6)
            act.activation(sb_oT[:, :, :], ps[:, 6, :], ACT.Copy).then_inc(M["sb_act"], 1)
            if upto < 6:
                return

            xnT_copy(3)
            act.wait_ge(M["mo_psum"], 1)
            act.activation(mo_rT[:, :, :], ps[:, 1, 0:KC * E], ACT.Copy).then_inc(M["mo_act"], 1)
            act.wait_ge(M["mo_centred"], 1)
            act.activation(mo_s[:, :, :], mo_s[:, :, :], ACT.Exp).then_inc(M["mo_act"], 1)
            for e in range(E):
                act.wait_ge(M["mo_gu_psum"], e + 1)
                if e >= 2:
                    act.wait_ge(M["mo_a_done"], e - 1)
                act.activation(mo_sg[:, e % 2, :, :], ps[0:IP, 3 + 2 * (e % 2), :], ACT.Silu).then_inc(M["mo_silu"], 1)

        @block.vector
        def _(dve):
            links = [0]

            def chained(ins):
                links[0] += 1
                ins.then_inc(M["dve_chain"], 1)
                dve.wait_ge(M["dve_chain"], links[0])

            def layernorm(k):
                for b in range(B):
                    if k > 0:
                        dve.wait_ge(M["x_updated"], B * (k - 1) + b + 1)
                    chained(dve.bn_stats(stats[:, b, :], x_sb[:, b, :]))
                    dve.bn_aggr(meanvar[:, b, :], stats[:, b, :]).then_inc(M["ln_var"], 1)
                dve.wait_ge(M["ln_var"], B * (k + 1))
                dve.wait_ge(M["ln_rstd"], k + 1)
                for b in range(B):
                    dve.tensor_scalar(xn[:, b, :], x_sb[:, b, :], meanvar[:, b, 0:1], rstd[:, b:b + 1],
                                      ALU.subtract, ALU.mult).then_inc(M["xn_ready"], 1)

            dve.wait_ge(M["x_loaded"], 16)
            layernorm(0)
            dve.wait_ge(M["gains_loaded"], 32)
            dve.tensor_scalar(gqk[:, :], gains[:, 0:1], gains[:, 1:2], float(HD0) ** -0.5, ALU.mult, ALU.mult).then_inc(M["gqk_done"], 1)
            chained(dve.memset(shift[:, :], 0.0))
            dve.wait_ge(M["wk_loaded"], 16)
            chained(dve.tensor_copy(wk_hi[:, :], wk[:, :]))
            dve.tensor_tensor(wk_lo[:, :], wk[:, :], wk_hi[:, :].bitcast(F32), ALU.subtract).then_inc(M["wk_split"], 1)
            for b in range(B):
                for g in range(NG):
                    i = b * NG + g
                    dve.wait_ge(M["q_squared"], i + 1)
                    dve.tensor_reduce(q_ss[:, b, G * g:G * g + G], sq[:, i % 2, :].rearrange("p (h d) -> p h d", h=G),
                                      AX.X, ALU.add).then_inc(M["q_ss_done"], 1)
                dve.wait_ge(M["q_rstd_done"], b + 1)
                for g in range(NG):
                    i = b * NG + g
                    dve.tensor_tensor(qn[:, b, G * g:G * g + G, :], ps[:, (1 + i) % 8, :].rearrange("p (h d) -> p h d", h=G),
                                      q_rstd[:, b, G * g:G * g + G].unsqueeze(2).to_broadcast([P, G, HD0]),
                                      ALU.mult).then_inc(M["qn_done"], 1)
            for j in range(B * NC // 4):
                dve.wait_ge(M["ctxT_hi_done"], j + 1)
                dve.tensor_tensor(ctxT_lo[:, 4 * j:4 * j + 4, :], ps[:, j % 2, :].rearrange("p (c k) -> p c k", c=4),
                                  ctxT_hi[:, 4 * j:4 * j + 4, :].bitcast(F32), ALU.subtract).then_inc(M["ctxT_lo_done"], 1)
            for j in range(H // 2):
                dve.wait_ge(M["q3_hi_done"], j + 1)
                dve.tensor_tensor(q3_lo[:, :, 2 * j:2 * j + 2, :].rearrange("p b h s -> p h b s"),
                                  ps[:, 6 + j % 2, :].rearrange("p (h b s) -> p h b s", h=2, b=B),
                                  q3_hi[:, :, 2 * j:2 * j + 2, :].bitcast(F32).rearrange("p b h s -> p h b s"),
                                  ALU.subtract).then_inc(M["q3_lo_done"], 1)
            for c in range(B * NC):
                for g in range(NG):
                    i = c * NG + g
                    dve.wait_ge(M["k_squared"], i + 1)
                    dve.tensor_reduce(k_ss[:, c, G * g:G * g + G], sq[:, i % 2, :].rearrange("p (h d) -> p h d", h=G),
                                      AX.X, ALU.add).then_inc(M["k_ss_done"], 1)
            for b in range(B):
                dve.wait_ge(M["k_rstd_done"], b + 1)
                for g in range(NG):
                    for c2 in range(NC // 2):
                        i = (b * NG + g) * (NC // 2) + c2
                        c = b * NC + 2 * c2
                        dve.wait_ge(M["s_psum"], i + 1)
                        if i >= 2:
                            dve.wait_ge(M["p_done"], i - 1)
                        dve.tensor_tensor(s_sb[:, i % 2, :, :].rearrange("p c (h s) -> p c h s", h=G),
                                          ps[:, 2 * (i % 2):2 * (i % 2) + 2, :].rearrange("p c (h s) -> p c h s", h=G),
                                          k_rstd[:, c:c + 2, G * g:G * g + G].unsqueeze(3).to_broadcast([P, 2, G, S]),
                                          ALU.mult).then_inc(M["s_scaled"], 1)
                    j = b * NG + g
                    o = ps[:, 4 + 2 * (j % 2):6 + 2 * (j % 2), 0:2 * (C + 2)].rearrange("p k (h c) -> p k h c", h=2)
                    dve.wait_ge(M["o_psum"], j + 1)
                    chained(dve.reciprocal(o_den[:, j, :].rearrange("p (k h) -> p k h", k=2), o[:, :, :, C]))
                    dve.tensor_tensor(o_n[:, b, G * g:G * g + G, :].rearrange("p (k h) c -> p k h c", k=2), o[:, :, :, 0:C],
                                      o_den[:, j, :].rearrange("p (k h) -> p k h", k=2).unsqueeze(3).to_broadcast([P, 2, 2, C]),
                                      ALU.mult).then_inc(M["o_done"], 1)
            for b in range(B):
                dve.wait_ge(M["y_psum"], b + 1)
                dve.tensor_tensor(x_sb[:, b, :], x_sb[:, b, :], ps[:, 4 + b, 0:D], ALU.add).then_inc(M["x_updated"], 1)
            if upto < 2:
                return
            layernorm(1)
            dve.memset(sa_v[:, :, :, HD:HD + 2], 1.0).then_inc(M["sa_v_done"], 1)
            dve.wait_ge(M["mask_ready"], 1)
            dve.wait_ge(M["sa_qkT"], 2 * KC)
            for b in range(B):
                for j in range(KC):
                    i = b * KC + j
                    if i >= 2:
                        dve.wait_ge(M["sa_s_psum"], i - 1)
                    dve.tensor_tensor(sa_km[:, i % 2, :, :], sa_kT[:, j, b * S:(b + 1) * S].unsqueeze(1).to_broadcast([P, 8, S]),
                                      head_mask[:, :].unsqueeze(2).to_broadcast([P, 8, S]), ALU.mult).then_inc(M["sa_km_done"], 1)
            for b in range(B):
                for j in range(KC):
                    dve.wait_ge(M["sa_s_psum"], b * KC + j + 1)
                    bank = 4 * (1 - b) + 2 * j
                    dve.tensor_tensor(sa_s[:, b, 8 * j:8 * j + 8, :], ps[:, bank:bank + 2, :].rearrange("p k (h s) -> p (k h) s", s=S),
                                      causal[:, :].unsqueeze(1).to_broadcast([P, 8, S]), ALU.add).then_inc(M["sa_s_masked"], 1)
                dve.wait_ge(M["sa_s_masked"], KC * (b + 1))
                chained(dve.tensor_reduce(sa_max[:, b, :], sa_s[:, b, :, :], AX.X, ALU.max))
                dve.tensor_tensor(sa_s[:, b, :, :], sa_s[:, b, :, :], sa_max[:, b, :].unsqueeze(2).to_broadcast([P, H, S]),
                                  ALU.subtract).then_inc(M["sa_centred"], 1)
            for b in range(B):
                dve.wait_ge(M["sa_o_psum"], b + 1)
                o = ps[:, 4 * (1 - b), 0:H * (HD + 2)].rearrange("p (h d) -> p h d", h=H)
                chained(dve.reciprocal(sa_den[:, b, :], o[:, :, HD]))
                dve.tensor_tensor(sa_o[:, b, :].rearrange("p (h d) -> p h d", h=H), o[:, :, 0:HD],
                                  sa_den[:, b, :].unsqueeze(2).to_broadcast([P, H, HD]), ALU.mult).then_inc(M["sa_o_done"], 1)
            for b in range(B):
                dve.wait_ge(M["y_psum"], B + b + 1)
                dve.tensor_tensor(x_sb[:, b, :], x_sb[:, b, :], ps[:, 4 * (1 - b) + 2, 0:D], ALU.add).then_inc(M["x_updated"], 1)
            if upto < 3:
                return
            ROUND = 1.5 * 2.0 ** 23
            dve.wait_ge(M["ffw_loaded"], 32)
            dve.tensor_reduce(w_abs[:, 0:1], w1[:, :, :], AX.XY, ALU.add, apply_absolute_value=True).then_inc(M["wabs_done"], 1)
            dve.tensor_reduce(w_abs[:, 1:2], w2[:, :, :], AX.XY, ALU.add, apply_absolute_value=True).then_inc(M["wabs_done"], 1)
            dve.wait_ge(M["wabs_psum"], 1)
            chained(dve.tensor_scalar(w_mean[:, :], ps[:, 3, 0:2], 1.0 / (FI * D), 1e-5, ALU.mult, ALU.max))
            chained(dve.reciprocal(w_scale[:, :], w_mean[:, :]))
            for i, w in enumerate((w1, w2)):
                chained(dve.tensor_scalar(w[:, :, :], w[:, :, :], w_scale[:, i:i + 1], ROUND, ALU.mult, ALU.add))
                chained(dve.tensor_scalar(w[:, :, :], w[:, :, :], -ROUND, 1.0, ALU.add, ALU.min))
                dve.tensor_scalar(w[:, :, :], w[:, :, :], -1.0, None, ALU.max).then_inc(M["wq_quant"], 1)
            dve.wait_ge(M["x_updated"], 2 * B)
            layernorm(2)
            dve.wait_ge(M["xn_ready"], 3 * B)

            def quantise(i, src, dst):
                for b in range(B):
                    chained(dve.tensor_reduce(ff_max[:, i, b:b + 1], src[:, b, :], AX.X, ALU.max, apply_absolute_value=True))
                dve.wait_ge(M["ff_r_done"], i + 1)
                chained(dve.tensor_tensor(ff_max[:, i, :], ff_max[:, i, :], ff_r[:, i, :], ALU.mult))
                chained(dve.tensor_scalar(ff_max[:, i, :], ff_max[:, i, :], 1e-5, 1.0 / 127.0, ALU.max, ALU.mult))
                chained(dve.reciprocal(ff_s[:, i, :], ff_max[:, i, :]))
                chained(dve.tensor_scalar(ff_dq[:, i, :], ff_max[:, i, :], w_mean[:, i:i + 1], None, ALU.mult))
                for b in range(B):
                    chained(dve.tensor_scalar(dst[:, b, :], src[:, b, :], ff_r[:, i, b:b + 1], ff_s[:, i, b:b + 1], ALU.mult, ALU.mult))
                    chained(dve.tensor_scalar(dst[:, b, :], dst[:, b, :], ROUND, -ROUND, ALU.add, ALU.add))
                    dve.tensor_scalar(dst[:, b, :], dst[:, b, :], 127.0, -128.0, ALU.min, ALU.max).then_inc(M["ff_q_done"], 1)

            for b in range(B):
                dve.scalar_tensor_tensor(out=ff_sq[:, b, 0:D], in0=xn[:, b, :], scalar=1.0, in1=xn[:, b, :], op0=ALU.mult, op1=ALU.mult,
                                         accum_out=ff_ss[:, 0, b:b + 1]).then_inc(M["ff_ss_done"], 1)
            quantise(0, xn, ff_q1)
            dve.wait_ge(M["ffb_loaded"], 64)
            for b in range(B):
                dve.wait_ge(M["ff_h_psum"], b + 1)
                dve.scalar_tensor_tensor(out=ff_h[:, b, :], in0=ps[:, 4 + 2 * b:6 + 2 * b, :].rearrange("p k n -> p (k n)"), scalar=ff_dq[:, 0, b:b + 1],
                                         in1=b1_all[:, :], op0=ALU.mult, op1=ALU.add).then_inc(M["ff_h_done"], 1)
            for b in range(B):
                dve.wait_ge(M["ff_gelu"], b + 1)
                for t in range(2):
                    chained(dve.bn_stats(ff_stats[:, b, t, :], ff_h[:, b, t * 512:(t + 1) * 512]))
                dve.bn_aggr(ff_mv[:, b, :], ff_stats[:, b, :, :]).then_inc(M["ff_lnvar"], 1)
            dve.wait_ge(M["ff_lnvar"], B)
            dve.wait_ge(M["ff_lnrstd"], 1)
            for b in range(B):
                chained(dve.tensor_scalar(ff_h2[:, b, :], ff_h[:, b, :], ff_mv[:, b, 0:1], ff_rstd[:, b:b + 1], ALU.subtract, ALU.mult))
                chained(dve.tensor_tensor(ff_h2[:, b, :], ff_h2[:, b, :], lng_all[:, :], ALU.mult))
                chained(dve.tensor_tensor(ff_h2[:, b, :], ff_h2[:, b, :], lnb_all[:, :], ALU.add))
                dve.scalar_tensor_tensor(out=ff_sq[:, b, :], in0=ff_h2[:, b, :], scalar=1.0, in1=ff_h2[:, b, :], op0=ALU.mult, op1=ALU.mult,
                                         accum_out=ff_ss[:, 1, b:b + 1]).then_inc(M["ff_ss_done"], 1)
            quantise(1, ff_h2, ff_h)
            for b in range(B):
                dve.wait_ge(M["y_psum"], 2 * B + b + 1)
                chained(dve.tensor_tensor(x_sb[:, b, :], x_sb[:, b, :], b2_all[:, :], ALU.add))
                dve.scalar_tensor_tensor(out=x_sb[:, b, :], in0=ps[:, 1 + b, 0:D], scalar=ff_dq[:, 1, b:b + 1], in1=x_sb[:, b, :],
                                         op0=ALU.mult, op1=ALU.add).then_inc(M["x_updated"], 1)
            if upto < 4:
                return

            def heads(ap):
                return ap.rearrange("p (h d) -> p h d", d=HD)

            def per_head(ap, n):
                return ap.unsqueeze(2).to_broadcast([P, n, HD])

            dve.wait_ge(M["xb_wkv_loaded"], 64)
            for j, w in enumerate((xb_wkv, xb_bkv)):
                wv32 = w[:, :].rearrange("p (h d) -> p h d", d=2 * HD)
                chained(dve.tensor_reduce(xb_s32[:, j, 0:H], wv32[:, :, 0:HD], AX.X, ALU.add))
                chained(dve.tensor_scalar(xb_s32[:, j, 0:H], xb_s32[:, j, 0:H], 1.0 / HD, None, ALU.mult))
                dve.tensor_tensor(wv32[:, :, 0:HD], wv32[:, :, 0:HD], per_head(xb_s32[:, j, 0:H], H), ALU.subtract).then_inc(M["xb_centred"], 1)

            def key_rows(b):
                if b == 0:
                    chained(dve.memset(xb_kv[:, :, :, 2 * HD:2 * HD + 1], 1.0))
                    dve.wait_ge(M["xb_centred"], 2)
                for c in range(NC):
                    n = b * NC + c
                    dve.wait_ge(M["xb_kv_psum"], n + 1)
                    dve.tensor_tensor(xb_kv[:, c, :, 0:2 * HD], ps[:, 1 + c % 4, :].rearrange("p (h d) -> p h d", h=H),
                                      xb_bkv[:, :].rearrange("p (h d) -> p h d", h=H), ALU.add).then_inc(M["xb_kv_done"], 1)
                    if c % 2 == 1 and c >= 3:
                        key_sums(b, c // 2 - 1)
                key_sums(b, NC // 2 - 1)
                dve.wait_ge(M["xb_k_sqrt"], b + 1)
                dve.reciprocal(xb_rk[:, :, :], xb_rk[:, :, :]).then_inc(M["xb_kr_done"], 1)

            def key_sums(b, t):
                n = b * (NC // 2) + t
                dve.wait_ge(M["xb_k_sq"], n + 1)
                dve.tensor_reduce(xb_ss[:, 2 * t:2 * t + 2, :], sq[:, n % 2, :].rearrange("p (c h d) -> p c h d", c=2, h=H),
                                  AX.X, ALU.add).then_inc(M["xb_k_ss"], 1)

            def head_norm(dst, tmp, sums, n):
                chained(dve.tensor_reduce(sums[:, 0, 0:n], heads(dst), AX.X, ALU.add))
                chained(dve.tensor_scalar(sums[:, 0, 0:n], sums[:, 0, 0:n], 1.0 / HD, None, ALU.mult))
                chained(dve.tensor_tensor(heads(dst), heads(dst), per_head(sums[:, 0, 0:n], n), ALU.subtract))
                chained(dve.tensor_tensor(tmp, dst, dst, ALU.mult))

            key_rows(0)
            layernorm(3)
            q_all = xb_q[:, :, :].rearrange("p b d -> p (b d)")
            t_all = xb_t[:, :, :].rearrange("p b d -> p (b d)")
            qk_all = xb_qk[:, :, :].rearrange("p b d -> p (b d)")
            vec = lambda j, n: xb_vec[:, j, :].unsqueeze(1).to_broadcast([P, n, HD])
            dve.wait_ge(M["xb_w_loaded"], 13 * 16)
            dve.wait_ge(M["xb_q_psum"], 1)
            chained(dve.tensor_tensor(xb_q[:, :, :], ps[:, 0, :].rearrange("p (b d) -> p b d", b=B), xb_bq[:, :].unsqueeze(1).to_broadcast([P, B, D]), ALU.add))
            head_norm(q_all, t_all, xb_s32, B * H)
            dve.tensor_reduce(xb_s32[:, 1, :], heads(t_all), AX.X, ALU.add).then_inc(M["xb_q_ss"], 1)
            dve.wait_ge(M["xb_q_sqrt"], 1)
            chained(dve.reciprocal(xb_s32[:, 3, :], xb_s32[:, 2, :]))
            chained(dve.tensor_tensor(heads(q_all), heads(q_all), per_head(xb_s32[:, 3, :], B * H), ALU.mult))
            chained(dve.tensor_tensor(heads(q_all), heads(q_all), vec(0, B * H), ALU.mult))
            dve.tensor_tensor(heads(q_all), heads(q_all), vec(1, B * H), ALU.add).then_inc(M["xb_q_done"], 1)
            dve.wait_ge(M["xb_q_done"], 1)
            chained(dve.scalar_tensor_tensor(out=heads(qk_all), in0=heads(q_all), scalar=SC, in1=vec(2, B * H), op0=ALU.mult, op1=ALU.mult))
            chained(dve.scalar_tensor_tensor(out=heads(t_all), in0=heads(q_all), scalar=SC, in1=vec(3, B * H), op0=ALU.mult, op1=ALU.mult))
            chained(dve.tensor_reduce(xb_qb[:, :], heads(t_all), AX.X, ALU.add))

            for b in range(B):
                dve.wait_ge(M["xb_last_psum"], 1 + b + 1)
                chained(dve.tensor_tensor(xb_kd[:, b, :], ps[:, 3 + b, :], xb_bd[:, :], ALU.add))
            for b in range(B):
                half = xb_d32[:, :, b * H:(b + 1) * H]
                head_norm(xb_kd[:, b, 0:D], t_all[:, 0:D], half, H)
                chained(dve.tensor_reduce(half[:, 1, :], heads(t_all[:, 0:D]), AX.X, ALU.add))
            dve.engine_nop().then_inc(M["xb_kd_ss"], 1)
            dve.wait_ge(M["xb_last_act"], 2)
            chained(dve.reciprocal(xb_d32[:, 3, :], xb_d32[:, 2, :]))
            for b in range(B):
                k = heads(xb_kd[:, b, 0:D])
                chained(dve.tensor_tensor(k, k, per_head(xb_d32[:, 3, b * H:(b + 1) * H], H), ALU.mult))
                chained(dve.tensor_tensor(k, k, vec(4, H), ALU.mult))
                chained(dve.tensor_tensor(k, k, vec(5, H), ALU.add))
                dve.tensor_tensor(xb_kdm[:, b, :].rearrange("p (v h d) -> p v h d", h=8, d=HD), xb_kd[:, b, :].rearrange("p (v h d) -> p v h d", h=8, d=HD),
                                  head_mask[:, :].unsqueeze(1).unsqueeze(3).to_broadcast([P, 4, 8, HD]), ALU.mult).then_inc(M["xb_kdm_done"], 1)
            dve.wait_ge(M["xb_last_psum"], 5)
            sd = ps[:, 5, :].rearrange("p (h k) -> p h k", k=DCA)
            pd = xb_pd[:, :, :].rearrange("p b (h k) -> p (b h) k", k=DCA)
            chained(dve.tensor_reduce(xb_d32[:, 0, :], sd, AX.X, ALU.max))
            dve.tensor_tensor(pd, sd, per_head(xb_d32[:, 0, :], B * H), ALU.subtract).then_inc(M["xb_sd_centred"], 1)
            dve.wait_ge(M["xb_last_act"], 5)
            chained(dve.tensor_reduce(xb_d32[:, 1, :], pd, AX.X, ALU.add))
            chained(dve.reciprocal(xb_d32[:, 2, :], xb_d32[:, 1, :]))
            dve.tensor_tensor(pd, pd, per_head(xb_d32[:, 2, :], B * H), ALU.mult).then_inc(M["xb_pd_done"], 1)
            dve.wait_ge(M["xb_last_psum"], 7)
            dve.tensor_copy(xb_o[:, :, :], ps[:, 5, :]).then_inc(M["xb_od_done"], 1)
            dve.wait_ge(M["xb_od_done"], 1)

            def k_full(n):
                i = n % PAIRS
                if n >= 1:
                    dve.wait_ge(M["xb_klo"], n)
                    dve.wait_ge(M["xb_khi"], n)
                dve.tensor_tensor(xb_kt[:, :, :, :], xb_kv[:, :, 2 * i:2 * i + 2, 0:HD], xb_rk[:, :, 2 * i:2 * i + 2].unsqueeze(3).to_broadcast([P, NC, 2, HD]),
                                  ALU.mult).then_inc(M["xb_kt_done"], 1)

            def k_low(n):
                dve.wait_ge(M["xb_khi"], n + 1)
                dve.tensor_tensor(xb_kn[:, :, :, HD:2 * HD].rearrange("p c h d -> p (c h) d"), xb_kt[:, :, :, :].rearrange("p c h d -> p (c h) d"),
                                  xb_kn[:, :, :, 0:HD].bitcast(F32).rearrange("p c h d -> p (c h) d"), ALU.subtract).then_inc(M["xb_klo"], 1)

            def q_rows(b, h, n, value):
                chained(dve.tensor_copy(xb_qn[:, h:h + n, 3 * HD], value))
                return dve.tensor_tensor(xb_qn[:, h:h + n, 3 * HD + 1], value, xb_qn[:, h:h + n, 3 * HD].bitcast(F32), ALU.subtract)

            for b in range(B):
                if b == 1:
                    dve.wait_ge(M["xb_pv_done"], PAIRS * NU)
                    key_rows(1)
                dve.wait_ge(M["xb_kv_psum"], (b + 1) * NC)
                chained(dve.memset(xb_kn[:, :, :, 3 * HD:3 * HD + 2].bitcast(F32), 1.0))
                chained(dve.memset(xb_kn[:, :, :, 3 * HD + 2:W].bitcast(F32), 0.0))
                if b == 0:
                    chained(dve.memset(xb_qn[:, :, 3 * HD + 2:W].bitcast(F32), 0.0))
                    chained(dve.memset(xb_qT2[:, :, :].bitcast(F32), 0.0))
                qk = heads(xb_qk[:, b, :])
                chained(dve.tensor_copy(xb_qn[:, :, 0:HD], qk))
                chained(dve.tensor_copy(xb_qn[:, :, HD:2 * HD], qk))
                chained(dve.tensor_tensor(xb_qn[:, :, 2 * HD:3 * HD], qk, xb_qn[:, :, 0:HD].bitcast(F32), ALU.subtract))
                q_rows(b, 0, H, xb_qb[:, b * H:(b + 1) * H]).then_inc(M["xb_qn_done"], 1)
                dve.wait_ge(M["xb_qn_done"], b + 1)
                dve.wait_ge(M["xb_q1_done"], 2 * (b + 1))
                dve.wait_ge(M["xb_kr_done"], b + 1)
                k_full(b * PAIRS)
                k_low(b * PAIRS)
                k_full(b * PAIRS + 1)
                for i in range(PAIRS):
                    n = b * PAIRS + i
                    for m in range(8):
                        dve.wait_ge(M["xb_m_psum"], 8 * n + m + 1)
                        dve.tensor_reduce(xb_pm[:, n % 2, 4 * (m % 2) + m // 2:4 * (m % 2) + m // 2 + 1],
                                          ps[:, 1 + (8 * n + m) % 3, :].rearrange("p (c k) -> p c k", k=P)[:, :, 0:P - 1],
                                          AX.XY, ALU.max).then_inc(M["xb_m_done"], 1)
                        if m == 1 and i + 1 < PAIRS:
                            k_low(n + 1)
                    dve.wait_ge(M["xb_m_done"], 8 * n + 8)
                    chained(dve.tensor_reduce(xb_m[:, n % 2, :], xb_pm[:, n % 2, :].rearrange("p (h u) -> p h u", h=2), AX.X, ALU.max))
                    chained(dve.tensor_tensor(xb_m[:, n % 2, :], xb_qb[:, b * H + 2 * i:b * H + 2 * i + 2], xb_m[:, n % 2, :], ALU.subtract))
                    q_rows(b, 2 * i, 2, xb_m[:, n % 2, :]).then_inc(M["xb_row_done"], 1)
                    if i + 2 < PAIRS:
                        k_full(n + 2)
                dve.wait_ge(M["xb_o_psum"], b + 1)
                dve.tensor_copy(xb_oh[:, :], ps[:, 7, :]).then_inc(M["xb_oh_done"], 1)
                dve.wait_ge(M["xb_ohT_psum"], b + 1)
                o = ps[:, 5, :].rearrange("p (h d) -> p h d", h=H)
                chained(dve.reciprocal(xb_den[:, b, :], o[:, :, 2 * HD - 1]))
                chained(dve.tensor_tensor(heads(xb_t[:, b, :]), o[:, :, HD - 1:2 * HD - 1], per_head(xb_den[:, b, :], H), ALU.mult))
                dve.tensor_tensor(xb_o[:, b, :], xb_o[:, b, :], xb_t[:, b, :], ALU.add).then_inc(M["xb_o_done"], 1)
            for b in range(B):
                dve.wait_ge(M["y_psum"], 3 * B + b + 1)
                dve.tensor_tensor(x_sb[:, b, :], x_sb[:, b, :], ps[:, 3 + b, 0:D], ALU.add).then_inc(M["x_updated"], 1)
            if upto < 5:
                return

            layernorm(4)
            dve.wait_ge(M["xn_ready"], 5 * B)
            for b in range(B):
                chained(dve.bn_stats(stats[:, b, :], xn[:, b, :]))
                dve.bn_aggr(sb_mv[:, b, :], stats[:, b, :]).then_inc(M["sb_var"], 1)
            dve.wait_ge(M["sb_var"], B)
            dve.wait_ge(M["sb_rstd_done"], 1)
            dve.wait_ge(M["sb_w_loaded"], 64)
            for b in range(B):
                chained(dve.tensor_scalar(sb_h[:, b, :], xn[:, b, :], sb_mv[:, b, 0:1], sb_rstd[:, b:b + 1], ALU.subtract, ALU.mult))
            chained(dve.tensor_tensor(sb_h[:, :, :], sb_h[:, :, :], sb_g[:, 0, :].unsqueeze(1).to_broadcast([P, B, D]), ALU.mult))
            dve.tensor_tensor(sb_h[:, :, :], sb_h[:, :, :], sb_g[:, 1, :].unsqueeze(1).to_broadcast([P, B, D]), ALU.add).then_inc(M["sb_dve"], 1)
            dve.wait_ge(M["sb_psum"], 4)
            dve.wait_ge(M["sb_masks"], 2)
            chained(dve.tensor_tensor(sb_s[:, :, :], ps[:, 4, 0:B * S].rearrange("p (b s) -> p b s", b=B), causal2[:, :].unsqueeze(1).to_broadcast([P, B, S]), ALU.add))
            chained(dve.tensor_reduce(sb_m[:, 0, :], sb_s[:, :, :], AX.X, ALU.max))
            dve.tensor_tensor(sb_s[:, :, :], sb_s[:, :, :], sb_m[:, 0, :].unsqueeze(2).to_broadcast([P, B, S]), ALU.subtract).then_inc(M["sb_dve"], 1)
            dve.wait_ge(M["sb_act"], 5)
            chained(dve.tensor_reduce(sb_m[:, 1, :], sb_s[:, :, :], AX.X, ALU.add))
            chained(dve.reciprocal(sb_m[:, 2, :], sb_m[:, 1, :]))
            dve.tensor_tensor(sb_s[:, :, :], sb_s[:, :, :], sb_m[:, 2, :].unsqueeze(2).to_broadcast([P, B, S]), ALU.mult).then_inc(M["sb_dve"], 1)
            for b in range(B):
                chained(dve.tensor_tensor(x_sb[:, b, :], x_sb[:, b, :], xn[:, b, :], ALU.add))
            for b in range(B):
                dve.wait_ge(M["y_psum"], 5 * B)
                dve.tensor_tensor(x_sb[:, b, :], x_sb[:, b, :], ps[:, 7, b * D:(b + 1) * D], ALU.add).then_inc(M["x_updated"], 1)
            if upto < 6:
                return

            layernorm(5)
            dve.wait_ge(M["mo_r_loaded"], 32)
            dve.wait_ge(M["mo_psum"], 2)
            chained(dve.tensor_tensor(mo_s[:, :, :], ps[:, 2, 0:B * E].rearrange("p (b e) -> p b e", b=B), mo_bias[:, :].unsqueeze(1).to_broadcast([P, B, E]), ALU.add))
            chained(dve.tensor_reduce(mo_m[:, 0, :], mo_s[:, :, :], AX.X, ALU.max))
            dve.tensor_tensor(mo_s[:, :, :], mo_s[:, :, :], mo_m[:, 0, :].unsqueeze(2).to_broadcast([P, B, E]), ALU.subtract).then_inc(M["mo_centred"], 1)
            dve.wait_ge(M["mo_act"], 2)
            chained(dve.tensor_reduce(mo_m[:, 1, :], mo_s[:, :, :], AX.X, ALU.add))
            chained(dve.reciprocal(mo_m[:, 2, :], mo_m[:, 1, :]))
            chained(dve.tensor_tensor(mo_s[:, :, :], mo_s[:, :, :], mo_m[:, 2, :].unsqueeze(2).to_broadcast([P, B, E]), ALU.mult))
            for b in range(B):
                mine = mo_s[:, b, :].unsqueeze(2).to_broadcast([P, E, E])
                other = mo_s[:, b, :].unsqueeze(1).to_broadcast([P, E, E])
                chained(dve.tensor_tensor(mo_gt[:, b, :, :], other, mine, ALU.is_gt))
                chained(dve.tensor_tensor(mo_eq[:, b, :, :], other, mine, ALU.is_equal))
                chained(dve.tensor_tensor(mo_eq[:, b, :, :], mo_eq[:, b, :, :], mo_first[:, :, :], ALU.mult))
                chained(dve.tensor_tensor(mo_gt[:, b, :, :], mo_gt[:, b, :, :], mo_eq[:, b, :, :], ALU.add))
                chained(dve.tensor_reduce(mo_rank[:, b, :], mo_gt[:, b, :, :], AX.X, ALU.add))
            chained(dve.scalar_tensor_tensor(out=mo_s[:, :, :], in0=mo_rank[:, :, :], scalar=TOP - 0.5, in1=mo_s[:, :, :], op0=ALU.is_lt, op1=ALU.mult))
            chained(dve.tensor_reduce(mo_m[:, 1, :], mo_s[:, :, :], AX.X, ALU.add))
            chained(dve.reciprocal(mo_m[:, 2, :], mo_m[:, 1, :]))
            chained(dve.tensor_tensor(mo_s[:, :, :], mo_s[:, :, :], mo_m[:, 2, :].unsqueeze(2).to_broadcast([P, B, E]), ALU.mult))

            def add_expert(e):
                dve.wait_ge(M["mo_y_psum"], e + 1)
                if e >= 1:
                    dve.wait_ge(M["mo_y_done"], B * e)
                for b in range(B):
                    ins = dve.scalar_tensor_tensor(out=x_sb[:, b, :], in0=ps[:, 0 + 7 * (e % 2), b * D:(b + 1) * D], scalar=mo_s[:, b, e:e + 1], in1=x_sb[:, b, :],
                                                   op0=ALU.mult, op1=ALU.add)
                    ins.then_inc(M["x_updated"] if e == E - 1 else M["mo_y_done"], 1)

            for e in range(E):
                dve.wait_ge(M["mo_silu"], e + 1)
                if e >= 2:
                    dve.wait_ge(M["mo_y_psum"], e - 1)
                dve.tensor_tensor(mo_a[:, e % 2, :, :].rearrange("p i s -> p (i s)"), ps[0:IP, 4 + 2 * (e % 2), :], mo_sg[:, e % 2, :, :].rearrange("p i s -> p (i s)"),
                                  ALU.mult).then_inc(M["mo_a_done"], 1)
                if e >= 1:
                    add_expert(e - 1)
            add_expert(E - 1)

        @block.tensor
        def _(pe):
            def xn_transposes(k):
                pe.wait_ge(M["xn_ready"], B * (k + 1))
                for kc in range(KC):
                    for b in range(B):
                        last = pe.transpose(ps[:, 0, (kc * B + b) * P:(kc * B + b + 1) * P], xn[:, b, kc * P:(kc + 1) * P], ident[:, :])
                last.then_inc(M["xT_psum"], 1)

            pe.wait_ge(M["ident_ready"], 1)
            xn_transposes(0)
            pe.wait_ge(M["xnT_ready"], 1)
            pe.wait_ge(M["wq_loaded"], 16)
            for b in range(B):
                for g in range(NG):
                    i = b * NG + g
                    for kc in range(KC):
                        last = pe.matmul(ps[:, (1 + i) % 8, :], xnT[:, kc, b * S:(b + 1) * S],
                                         wq[:, kc, g * 512:(g + 1) * 512], start=(kc == 0), stop=(kc == KC - 1))
                    last.then_inc(M["q_psum"], 1)
            pe.wait_ge(M["ctx_loaded"], 32)
            for j in range(B * NC // 4):
                if j < 2:
                    pe.wait_ge(M["qn_done"], B * NG if j == 0 else 1)
                else:
                    pe.wait_ge(M["ctxT_lo_done"], j - 1)
                for t in range(4):
                    last = pe.transpose(ps[:, j % 2, t * P:(t + 1) * P], ctx_nat[:, 4 * j + t, 0:C], ident[:, :])
                last.then_inc(M["ctxT_psum"], 1)
            pe.wait_ge(M["wk_loaded"], 16)
            for j in range(H // 4):
                if j >= 2:
                    pe.wait_ge(M["wkT_done"], j - 1)
                for t in range(4):
                    h = 4 * j + t
                    last = pe.transpose(ps[:, 2 + j % 2, t * P:(t + 1) * P], wk[:, h * P:(h + 1) * P], ident[:, :])
                last.then_inc(M["wkT_psum"], 1)
            for j in range(H // 2):
                if j >= 2:
                    pe.wait_ge(M["qT_done"], j - 1)
                for t in range(2):
                    for b in range(B):
                        last = pe.transpose(ps[:, 4 + j % 2, (t * B + b) * P:(t * B + b + 1) * P], qn[:, b, 2 * j + t, :], ident[:, :])
                last.then_inc(M["qT_psum"], 1)
            pe.wait_ge(M["wkT_done"], H // 4)
            for j in range(H // 2):
                pe.wait_ge(M["qT_done"], j + 1)
                if j >= 2:
                    pe.wait_ge(M["q3_lo_done"], j - 1)
                for t in range(2):
                    h = 2 * j + t
                    last = pe.matmul(ps[:, 6 + j % 2, t * B * S:(t + 1) * B * S], wkT[:, h, :], qT[:, h, :], start=True, stop=True)
                last.then_inc(M["q3_psum"], 1)
            pe.wait_ge(M["wk_split"], 1)
            pe.wait_ge(M["ctxT_lo_done"], B * NC // 4)
            for c in range(B * NC):
                for g in range(NG):
                    i = c * NG + g
                    if i >= 4:
                        pe.wait_ge(M["k_squared"], i - 3)
                    r = slice(g * 512, (g + 1) * 512)
                    pe.matmul(ps[:, i % 4, :], ctxT_hi[:, c, :], wk_hi[:, r], start=True, stop=False)
                    pe.matmul(ps[:, i % 4, :], ctxT_hi[:, c, :], wk_lo[:, r], start=False, stop=False)
                    pe.matmul(ps[:, i % 4, :], ctxT_lo[:, c, :], wk_hi[:, r], start=False, stop=True).then_inc(M["k_psum"], 1)
            pe.wait_ge(M["q3_lo_done"], H // 2)
            pe.wait_ge(M["k_squared"], B * NC * NG)

            STEPS = B * NG * (NC // 2)

            def scores(i):
                b, g, c2 = i // (NG * NC // 2), i // (NC // 2) % NG, i % (NC // 2)
                if i >= 2:
                    pe.wait_ge(M["s_scaled"], i - 1)
                for t in range(2):
                    c = b * NC + 2 * c2 + t
                    bank = 2 * (i % 2) + t
                    q_hi = q3_hi[:, b, G * g:G * g + G, :]
                    q_lo = q3_lo[:, b, G * g:G * g + G, :]
                    pe.matmul(ps[:, bank, :], ctxT_hi[:, c, :], q_hi, start=True, stop=False)
                    pe.matmul(ps[:, bank, :], ctxT_hi[:, c, :], q_lo, start=False, stop=False)
                    last = pe.matmul(ps[:, bank, :], ctxT_lo[:, c, :], q_hi, start=False, stop=True)
                last.then_inc(M["s_psum"], 1)

            def weighted_sums(i):
                b, g, c2 = i // (NG * NC // 2), i // (NC // 2) % NG, i % (NC // 2)
                j = b * NG + g
                pe.wait_ge(M["p_done"], i + 1)
                if c2 == 0 and j >= 2:
                    pe.wait_ge(M["o_done"], j - 1)
                for t in range(2):
                    c = b * NC + 2 * c2 + t
                    for h in range(G):
                        at = ps[:, 4 + 2 * (j % 2) + h // 2, (h % 2) * (C + 2):(h % 2) * (C + 2) + C + 1]
                        first = c2 == 0 and t == 0
                        last = pe.matmul(at, p_sb[:, i % 2, t, h * S:(h + 1) * S], ctx_nat[:, c, 0:C + 1],
                                         start=first and h % 2 == 0, stop=(c2 == NC // 2 - 1 and t == 1), skip_group_check=True)
                last.then_inc(M["pv_chunk"], 1)
                if c2 == NC // 2 - 1:
                    pe.wait_ge(M["pv_chunk"], i + 1)
                    pe.nop().then_inc(M["o_psum"], 1)

            for i in range(STEPS + 1):
                if i < STEPS:
                    scores(i)
                if i >= 1:
                    weighted_sums(i - 1)
            pe.wait_ge(M["o_done"], B * NG)
            pe.wait_ge(M["wv_loaded"], 16)
            pe.wait_ge(M["wo_loaded"], 16)
            for j in range(H // 2):
                if j >= 2:
                    pe.wait_ge(M["oT_done"], j - 1)
                for t in range(2):
                    for b in range(B):
                        last = pe.transpose(ps[:, j % 2, (t * B + b) * P:(t * B + b + 1) * P], o_n[:, b, 2 * j + t, :], ident[:, :])
                last.then_inc(M["oT_psum"], 1)
            for j in range(H // 2):
                pe.wait_ge(M["oT_done"], j + 1)
                if j >= 2:
                    pe.wait_ge(M["aT_done"], j - 1)
                for t in range(2):
                    h = 2 * j + t
                    last = pe.matmul(ps[:, 2 + j % 2, t * B * S:(t + 1) * B * S], wv[:, h, :], oT[:, h, :], start=True, stop=True)
                last.then_inc(M["aT_psum"], 1)
            pe.wait_ge(M["aT_done"], H // 2)
            for b in range(B):
                for h in range(H):
                    last = pe.matmul(ps[:, 4 + b, 0:D], aT[:, h, b * S:(b + 1) * S], wo[:, h, :], start=(h == 0), stop=(h == H - 1))
                last.then_inc(M["y_psum"], 1)

            if upto < 2:
                return
            xn_transposes(1)
            pe.wait_ge(M["xnT_ready"], 2)
            pe.wait_ge(M["sa_w_loaded"], 128)
            for t in range(2):
                for j in range(KC):
                    for kc in range(KC):
                        last = pe.matmul(ps[:, 1 + t, j * B * S:(j + 1) * B * S], w_in[:, kc, t * D + j * P:t * D + (j + 1) * P],
                                         xnT[:, kc, :], start=(kc == 0), stop=(kc == KC - 1))
            last.then_inc(M["sa_q_psum"], 1)
            for b in range(B):
                for kc in range(KC):
                    pe.matmul(ps[:, 3, b * D:(b + 1) * D], xnT[:, kc, b * S:(b + 1) * S], w_in[:, kc, 2 * D:3 * D], start=(kc == 0), stop=False)
                last = pe.matmul(ps[:, 3, b * D:(b + 1) * D], ones[0:1, :], b_in_row[:, 2 * D:3 * D], start=False, stop=True)
            last.then_inc(M["sa_v_psum"], 1)
            for b in range(B):
                if b == 1:
                    pe.wait_ge(M["sa_v_done"], 2)
                    pe.wait_ge(M["sa_qkT"], 2 * KC)
                for j in range(KC):
                    i = b * KC + j
                    pe.wait_ge(M["sa_km_done"], i + 1)
                    for t in range(2):
                        last = pe.matmul(ps[:, 4 * (1 - b) + 2 * j + t, :], sa_qT[:, j, b * S:(b + 1) * S],
                                         sa_km[:, i % 2, 4 * t:4 * t + 4, :], start=True, stop=True)
                    last.then_inc(M["sa_s_psum"], 1)
            for b in range(B):
                pe.wait_ge(M["sa_p_done"], b + 1)
                for g in range(4):
                    for t in range(4):
                        last = pe.transpose(ps[:, 4 * (1 - b) + g, t * P:(t + 1) * P], sa_s[:, b, 4 * g + t, :], ident[:, :])
                    last.then_inc(M["sa_pT_psum"], 1)
            for b in range(B):
                pe.wait_ge(M["sa_pT_done"], 4 * b + 4)
                for h in range(H):
                    last = pe.matmul(ps[:, 4 * (1 - b), h * (HD + 2):h * (HD + 2) + HD + 1], sa_pT[:, b, h, :], sa_v[:, b, h, 0:HD + 1],
                                     start=True, stop=True)
                last.then_inc(M["sa_o_psum"], 1)
            for b in range(B):
                pe.wait_ge(M["sa_o_done"], b + 1)
                for kc in range(KC):
                    last = pe.transpose(ps[:, 4 * (1 - b) + 1, kc * S:(kc + 1) * S], sa_o[:, b, kc * P:(kc + 1) * P], ident[:, :])
                last.then_inc(M["sa_oT_psum"], 1)
            for b in range(B):
                pe.wait_ge(M["sa_oT_done"], b + 1)
                y = ps[:, 4 * (1 - b) + 2, 0:D]
                for kc in range(KC):
                    pe.matmul(y, sa_oT[:, kc, b * S:(b + 1) * S], w_out[:, kc, :], start=(kc == 0), stop=False)
                pe.matmul(y, ones[0:1, :], b_out_row[:, :], start=False, stop=True).then_inc(M["y_psum"], 1)
            if upto < 3:
                return
            pe.wait_ge(M["wabs_done"], 2)
            pe.matmul(ps[:, 3, 0:2], ones[:, :], w_abs[:, :], start=True, stop=True).then_inc(M["wabs_psum"], 1)
            for i in range(8):
                pe.wait_ge(M["wq_quant"], 1 + i // 4)
                if i >= 4:
                    pe.wait_ge(M["wqT_done"], i - 3)
                if i == 0:
                    pe.wait_ge(M["x_updated"], 2 * B)
                for t in range(4):
                    if i < 4:
                        src = w1[:, 4 * (i % 2) + t, (i // 2) * P:(i // 2 + 1) * P]
                    else:
                        ic, o = 2 * (i - 4) + t // 2, t % 2
                        src = w2[:, o, ic * P:(ic + 1) * P]
                    last = pe.transpose(ps[:, 4 + i % 4, t * P:(t + 1) * P], src, ident[:, :])
                last.then_inc(M["wqT_psum"], 1)
            pe.wait_ge(M["ff_q_done"], B)
            for kc in range(KC):
                for b in range(B):
                    last = pe.transpose(ps[:, 0, (kc * B + b) * P:(kc * B + b + 1) * P], ff_q1[:, b, kc * P:(kc + 1) * P], ident[:, :])
            last.then_inc(M["ff_qT_psum"], 1)
            pe.wait_ge(M["ff_qT_done"], 1)
            pe.wait_ge(M["wqT_done"], 8)
            for b in range(B):
                for t in range(2):
                    for kc in range(KC):
                        last = pe.matmul(ps[:, 4 + 2 * b + t, :], ff_qT1[:, kc, b * S:(b + 1) * S], w1qT[:, kc, t * 512:(t + 1) * 512],
                                         start=(kc == 0), stop=(kc == KC - 1))
                last.then_inc(M["ff_h_psum"], 1)
            for b in range(B):
                pe.wait_ge(M["ff_q_done"], B + b + 1)
                for g in range(2):
                    for t in range(4):
                        last = pe.transpose(ps[:, 4 + 2 * b + g, t * P:(t + 1) * P], ff_h[:, b, (4 * g + t) * P:(4 * g + t + 1) * P], ident[:, :])
                    last.then_inc(M["ff_qT_psum"], 1)
            for b in range(B):
                pe.wait_ge(M["ff_qT_done"], 1 + 2 * (b + 1))
                for ic in range(FC):
                    last = pe.matmul(ps[:, 1 + b, 0:D], ff_qT2[:, ic, b * S:(b + 1) * S], w2qT[:, ic, :], start=(ic == 0), stop=(ic == FC - 1))
                last.then_inc(M["y_psum"], 1)
            if upto < 4:
                return

            def key_products(b):
                for g in range(4):
                    if g == 0 and b == 0:
                        pe.wait_ge(M["x_updated"], 3 * B)
                    for t in range(4):
                        last = pe.transpose(ps[:, 1 + g, t * P:(t + 1) * P], ctx_nat[:, b * NC + 4 * g + t, 0:C], ident[:, :])
                    last.then_inc(M["xb_cT_psum"], 1)
                pe.wait_ge(M["xb_cT_done"], 4 * (b + 1))
                pe.wait_ge(M["xb_centred"], 2)
                for c in range(NC):
                    n = b * NC + c
                    if c >= 4:
                        pe.wait_ge(M["xb_kv_done"], n - 3)
                    pe.matmul(ps[:, 1 + c % 4, :], xb_cT[:, c, :], xb_wkv[:, :], start=True, stop=True).then_inc(M["xb_kv_psum"], 1)

            key_products(0)
            xn_transposes(3)
            pe.wait_ge(M["xnT_ready"], 3)
            pe.wait_ge(M["xb_w_loaded"], 13 * 16)
            for b in range(B):
                for kc in range(KC):
                    last = pe.matmul(ps[:, 0, b * D:(b + 1) * D], xnT[:, kc, b * S:(b + 1) * S], xb_wq[:, kc, :], start=(kc == 0), stop=(kc == KC - 1))
            last.then_inc(M["xb_q_psum"], 1)
            for b in range(B):
                last = pe.transpose(ps[:, 5, b * DCA:(b + 1) * DCA], xb_yd[:, b, :], ident[0:DCA, 0:DCA])
            last.then_inc(M["xb_last_psum"], 1)
            pe.wait_ge(M["xb_last_act"], 1)
            pe.wait_ge(M["xb_kv_done"], NC)
            for b in range(B):
                pe.matmul(ps[:, 3 + b, :], xb_ydT[:, b, :, :].rearrange("p r k -> p (r k)"), xb_wd[:, :], start=True, stop=True).then_inc(M["xb_last_psum"], 1)
            pe.wait_ge(M["xb_q_done"], 1)
            for kc in range(KC):
                for b in range(B):
                    pe.transpose(ps[:, 6, (kc * B + b) * S:(kc * B + b + 1) * S], xb_q[:, b, kc * P:(kc + 1) * P], ident[:, :])
            pe.wait_ge(M["xb_kdm_done"], B)
            for b in range(B):
                for kc in range(KC):
                    last = pe.transpose(ps[:, 5, (b * KC + kc) * P:(b * KC + kc + 1) * P], xb_kdm[:, b, kc * P:(kc + 1) * P], ident[:, :])
            last.then_inc(M["xb_last_psum"], 1)
            pe.wait_ge(M["xb_last_act"], 4)
            for b in range(B):
                for kc in range(KC):
                    last = pe.matmul(ps[:, 5, b * D + kc * P:b * D + (kc + 1) * P], xb_qfT[:, kc, b * S:(b + 1) * S], xb_kdT[:, b, kc, :], start=True, stop=True)
            last.then_inc(M["xb_last_psum"], 1)
            pe.wait_ge(M["xb_pd_done"], 1)
            for kc in range(KC):
                for b in range(B):
                    last = pe.transpose(ps[:, 6, (kc * B + b) * S:(kc * B + b + 1) * S], xb_pd[:, b, kc * P:(kc + 1) * P], ident[:, :])
            last.then_inc(M["xb_last_psum"], 1)
            pe.wait_ge(M["xb_last_act"], 6)
            for b in range(B):
                for kc in range(KC):
                    last = pe.matmul(ps[:, 5, b * D + kc * P:b * D + (kc + 1) * P], xb_pdT[:, kc, b * S:(b + 1) * S],
                                     xb_kdm[:, b, D + kc * P:D + (kc + 1) * P], start=True, stop=True)
            last.then_inc(M["xb_last_psum"], 1)
            pe.wait_ge(M["xb_od_done"], 1)

            def k_transposes(n, g):
                pe.wait_ge(M["xb_klo"], n + 1)
                if 4 * n + g >= 2:
                    pe.wait_ge(M["xb_kT_done"], 4 * n + g - 1)
                for t in range(4):
                    last = pe.transpose(ps[:, 4 * (g % 2), t * P:(t + 1) * P],
                                        xb_kn[:, 4 * g + t, :, :].bitcast(F32).rearrange("p h w -> p (h w)"), ident[:, :])
                last.then_inc(M["xb_kT_psum"], 1)

            def maxima(n, m):
                pe.wait_ge(M["xb_kT_done"], 4 * n + m // 2 + 1)
                if 8 * n + m >= 3:
                    pe.wait_ge(M["xb_m_done"], 8 * n + m - 2)
                r = slice(W * (m % 2), W * (m % 2) + W)
                pe.matmul(ps[:, 1 + (8 * n + m) % 3, :], xb_qT1[r, n % PAIRS, :], xb_kT[r, n % 2, 4 * (m // 2):4 * (m // 2) + 4, :],
                          start=True, stop=True).then_inc(M["xb_m_psum"], 1)

            def q_transpose(n):
                i = n % PAIRS
                pe.wait_ge(M["xb_row_done"], n + 1)
                pe.wait_ge(M["xb_kT_done"], min(4 * n + 7, 4 * PAIRS * (n // PAIRS + 1)))
                pe.transpose(ps[:, 0, 0:S], xb_qn[:, 2 * i:2 * i + 2, :].bitcast(F32).rearrange("p h w -> p (h w)"), ident[:, :]).then_inc(M["xb_q2_psum"], 1)

            def scores_t(n, u):
                m = n * NU + u
                pe.wait_ge(M["xb_q2_done"], n + 1)
                if m >= 2:
                    pe.wait_ge(M["xb_p_done"], m - 1)
                for t in range(2):
                    last = pe.matmul(ps[:, 5 + u % 2, t * 2 * S:(t + 1) * 2 * S], xb_kT[:, n % 2, 2 * u + t, :], xb_qT2[:, n % 2, :],
                                     start=True, stop=True)
                last.then_inc(M["xb_s_psum"], 1)

            def head_sums(n, u):
                m, i = n * NU + u, n % PAIRS
                pe.wait_ge(M["xb_p_done"], m + 1)
                for t in range(2):
                    c = 2 * u + t
                    for h in (2 * i, 2 * i + 1):
                        last = pe.matmul(ps[32 * (h % 4):32 * (h % 4) + 32, 7, (h // 4) * S:(h // 4 + 1) * S], xb_kv[0:P - 1, c, h, 1:2 * HD + 1],
                                         xb_p[0:P - 1, m % 2, 2 * t + h % 2, :], start=(c == 0), stop=(c == NC - 1), skip_group_check=True)
                last.then_inc(M["xb_pv_done"], 1)

            for b in range(B):
                if b == 1:
                    pe.wait_ge(M["xb_m_done"], 8 * PAIRS)
                    key_products(1)
                pe.wait_ge(M["xb_qn_done"], b + 1)
                pe.wait_ge(M["xb_kv_done"], (b + 1) * NC)
                for g in range(2):
                    for t in range(4):
                        j = 4 * g + t
                        last = pe.transpose(ps[:, 1 + g, t * P:(t + 1) * P], xb_qn[:, 2 * j:2 * j + 2, :].bitcast(F32).rearrange("p h w -> p (h w)"), ident[:, :])
                    last.then_inc(M["xb_q1_psum"], 1)
                pe.wait_ge(M["xb_q1_done"], 2 * (b + 1))
                if b == 1:
                    pe.wait_ge(M["xb_o_done"], 1)
                for g in range(4):
                    k_transposes(b * PAIRS, g)
                for i in range(PAIRS + 1):
                    n = b * PAIRS + i
                    for u in range(NU + 1):
                        if i >= 1 and u < NU:
                            scores_t(n - 1, u)
                        if i < PAIRS and u < 4:
                            maxima(n, 2 * u)
                            maxima(n, 2 * u + 1)
                        if i + 1 < PAIRS and u in (2, 4, 6, 8):
                            k_transposes(n + 1, u // 2 - 1)
                        if i < PAIRS and u == 7:
                            q_transpose(n)
                        if i >= 1 and u >= 1:
                            head_sums(n - 1, u - 1)
                pe.wait_ge(M["xb_pv_done"], (b + 1) * PAIRS * NU)
                pe.nop().then_inc(M["xb_o_psum"], 1)
                pe.wait_ge(M["xb_oh_done"], b + 1)
                pe.wait_ge(M["xb_p_done"], (b + 1) * PAIRS * NU)
                for g in range(4):
                    last = pe.transpose(ps[:, 5, g * S:(g + 1) * S], xb_oh[:, g * S:(g + 1) * S], ident[:, :])
                last.then_inc(M["xb_ohT_psum"], 1)
            for b in range(B):
                pe.wait_ge(M["xb_o_done"], b + 1)
                for kc in range(KC):
                    last = pe.transpose(ps[:, 1 + b, kc * S:(kc + 1) * S], xb_o[:, b, kc * P:(kc + 1) * P], ident[:, :])
                last.then_inc(M["xb_oT_psum"], 1)
            for b in range(B):
                pe.wait_ge(M["xb_oT_done"], b + 1)
                for kc in range(KC):
                    pe.matmul(ps[:, 3 + b, 0:D], xb_qfT[:, kc, b * S:(b + 1) * S], xb_wo[:, kc, :], start=(kc == 0), stop=False)
                pe.matmul(ps[:, 3 + b, 0:D], ones[0:1, :], xb_wo_row[:, :], start=False, stop=True).then_inc(M["y_psum"], 1)
            if upto < 5:
                return

            pe.wait_ge(M["sb_dve"], 1)
            for kc in range(KC):
                for b in range(B):
                    last = pe.transpose(ps[:, 0, (kc * B + b) * P:(kc * B + b + 1) * P], sb_h[:, b, kc * P:(kc + 1) * P], ident[:, :])
            last.then_inc(M["sb_psum"], 1)
            pe.wait_ge(M["sb_act"], 1)
            for t in range(2):
                for j in range(KC):
                    for kc in range(KC):
                        last = pe.matmul(ps[:, 1 + t, j * B * S:(j + 1) * B * S], sb_w[:, kc, t * D + j * P:t * D + (j + 1) * P], sb_hT[:, kc, :],
                                         start=(kc == 0), stop=(kc == KC - 1))
            last.then_inc(M["sb_psum"], 1)
            pe.wait_ge(M["x_updated"], 4 * B)
            for b in range(B):
                for kc in range(KC):
                    last = pe.matmul(ps[:, 3, b * D:(b + 1) * D], sb_hT[:, kc, b * S:(b + 1) * S], sb_w[:, kc, 2 * D:3 * D], start=(kc == 0), stop=(kc == KC - 1))
            last.then_inc(M["sb_psum"], 1)
            pe.wait_ge(M["sb_act"], 3)
            for b in range(B):
                for kc in range(KC):
                    last = pe.matmul(ps[:, 4, b * S:(b + 1) * S], sb_qT[:, kc, b * S:(b + 1) * S], sb_kT[:, kc, b * S:(b + 1) * S], start=(kc == 0), stop=(kc == KC - 1))
            last.then_inc(M["sb_psum"], 1)
            pe.wait_ge(M["sb_dve"], 3)
            for b in range(B):
                last = pe.transpose(ps[:, 5, b * S:(b + 1) * S], sb_s[:, b, :], ident[:, :])
            last.then_inc(M["sb_psum"], 1)
            pe.wait_ge(M["sb_act"], 6)
            pe.wait_ge(M["sb_act"], 4)
            for kc in range(KC):
                for b in range(B):
                    last = pe.matmul(ps[:, 6, (kc * B + b) * S:(kc * B + b + 1) * S], sb_v[:, b, kc * P:(kc + 1) * P], sb_pT[:, b, :], start=True, stop=True)
            last.then_inc(M["sb_psum"], 1)
            pe.wait_ge(M["sb_act"], 7)
            for b in range(B):
                for kc in range(KC):
                    last = pe.matmul(ps[:, 7, b * D:(b + 1) * D], sb_oT[:, kc, b * S:(b + 1) * S], sb_wo[:, kc, :], start=(kc == 0), stop=(kc == KC - 1))
                last.then_inc(M["y_psum"], 1)
            if upto < 6:
                return

            pe.wait_ge(M["mo_r_loaded"], 32)
            for kc in range(KC):
                last = pe.transpose(ps[:, 1, kc * E:(kc + 1) * E], mo_r[:, kc * P:(kc + 1) * P], ident[0:E, 0:E])
            last.then_inc(M["mo_psum"], 1)
            xn_transposes(5)
            pe.wait_ge(M["xnT_ready"], 4)
            pe.wait_ge(M["mo_act"], 1)
            for b in range(B):
                for kc in range(KC):
                    last = pe.matmul(ps[:, 2, b * E:(b + 1) * E], xnT[:, kc, b * S:(b + 1) * S], mo_rT[:, kc, :], start=(kc == 0), stop=(kc == KC - 1))
            last.then_inc(M["mo_psum"], 1)
            pe.wait_ge(M["mo_w_loaded"], 16 * 16)
            pe.wait_ge(M["mo_down_loaded"], 8 * 16)
            for e in range(E + 1):
                if e < E:
                    if e >= 2:
                        pe.wait_ge(M["mo_a_done"], e - 1)
                    for t, w in ((0, mo_gate), (1, mo_up)):
                        for ic in range(IC):
                            for kc in range(KC):
                                last = pe.matmul(ps[0:IP, 3 + 2 * (e % 2) + t, ic * B * S:(ic + 1) * B * S], w[:, e, kc, ic * IP:(ic + 1) * IP], xnT[:, kc, :],
                                                 start=(kc == 0), stop=(kc == KC - 1))
                    last.then_inc(M["mo_gu_psum"], 1)
                if e >= 1:
                    f = e - 1
                    pe.wait_ge(M["mo_a_done"], f + 1)
                    if f == 1:
                        pe.wait_ge(M["x_updated"], 5 * B)
                    if f >= 2:
                        pe.wait_ge(M["mo_y_done"], B * (f - 1))
                    for b in range(B):
                        for ic in range(IC):
                            last = pe.matmul(ps[:, 7 * (f % 2), b * D:(b + 1) * D], mo_a[:, f % 2, ic, b * S:(b + 1) * S], mo_down[:, f, ic, :],
                                             start=(ic == 0), stop=(ic == IC - 1))
                    last.then_inc(M["mo_y_psum"], 1)


def kernel(**inputs):
    import concourse.bacc as bacc
    from concourse.bass_utils import run_bass_kernel_spmd

    nc = bacc.Bacc("TRN2", target_bir_lowering=False, num_devices=1)
    arrays, args = {}, {}
    for name, value in inputs.items():
        value = np.ascontiguousarray(value)
        arrays[f"in_{name}"] = value
        args[name] = nc.dram_tensor(f"in_{name}", value.shape, mybir.dt.from_np(value.dtype), kind="ExternalInput").ap()
    out = nc.dram_tensor("out", inputs["x"].shape, F32, kind="ExternalOutput").ap()
    build(nc, args, out)
    return run_bass_kernel_spmd(nc, [arrays], core_ids=[0]).results[0]["out"]
```

```python
from contextlib import ExitStack

import numpy as np
import concourse.bass as bass
from concourse import mybir

F32 = mybir.dt.float32
F32R = mybir.dt.float32r
BF16 = mybir.dt.bfloat16
ALU = mybir.AluOpType
ACT = mybir.ActivationFunctionType
AX = mybir.AxisListType

P = 128
EPS = 1e-5


def build(nc, a, out, upto=6):
    B, S, D = a["x"].shape
    KV = a["ctx_1024"].shape[1]
    C = a["ctx_1024"].shape[2]
    H = 16
    HD0 = a["L0_xattn_gq"].shape[0]
    NC = KV // P
    KC = D // P
    G = 4
    NG = H // G
    assert S == P and C == P and HD0 == P

    ctx = ExitStack()
    with ctx:
        def sb(name, shape, dt=F32):
            return ctx.enter_context(nc.sbuf_tensor(name, shape, dt))

        def sem(name):
            return ctx.enter_context(nc.semaphore(name))

        ps = ctx.enter_context(nc.psum_tensor("ps", [P, 8, 512], F32))

        ident = sb("ident", [P, P])
        ones = sb("ones", [P, P])
        neg_half = sb("neg_half", [P, 32])
        x_sb = sb("x_sb", [P, B, D])
        stats = sb("stats", [P, B, 6])
        meanvar = sb("meanvar", [P, B, 2])
        veps = sb("veps", [P, B])
        rstd = sb("rstd", [P, B])
        xn = sb("xn", [P, B, D])
        xnT = sb("xnT", [P, KC, B * S])
        ctx_nat = sb("ctx_nat", [P, B * NC, C + 2])
        KB = 1024
        ARENA = 168 * KB
        arena_start = nc.sbuf_base
        arena = sb("arena", [P, ARENA // 4])
        base = -(-arena_start // 32) * 32

        def at(name, offset, shape, dt=F32):
            size = int(np.prod(shape[1:])) * mybir.dt.size(dt)
            assert offset + size <= ARENA
            return nc.alloc_sbuf_tensor_at(name, shape, dt, offset=base + offset)

        ctxT_hi = at("ctxT_hi", 0, [P, B * NC, P], F32R)
        ctxT_lo = at("ctxT_lo", 16 * KB, [P, B * NC, P], F32R)
        wk_hi = at("wk_hi", 32 * KB, [P, H * HD0], F32R)
        wk_lo = at("wk_lo", 40 * KB, [P, H * HD0], F32R)
        wk = at("wk", 48 * KB, [P, H * HD0])
        s_sb = at("s_sb", 48 * KB, [P, 2, 2, 512])
        wkT = at("wkT", 56 * KB, [P, H, C])
        p_sb = at("p_sb", 56 * KB, [P, 2, 2, 512])
        q3_hi = at("q3_hi", 64 * KB, [P, B, H, S], F32R)
        q3_lo = at("q3_lo", 80 * KB, [P, B, H, S], F32R)
        wq = at("wq", 96 * KB, [P, KC, H * HD0])
        wv = at("wv", 112 * KB, [P, H, HD0])
        wo = at("wo", 120 * KB, [P, H, D])
        qn = at("qn", 136 * KB, [P, B, H, HD0])
        qT = at("qT", 152 * KB, [P, H, B * S])
        gains = sb("gains", [P, 2])
        gqk = sb("gqk", [P, 1])
        sq = sb("sq", [P, 2, 512])
        q_sq = at("q_sq", 64 * KB, [P, 2, 512])
        q_ss = sb("q_ss", [P, B, H])
        q_rstd = sb("q_rstd", [P, B, H])
        k_stats = sb("k_stats", [P, 2, B * NC, H])
        k_ss, k_rstd = k_stats[:, 0, :, :], k_stats[:, 1, :, :]
        shift = sb("shift", [P, 1])
        o_den = sb("o_den", [P, B * NG, G])
        o_n = qn
        oT = qT
        aT = at("aT", 64 * KB, [P, H, B * S])

        HD = D // H
        w_in = at("w_in", 0, [P, KC, 3 * D])
        w_out = at("w_out", 6 * KB, [P, KC, D])
        bqk = sb("bqk", [P, 2 * KC])
        b_in_row = at("b_in_row", 16 * KB, [1, 3 * D])
        b_out_row = at("b_out_row", 19 * KB, [1, D])
        head_mask = sb("head_mask", [P, 8])
        causal = at("causal", 28 * KB, [P, S])
        sa_s = at("sa_s", 152 * KB, [P, B, H, S])
        sa_qT = at("sa_qT", 120 * KB, [P, KC, B * S])
        sa_kT = at("sa_kT", 122 * KB, [P, KC, B * S])
        sa_km = at("sa_km", 124 * KB, [P, 2, 8, S])
        sa_v = at("sa_v", 132 * KB, [P, B, H, HD + 2])
        sa_o = at("sa_o", 135 * KB, [P, B, D])
        sa_oT = at("sa_oT", 137 * KB, [P, KC, B * S])
        sa_pT = at("sa_pT", 48 * KB, [P, B, H, S])
        sa_max = sb("sa_max", [P, B, H])
        sa_den = sb("sa_den", [P, B, H])
        FI = a["L0_ffn_w1"].shape[0]
        FC = FI // P
        w1 = at("w1", 96 * KB, [P, FC, D])
        w2 = at("w2", 104 * KB, [P, KC, FI])
        w1qT = at("w1qT", 139 * KB, [P, KC, FI], BF16)
        w2qT = at("w2qT", 143 * KB, [P, FC, D], BF16)
        b1_all = at("b1_all", 8 * KB, [P, FI])
        lng_all = at("lng_all", 12 * KB, [P, FI])
        lnb_all = at("lnb_all", 24 * KB, [P, FI])
        b2_all = at("b2_all", 20 * KB, [P, D])
        w_sizes = at("w_sizes", 136 * KB, [P, FC * D])
        w_abs = sb("w_abs", [P, 2])
        w_mean = sb("w_mean", [P, 2])
        w_scale = sb("w_scale", [P, 2])
        ff_ss = sb("ff_ss", [P, 2, B])
        ff_r = sb("ff_r", [P, 2, B])
        ff_max = sb("ff_max", [P, 2, B])
        ff_s = sb("ff_s", [P, 2, B])
        ff_dq = sb("ff_dq", [P, 2, B])
        ff_q1 = at("ff_q1", 128 * KB, [P, B, D])
        ff_sq = at("ff_sq", 152 * KB, [P, B, FI])
        ff_qT1 = at("ff_qT1", 130 * KB, [P, KC, B * S], BF16)
        ff_h = at("ff_h", 48 * KB, [P, B, FI])
        ff_h2 = at("ff_h2", 56 * KB, [P, B, FI])
        ff_qT2 = at("ff_qT2", 124 * KB, [P, FC, B * S], BF16)
        ff_stats = sb("ff_stats", [P, B, 2, 6])
        ff_mv = sb("ff_mv", [P, B, 2])
        ff_rstd = sb("ff_rstd", [P, B])

        DCA = 16
        assert DCA == NC
        PAIRS = H // 2
        W = 64
        NU = NC // 2
        EPS2 = 1e-6
        SC = float(HD) ** -0.5
        UNITS = PAIRS * NU
        KEY_BANKS = [7, 3] * (NC // 4) + [3, 0] * (NC // 4)
        xb_cT = [at("xb_cT_first", 112 * KB, [P, NC, P]), at("xb_cT_second", 0, [P, NC, P])]
        xb_kn = [at("xb_kn_even", 0, [P, NC, 2, W], F32R), at("xb_kn_odd", 141 * KB, [P, NC, 2, W], F32R)]
        xb_kv = at("xb_kv", 64 * KB, [P, NC, H, 2 * HD + 1])
        xb_p = at("xb_p", 126 * KB, [P, 2, 4, S])
        xb_qn = at("xb_qn", 48 * KB, [P, H, W], F32R)
        xb_qT1 = at("xb_qT1", 52 * KB, [P, PAIRS, S], F32R)
        xb_qT2 = at("xb_qT2", 130 * KB, [P, 2, 2 * S], F32R)
        xb_kt = at("xb_kt", 56 * KB, [P, NC, 2, HD])
        xb_oh = at("xb_oh", 56 * KB, [P, 4 * S])
        xb_kT = at("xb_kT", 152 * KB, [P, 2, NC, P], F32R)
        xb_wkv = at("xb_wkv", 36 * KB, [P, 2 * D])
        xb_bkv = at("xb_bkv", 38 * KB, [P, 2 * D])
        xb_wq = at("xb_wq", 40 * KB, [P, KC, D])
        xb_wo = at("xb_wo", 42 * KB, [P, KC, D])
        xb_wd = at("xb_wd", 44 * KB, [P, 2 * D])
        xb_bd = at("xb_bd", 46 * KB, [P, 2 * D])
        xb_bq = at("xb_bq", 30 * KB, [P, D])
        xb_q = at("xb_q", 133 * KB, [P, B, D])
        xb_qk = at("xb_qk", 135 * KB, [P, B, D])
        xb_t = at("xb_t", 137 * KB, [P, B, D])
        xb_qfT = at("xb_qfT", 139 * KB, [P, KC, B * S])
        xb_kd = k_stats[:, :, :, :].rearrange("p b n h -> p b (n h)")
        xb_kdm = [xn[:, :, :].rearrange("p b d -> p (b d)"), xnT[:, :, :].rearrange("p k s -> p (k s)")]
        xb_kdT = at("xb_kdT", 149 * KB, [P, B, KC, P])
        xb_wo_row = at("xb_wo_row", 151 * KB, [1, D])
        xb_yd = sb("xb_yd", [DCA, B, C])
        xb_ydT = sb("xb_ydT", [P, B, 8, DCA])
        xb_pd = at("xb_pd", 58 * KB, [P, B, D])
        xb_pdT = at("xb_pdT", 60 * KB, [P, KC, B * S])
        xb_o = at("xb_o", 62 * KB, [P, B, D])
        eps2 = sb("eps2", [P, 1])
        xb_vec = sb("xb_vec", [P, 6, HD])
        xb_ss = sb("xb_ss", [P, NC, H])
        xb_rk = sb("xb_rk", [P, NC, H])
        xb_s32 = sb("xb_s32", [P, 4, B * H])
        xb_d32 = sb("xb_d32", [P, 4, B * H])
        xb_qb = sb("xb_qb", [P, B * H])
        xb_pm = sb("xb_pm", [P, 2, 8])
        xb_m = sb("xb_m", [P, 2, 2])
        xb_den = sb("xb_den", [P, B, H])

        sb_w = at("sb_w", 126 * KB, [P, KC, 3 * D])
        sb_wo = at("sb_wo", 132 * KB, [P, KC, D])
        sb_g = at("sb_g", 134 * KB, [P, 2, D])
        sb_h = at("sb_h", 136 * KB, [P, B, D])
        sb_hT = at("sb_hT", 138 * KB, [P, KC, B * S])
        sb_qT = at("sb_qT", 140 * KB, [P, KC, B * S])
        sb_kT = at("sb_kT", 142 * KB, [P, KC, B * S])
        sb_v = at("sb_v", 144 * KB, [P, B, D])
        sb_s = at("sb_s", 146 * KB, [P, B, S])
        sb_pT = at("sb_pT", 147 * KB, [P, B, S])
        sb_oT = at("sb_oT", 148 * KB, [P, KC, B * S])
        causal2 = at("causal2", 150 * KB, [P, S])
        sb_mv = sb("sb_mv", [P, B, 2])
        sb_rstd = sb("sb_rstd", [P, B])
        sb_m = sb("sb_m", [P, 3, B])
        E = a["L1_ffn_router_w"].shape[0]
        TOP = 4
        EI = a["L1_ffn_gate_proj"].shape[2]
        IC = 2
        IP = EI // IC
        mo_gate = at("mo_gate", 8 * KB, [P, E, KC, EI])
        mo_up = at("mo_up", 98 * KB, [P, E, KC, EI])
        mo_down = at("mo_down", 36 * KB, [IP, E, IC, D])
        mo_r = at("mo_r", 68 * KB, [E, D])
        mo_rT = at("mo_rT", 69 * KB, [P, KC, E])
        mo_bias = at("mo_bias", 70 * KB, [P, E])
        mo_s = at("mo_s", 71 * KB, [P, B, E])
        mo_gt = at("mo_gt", 72 * KB, [P, B, E, E])
        mo_eq = at("mo_eq", 74 * KB, [P, B, E, E])
        mo_rank = at("mo_rank", 76 * KB, [P, B, E])
        mo_first = at("mo_first", 77 * KB, [P, E, E])
        mo_m = sb("mo_m", [P, 3, B])
        mo_sg = at("mo_sg", 80 * KB, [IP, 2, IC, B * S])
        mo_a = at("mo_a", 84 * KB, [IP, 2, IC, B * S])

        names = ["x_loaded", "ctx_loaded", "ctx1_loaded", "wk_loaded", "wq_loaded", "wv_loaded", "wo_loaded", "gains_loaded", "sb_psum", "sb_act", "sb_dve", "mo_psum", "mo_act", "xb_last_psum", "xb_last_act", "out_done",
                 "const_made", "pool_chain", "ident_ready", "dve_chain", "ln_var", "ln_rstd", "xn_ready", "xT_psum", "xnT_ready",
                 "ctxT_psum", "ctxT_hi_done", "ctxT_lo_done", "wk_split", "wkT_psum", "wkT_done", "q_psum", "q_squared", "q_ss_done",
                 "q_rstd_done", "qn_done", "qT_psum", "qT_done", "gqk_done", "q3_psum", "q3_hi_done", "q3_lo_done",
                 "k_psum", "k_squared", "k_ss_done", "k_rstd_done", "s_psum", "s_scaled", "p_done", "pv_chunk", "o_psum", "o_done",
                 "oT_psum", "oT_done", "aT_psum", "aT_done", "y_psum", "x_updated",
                 "sa_w_loaded", "mask_ready", "sa_q_psum", "sa_qkT", "sa_v_psum", "sa_v_done", "sa_km_done", "sa_s_psum", "sa_s_masked", "sa_centred",
                 "sa_p_done", "sa_pT_psum", "sa_pT_done", "sa_o_psum", "sa_o_done", "sa_oT_psum", "sa_oT_done",
                 "ffw_loaded", "ffb_loaded", "wabs_done", "wabs_psum", "wq_quant", "wqT_psum", "wqT_done",
                 "ff_ss_done", "ff_r_done", "ff_q_done", "ff_qT_psum", "ff_qT_done", "ff_h_psum", "ff_h_done", "ff_silu", "ff_gelu",
                 "ff_lnvar", "ff_lnrstd",
                 "xb_w_loaded", "xb_wkv_loaded", "xb_centred", "xb_cT_psum", "xb_cT_done", "xb_kv_psum", "xb_kv_done", "xb_k_sq", "xb_k_ss",
                 "xb_k_sqrt", "xb_kr_done", "xb_kt_done", "xb_khi", "xb_klo", "xb_kT_psum", "xb_kT_done", "xb_q_psum", "xb_q_ss", "xb_q_sqrt",
                 "xb_q_done", "xb_qn_done", "xb_q1_psum", "xb_q1_done", "xb_row_done", "xb_q2_psum", "xb_q2_done", "xb_m_psum", "xb_m_done",
                 "xb_s_psum", "xb_p_done", "xb_pv_done", "xb_o_psum", "xb_const", "xb_kd_ss", "xb_kd_read", "xb_kd_rstd", "xb_oh_done", "xb_ohT_psum", "xb_kdm_done", "xb_sd_centred", "xb_pd_done", "xb_od_done", "xb_o_done", "xb_oT_psum", "xb_oT_done",
                 "sb_w_loaded", "sb_masks", "sb_var", "sb_rstd_done", "mo_w_loaded", "mo_down_loaded", "mo_r_loaded", "mo_centred",
                 "mo_gu_psum", "mo_silu", "mo_a_done", "mo_y_psum", "mo_y_done"]
        M = {n: sem(n) for n in names}

        block = ctx.enter_context(nc.Block())
        LNS = upto

        @block.sync
        def _(sp):
            sp.dma_start(x_sb[:, :, :], a["x"].rearrange("b s d -> s b d")).then_inc(M["x_loaded"], 16)
            def load_context(b):
                sp.dma_start(ctx_nat[:, b * NC:(b + 1) * NC, 0:C],
                             a["ctx_1024"][b].rearrange("(p c) d -> p c d", c=NC)).then_inc(M["ctx_loaded"] if b == 0 else M["ctx1_loaded"], 16)

            sp.dma_start(wk[:, :], a["L0_xattn_Wk"]).then_inc(M["wk_loaded"], 16)
            load_context(0)
            sp.dma_start(wq[:, :, :], a["L0_xattn_Wq"].rearrange("(k p) n -> p k n", p=P)).then_inc(M["wq_loaded"], 16)
            load_context(1)
            sp.dma_start(gains[:, 0:1], a["L0_xattn_gq"].rearrange("(p o) -> p o", o=1)).then_inc(M["gains_loaded"], 16)
            sp.dma_start(gains[:, 1:2], a["L0_xattn_gk"].rearrange("(p o) -> p o", o=1)).then_inc(M["gains_loaded"], 16)
            sp.dma_start(wv[:, :, :], a["L0_xattn_Wv"].rearrange("p (h d) -> p h d", h=H)).then_inc(M["wv_loaded"], 16)
            sp.dma_start(wo[:, :, :], a["L0_xattn_Wo"].rearrange("(h p) n -> p h n", p=P)).then_inc(M["wo_loaded"], 16)
            sp.wait_ge(M["q_psum"], B * NG)
            sp.dma_start(w1[:, :, :], a["L0_ffn_w1"].rearrange("(o p) d -> p o d", p=P)).then_inc(M["ffw_loaded"], 16)
            sp.dma_start(w2[:, :, :], a["L0_ffn_w2"].rearrange("(o p) d -> p o d", p=P)).then_inc(M["ffw_loaded"], 16)
            sp.wait_ge(M["o_psum"], NG)
            sp.dma_start(w_in[:, :, :], a["L0_attn_w_in"].rearrange("(k p) n -> p k n", p=P)).then_inc(M["sa_w_loaded"], 16)
            sp.dma_start(w_out[:, :, :], a["L0_attn_w_out"].rearrange("(k p) n -> p k n", p=P)).then_inc(M["sa_w_loaded"], 16)
            for j in range(2 * KC):
                sp.dma_start(bqk[:, j:j + 1], a["L0_attn_b_in"][j * P:(j + 1) * P].rearrange("(p o) -> p o", o=1)).then_inc(M["sa_w_loaded"], 16)
            sp.dma_start(b_in_row[:, :], a["L0_attn_b_in"].rearrange("(o n) -> o n", o=1)).then_inc(M["sa_w_loaded"], 16)
            sp.dma_start(b_out_row[:, :], a["L0_attn_b_out"].rearrange("(o n) -> o n", o=1)).then_inc(M["sa_w_loaded"], 16)
            sp.wait_ge(M["o_psum"], B * NG)
            for t, name in ((b1_all, "L0_ffn_b1"), (lng_all, "L0_ffn_ln_g"), (lnb_all, "L0_ffn_ln_b"), (b2_all, "L0_ffn_b2")):
                sp.dma_start(t[:, :], a[name].rearrange("(o n) -> o n", o=1).to_broadcast([P, a[name].shape[0]])).then_inc(M["ffb_loaded"], 16)
            if upto >= 4:
                wkv = M["xb_wkv_loaded"]
                sp.dma_start(xb_wkv[:, 0:D], a["L1_xattn_Wk"]).then_inc(wkv, 16)
                sp.dma_start(xb_wkv[:, D:2 * D], a["L1_xattn_Wv"]).then_inc(wkv, 16)
                everywhere = ((xb_bkv[:, 0:D], "L1_xattn_bk"), (xb_bkv[:, D:2 * D], "L1_xattn_bv"))
                for dst, name in everywhere:
                    sp.dma_start(dst, a[name].rearrange("(o n) -> o n", o=1).to_broadcast([P, D])).then_inc(wkv, 16)
                xw = M["xb_w_loaded"]
                sp.wait_ge(M["y_psum"], B)
                sp.dma_start(xb_wq[:, :, :], a["L1_xattn_Wq"].rearrange("(k p) n -> p k n", p=P)).then_inc(xw, 16)
                sp.dma_start(xb_wo[:, :, :], a["L1_xattn_Wo"].rearrange("(k p) n -> p k n", p=P)).then_inc(xw, 16)
                sp.dma_start(xb_wd[:, :], a["L1_xattn_Wkv_dca"]).then_inc(xw, 16)
                sp.dma_start(xb_bd[:, :], a["L1_xattn_bkv_dca"].rearrange("(o n) -> o n", o=1).to_broadcast([P, 2 * D])).then_inc(xw, 16)
                sp.dma_start(xb_bq[:, :], a["L1_xattn_bq"].rearrange("(o n) -> o n", o=1).to_broadcast([P, D])).then_inc(xw, 16)
                sp.dma_start(xb_wo_row[:, :], a["L1_xattn_bo"].rearrange("(o n) -> o n", o=1)).then_inc(xw, 16)
                sp.dma_start(xb_yd[:, :, :], a["ctx_1024"][:, KV - DCA:KV, :].rearrange("b k c -> k b c")).then_inc(xw, 16)
                for j, name in enumerate(("qn_w", "qn_b", "kn_w", "kn_b", "kn_dca_w", "kn_dca_b")):
                    sp.dma_start(xb_vec[:, j, :], a["L1_xattn_" + name].rearrange("(o n) -> o n", o=1).to_broadcast([P, HD])).then_inc(xw, 16)
            if upto >= 6:
                sp.wait_ge(M["x_updated"], 3 * B)
                sp.wait_ge(M["xb_q_done"], 1)
                for t, name in ((mo_gate, "L1_ffn_gate_proj"), (mo_up, "L1_ffn_up_proj")):
                    for e in range(0, E, 4):
                        for kc in range(KC):
                            sp.dma_start(t[:, e:e + 4, kc, :], a[name][e:e + 4, kc * P:(kc + 1) * P, :].rearrange("e p i -> p e i")).then_inc(M["mo_w_loaded"], 16)
            if upto >= 5:
                sp.wait_ge(M["xb_o_psum"], B)
                lw = M["sb_w_loaded"]
                sp.dma_start(sb_w[:, :, :], a["L1_attn_qkv"].rearrange("(k p) n -> p k n", p=P)).then_inc(lw, 16)
                sp.dma_start(sb_wo[:, :, :], a["L1_attn_o_proj"].rearrange("(k p) n -> p k n", p=P)).then_inc(lw, 16)
                sp.dma_start(sb_g[:, 0, :], a["L1_attn_gamma"].rearrange("(o n) -> o n", o=1).to_broadcast([P, D])).then_inc(lw, 16)
                sp.dma_start(sb_g[:, 1, :], a["L1_attn_beta"].rearrange("(o n) -> o n", o=1).to_broadcast([P, D])).then_inc(lw, 16)
            if upto >= 6:
                sp.dma_start(mo_r[:, :], a["L1_ffn_router_w"]).then_inc(M["mo_r_loaded"], 16)
                sp.dma_start(mo_bias[:, :], a["L1_ffn_expert_bias"].rearrange("(o n) -> o n", o=1).to_broadcast([P, E])).then_inc(M["mo_r_loaded"], 16)
                sp.wait_ge(M["y_psum"], 4 * B)
                for e in range(0, E, 4):
                    for ic in range(IC):
                        sp.dma_start(mo_down[:, e:e + 4, ic, :], a["L1_ffn_down_proj"][e:e + 4, ic * IP:(ic + 1) * IP, :].rearrange("e p n -> p e n")).then_inc(M["mo_down_loaded"], 16)
            sp.wait_ge(M["x_updated"], B * upto)
            sp.dma_start(out.rearrange("b s d -> s b d"), x_sb[:, :, :]).then_inc(M["out_done"], 16)
            sp.wait_ge(M["out_done"], 16)

        @block.gpsimd
        def _(pool):
            links = [0]

            def chained(ins):
                links[0] += 1
                ins.then_inc(M["pool_chain"], 1)
                pool.wait_ge(M["pool_chain"], links[0])

            pool.memset(neg_half[:, :], -0.5).then_inc(M["const_made"], 1)
            pool.memset(ones[:, :], 1.0).then_inc(M["const_made"], 1)
            pool.memset(ctx_nat[:, :, C:C + 2], 1.0).then_inc(M["const_made"], 1)
            pool.memset(eps2[:, :], EPS2).then_inc(M["const_made"], 1)
            chained(pool.memset(ident[:, :], 0.0))
            pool.affine_select(out=ident[:, :], in_=ident[:, :], compare_op=ALU.not_equal, fill=1.0,
                               base=0, pattern=[[-1, P]], channel_multiplier=1).then_inc(M["ident_ready"], 1)
            pool.wait_ge(M["const_made"], 3)

            def ln_rstd(k):
                pool.wait_ge(M["ln_var"], B * (k + 1))
                chained(pool.tensor_scalar(veps[:, :], meanvar[:, :, 1], EPS, None, ALU.add))
                pool.tensor_tensor(rstd[:, :], veps[:, :], neg_half[:, 0:B], ALU.pow).then_inc(M["ln_rstd"], 1)

            ln_rstd(0)
            for b in range(B):
                for g in range(NG):
                    pool.wait_ge(M["q_ss_done"], NG * b + g + 1)
                    r = slice(G * g, G * g + G)
                    chained(pool.tensor_scalar(q_ss[:, b, r], q_ss[:, b, r], 1.0 / HD0, EPS, ALU.mult, ALU.add))
                    pool.tensor_tensor(q_rstd[:, b, r], q_ss[:, b, r], neg_half[:, 0:G], ALU.pow).then_inc(M["q_rstd_done"], 1)
            for b in range(B):
                pool.wait_ge(M["k_ss_done"], NG * NC * (b + 1))
                r = slice(b * NC, (b + 1) * NC)
                chained(pool.tensor_scalar(k_ss[:, r, :], k_ss[:, r, :], 1.0 / HD0, EPS, ALU.mult, ALU.add))
                pool.tensor_tensor(k_rstd[:, r, :], k_ss[:, r, :],
                                   neg_half[:, 0:1].unsqueeze(1).to_broadcast([P, NC, H]), ALU.pow).then_inc(M["k_rstd_done"], 1)


            pool.wait_ge(M["o_psum"], B * NG)
            chained(pool.memset(causal[:, :], 0.0))
            chained(pool.affine_select(out=causal[:, :], in_=causal[:, :], compare_op=ALU.is_ge, fill=-1e30,
                                       base=0, pattern=[[-1, S]], channel_multiplier=1))
            chained(pool.memset(head_mask[:, :], 1.0))
            chained(pool.affine_select(out=head_mask[:, :], in_=head_mask[:, :], compare_op=ALU.is_ge, fill=0.0,
                                       base=0, pattern=[[-HD, 8]], channel_multiplier=1))
            pool.affine_select(out=head_mask[:, :], in_=head_mask[:, :], compare_op=ALU.is_ge, fill=0.0,
                               base=HD - 1, pattern=[[HD, 8]], channel_multiplier=-1).then_inc(M["mask_ready"], 1)
            if upto < 2:
                return
            ln_rstd(1)
            if upto >= 4:
                pool.wait_ge(M["wqT_psum"], 8)
                pool.memset(xb_kv[:, :, :, 2 * HD:2 * HD + 1], 1.0).then_inc(M["xb_const"], 1)
            if upto < 3:
                return
            ln_rstd(2)

            def rms(i, n):
                pool.wait_ge(M["ff_ss_done"], B * (i + 1))
                chained(pool.tensor_scalar(ff_ss[:, i, :], ff_ss[:, i, :], 1.0 / n, EPS, ALU.mult, ALU.add))
                pool.tensor_tensor(ff_r[:, i, :], ff_ss[:, i, :], neg_half[:, 0:B], ALU.pow).then_inc(M["ff_r_done"], 1)

            rms(0, D)
            pool.wait_ge(M["ff_lnvar"], B)
            chained(pool.tensor_scalar(ff_rstd[:, :], ff_mv[:, :, 1], EPS, None, ALU.add))
            pool.tensor_tensor(ff_rstd[:, :], ff_rstd[:, :], neg_half[:, 0:B], ALU.pow).then_inc(M["ff_lnrstd"], 1)
            rms(1, FI)
            if upto < 4:
                return
            pool.wait_ge(M["y_psum"], 3 * B)
            for kn in xb_kn:
                pool.memset(kn[:, :, :, 3 * HD:3 * HD + 2].bitcast(F32), 1.0).then_inc(M["xb_const"], 1)
                pool.memset(kn[:, :, :, 3 * HD + 2:W].bitcast(F32), 0.0).then_inc(M["xb_const"], 1)
            pool.memset(xb_qn[:, :, 3 * HD + 2:W].bitcast(F32), 0.0).then_inc(M["xb_const"], 1)
            pool.memset(xb_qT2[:, :, :].bitcast(F32), 0.0).then_inc(M["xb_const"], 1)
            ln_rstd(3)
            pool.wait_ge(M["xb_kd_ss"], 1)
            chained(pool.tensor_scalar(xb_d32[:, 1, :], xb_d32[:, 1, :], 1.0 / HD, EPS2, ALU.mult, ALU.add))
            pool.tensor_tensor(xb_d32[:, 3, :], xb_d32[:, 1, :], neg_half[:, 0:B * H], ALU.pow).then_inc(M["xb_kd_rstd"], 1)
            pool.wait_ge(M["xb_kv_psum"], B * NC)
            pool.memset(xb_kn[0][:, :, :, 3 * HD:3 * HD + 2].bitcast(F32), 1.0).then_inc(M["xb_const"], 1)
            pool.memset(xb_kn[0][:, :, :, 3 * HD + 2:W].bitcast(F32), 0.0).then_inc(M["xb_const"], 1)
            if upto < 5:
                return
            pool.wait_ge(M["xb_o_psum"], B)
            chained(pool.memset(causal2[:, :], 0.0))
            pool.affine_select(out=causal2[:, :], in_=causal2[:, :], compare_op=ALU.is_ge, fill=-1e30,
                               base=0, pattern=[[-1, S]], channel_multiplier=1).then_inc(M["sb_masks"], 1)
            chained(pool.memset(mo_first[:, :, :], 1.0))
            pool.affine_select(out=mo_first[:, :, :], in_=mo_first[:, :, :], compare_op=ALU.is_gt, fill=0.0,
                               base=0, pattern=[[1, E], [-1, E]], channel_multiplier=0).then_inc(M["sb_masks"], 1)
            ln_rstd(4)
            pool.wait_ge(M["sb_var"], B)
            chained(pool.tensor_scalar(sb_rstd[:, :], sb_mv[:, :, 1], EPS, None, ALU.add))
            pool.tensor_tensor(sb_rstd[:, :], sb_rstd[:, :], neg_half[:, 0:B], ALU.pow).then_inc(M["sb_rstd_done"], 1)
            if upto < 6:
                return
            ln_rstd(5)
        @block.scalar
        def _(act):
            def xnT_copy(k):
                act.wait_ge(M["xT_psum"], k + 1)
                act.activation(xnT[:, :, :], ps[:, 0, :], ACT.Copy).then_inc(M["xnT_ready"], 1)

            xnT_copy(0)
            def context_high(j):
                act.wait_ge(M["ctxT_psum"], j + 1)
                act.activation(ctxT_hi[:, 4 * j:4 * j + 4, :], ps[:, 4 + j % 4, :], ACT.Copy).then_inc(M["ctxT_hi_done"], 1)

            def query_part(c):
                if c < 8:
                    act.wait_ge(M["q_psum"], c + 1)
                    if c >= 2:
                        act.wait_ge(M["q_ss_done"], c - 1)
                    act.activation(q_sq[:, c % 2, :], ps[:, 4 + c % 4, :], ACT.Square).then_inc(M["q_squared"], 1)
                elif c < 12:
                    context_high(c - 4)
                elif c < 14:
                    for j in (2 * (c - 12), 2 * (c - 12) + 1):
                        act.wait_ge(M["wkT_psum"], j + 1)
                        act.activation(wkT[:, 4 * j:4 * j + 4, :], ps[:, 4 + j, :], ACT.Copy).then_inc(M["wkT_done"], 1)
                elif c < 18:
                    if c == 14:
                        act.wait_ge(M["gqk_done"], 1)
                    for j in (2 * (c - 14), 2 * (c - 14) + 1):
                        act.wait_ge(M["qT_psum"], j + 1)
                        act.activation(qT[:, 2 * j:2 * j + 2, :], ps[:, 4 + j % 2, :], ACT.Copy, scale=gqk[:, 0:1]).then_inc(M["qT_done"], 1)
                elif c < 26:
                    j = c - 18
                    act.wait_ge(M["q3_psum"], j + 1)
                    if j == 0:
                        act.wait_ge(M["q_ss_done"], B * NG)
                    act.activation(q3_hi[:, :, 2 * j:2 * j + 2, :].rearrange("p b h s -> p h b s"),
                                   ps[:, 6 + j % 2, :].rearrange("p (h b s) -> p h b s", h=2, b=B),
                                   ACT.Copy).then_inc(M["q3_hi_done"], 1)
                elif c < 28:
                    if c == 26:
                        act.wait_ge(M["ffw_loaded"], 32)
                        act.wait_ge(M["qT_psum"], H // 2)
                    act.activation(w_sizes[:, :], (w1, w2)[c - 26][:, :, :].rearrange("p k n -> p (k n)"), ACT.Abs,
                                   accum_out=w_abs[:, c - 26:c - 25]).then_inc(M["wabs_done"], 1)

            for j in range(4):
                context_high(j)
            for c in range(B * NC):
                for g in range(NG):
                    i = c * NG + g
                    act.wait_ge(M["k_psum"], i + 1)
                    if i >= 2:
                        act.wait_ge(M["k_ss_done"], i - 1)
                    act.activation(sq[:, i % 2, :], ps[:, i % 4, :], ACT.Square).then_inc(M["k_squared"], 1)
                query_part(c)
            for i in range(B * NG * NC // 2):
                act.wait_ge(M["s_scaled"], i + 1)
                if i >= 2:
                    act.wait_ge(M["pv_chunk"], i - 1)
                act.activation(p_sb[:, i % 2, :, :], s_sb[:, i % 2, :, :], ACT.Exp, bias=shift[:, 0:1]).then_inc(M["p_done"], 1)
            for j in range(H // 2):
                act.wait_ge(M["oT_psum"], j + 1)
                act.activation(oT[:, 2 * j:2 * j + 2, :], ps[:, j % 2, :], ACT.Copy).then_inc(M["oT_done"], 1)
            for j in range(H // 2):
                act.wait_ge(M["aT_psum"], j + 1)
                act.activation(aT[:, 2 * j:2 * j + 2, :], ps[:, 2 + j % 2, :], ACT.Copy).then_inc(M["aT_done"], 1)
            if upto < 2:
                return
            xnT_copy(1)
            act.wait_ge(M["sa_w_loaded"], 128)
            act.wait_ge(M["sa_q_psum"], 1)
            for j in range(KC):
                act.activation(sa_qT[:, j, :], ps[:, 1, j * B * S:(j + 1) * B * S], ACT.Identity, bias=bqk[:, j:j + 1]).then_inc(M["sa_qkT"], 1)
            for j in range(KC):
                act.activation(sa_kT[:, j, :], ps[:, 2, j * B * S:(j + 1) * B * S], ACT.Identity, bias=bqk[:, KC + j:KC + j + 1]).then_inc(M["sa_qkT"], 1)
            act.wait_ge(M["sa_v_psum"], 1)
            act.activation(sa_v[:, :, :, 0:HD], ps[:, 3, :].rearrange("p (b h d) -> p b h d", b=B, h=H), ACT.Copy).then_inc(M["sa_v_done"], 1)
            def weight_copies(first):
                for i in range(first, first + 4):
                    act.wait_ge(M["wqT_psum"], i + 1)
                    if i < 4:
                        dst = w1qT[:, i // 2, (i % 2) * 512:(i % 2) * 512 + 512]
                    else:
                        dst = w2qT[:, 2 * (i - 4):2 * (i - 4) + 2, :]
                    act.activation(dst, ps[:, (4 + i) % 8, :], ACT.Copy).then_inc(M["wqT_done"], 1)

            def context_copy(b, g):
                act.wait_ge(M["xb_cT_psum"], 4 * b + g + 1)
                bank = 1 + g if b == 1 else 7 - 4 * (g % 2)
                act.activation(xb_cT[b][:, 4 * g:4 * g + 4, :], ps[:, bank, :], ACT.Copy).then_inc(M["xb_cT_done"], 1)

            def key_copies(first, last):
                for c in range(first, last):
                    if c == 0:
                        act.wait_ge(M["y_psum"], B)
                    act.wait_ge(M["xb_kv_psum"], c + 1)
                    act.activation(xb_kv[:, c, :, 0:2 * HD], ps[:, KEY_BANKS[c], :].rearrange("p (h d) -> p h d", h=H), ACT.Copy).then_inc(M["xb_kv_done"], 1)

            def k_squares(b, first, last):
                for t in range(first, last):
                    n = b * (NC // 2) + t
                    act.wait_ge(M["xb_kv_done"], b * NC + 2 * t + 2)
                    if n >= 2:
                        act.wait_ge(M["xb_k_ss"], n - 1)
                    act.activation(sq[:, n % 2, :].rearrange("p (c h d) -> p c h d", c=2, h=H), xb_kv[:, 2 * t:2 * t + 2, :, 0:HD],
                                   ACT.Square).then_inc(M["xb_k_sq"], 1)
                if last == NC // 2:
                    act.wait_ge(M["xb_k_ss"], (b + 1) * (NC // 2))
                    act.activation(xb_rk[:, :, :], xb_ss[:, :, :], ACT.Sqrt, scale=1.0 / HD, bias=eps2[:, 0:1]).then_inc(M["xb_k_sqrt"], 1)

            for b in range(B):
                weight_copies(4 * b)
                act.wait_ge(M["sa_centred"], b + 1)
                act.activation(sa_s[:, b, :, :], sa_s[:, b, :, :], ACT.Exp, scale=float(HD) ** -0.5).then_inc(M["sa_p_done"], 1)
            for b in range(B):
                for g in range(4):
                    act.wait_ge(M["sa_pT_psum"], b * 4 + g + 1)
                    act.activation(sa_pT[:, b, 4 * g:4 * g + 4, :], ps[:, 4 * (1 - b) + g, :], ACT.Copy).then_inc(M["sa_pT_done"], 1)
            if upto >= 4:
                for g in range(4):
                    context_copy(0, g)
                key_copies(0, 2)
            for b in range(B):
                act.wait_ge(M["sa_oT_psum"], b + 1)
                act.activation(sa_oT[:, :, b * S:(b + 1) * S], ps[:, 4 * (1 - b) + 1, 0:D].rearrange("p (k s) -> p k s", k=KC),
                               ACT.Copy).then_inc(M["sa_oT_done"], 1)
            if upto >= 4:
                key_copies(2, 8)
                k_squares(0, 0, 2)
            if upto < 3:
                return
            xnT_like = ps[:, 0, :]
            act.wait_ge(M["ff_qT_psum"], 1)
            act.activation(ff_qT1[:, :, :], xnT_like, ACT.Copy).then_inc(M["ff_qT_done"], 1)
            for b in range(B):
                act.wait_ge(M["ff_h_done"], b + 1)
                act.activation(ff_h2[:, b, :], ff_h[:, b, :], ACT.Silu).then_inc(M["ff_silu"], 1)
            for b in range(B):
                act.wait_ge(M["ff_silu"], b + 1)
                act.activation(ff_h[:, b, :], ff_h2[:, b, :], ACT.Gelu).then_inc(M["ff_gelu"], 1)
            if upto >= 4:
                key_copies(8, NC)
                k_squares(0, 2, 4)
            for b in range(B):
                for g in range(2):
                    act.wait_ge(M["ff_qT_psum"], 2 + 2 * b + g)
                    act.activation(ff_qT2[:, 4 * g:4 * g + 4, b * S:(b + 1) * S], ps[:, 4 + 2 * b + g, :], ACT.Copy).then_inc(M["ff_qT_done"], 1)
            if upto < 4:
                return

            def k_high(n):
                act.wait_ge(M["xb_kt_done"], n + 1)
                if n < 2:
                    act.wait_ge(M["y_psum"], 3 * B)
                if n >= 2:
                    act.wait_ge(M["xb_kT_psum"], 4 * (n - 1))
                src = xb_kt[:, :, :, :].rearrange("p c h d -> p (c h) d").unsqueeze(2).to_broadcast([P, 2 * NC, 2, HD])
                dst = xb_kn[n % 2][:, :, :, 0:4 * HD].rearrange("p c h (r t d) -> p (c h) r t d", r=2, t=2)[:, :, :, 0, :]
                act.activation(dst, src, ACT.Copy).then_inc(M["xb_khi"], 1)

            k_squares(0, 4, NC // 2)
            k_high(0)
            xnT_copy(2)
            act.wait_ge(M["xb_q_ss"], 1)
            act.activation(xb_s32[:, 2, :], xb_s32[:, 1, :], ACT.Sqrt, scale=1.0 / HD, bias=eps2[:, 0:1]).then_inc(M["xb_q_sqrt"], 1)

            def last_rows(stage):
                if stage == 0:
                    act.wait_ge(M["xb_last_psum"], 1)
                    act.activation(xb_ydT[:, :, :, :], ps[:, 3, 0:B * DCA].rearrange("p (b k) -> p b k", b=B).unsqueeze(2).to_broadcast([P, B, 8, DCA]),
                                   ACT.Copy).then_inc(M["xb_last_act"], 1)
                elif stage == 6:
                    act.wait_ge(M["xb_last_psum"], 4)
                    act.activation(xb_kdT[:, :, :, :], ps[:, 3, :], ACT.Copy).then_inc(M["xb_last_act"], 1)
                elif stage == 7:
                    act.wait_ge(M["xb_last_psum"], 5)
                    act.activation(xb_qfT[:, :, :], ps[:, 3, :], ACT.Copy).then_inc(M["xb_last_act"], 1)
                elif stage == 9:
                    act.wait_ge(M["xb_sd_centred"], 1)
                    act.activation(xb_pd[:, :, :], xb_pd[:, :, :], ACT.Exp, scale=SC).then_inc(M["xb_last_act"], 1)
                elif stage == 11:
                    act.wait_ge(M["xb_last_psum"], 7)
                    act.activation(xb_pdT[:, :, :], ps[:, 3, :], ACT.Copy).then_inc(M["xb_last_act"], 1)

            def k_copy(n, g):
                act.wait_ge(M["xb_kT_psum"], 4 * n + g + 1)
                act.activation(xb_kT[:, n % 2, 4 * g:4 * g + 4, :], ps[:, 4 * (g % 2), :], ACT.Copy).then_inc(M["xb_kT_done"], 1)

            def q_copy(n):
                act.wait_ge(M["xb_q2_psum"], n + 1)
                if n == 0:
                    act.wait_ge(M["xb_const"], 7)
                act.activation(xb_qT2[0:W, n % 2, 0:S], ps[0:W, 0, 0:S], ACT.Copy)
                act.activation(xb_qT2[W:2 * W, n % 2, S:2 * S], ps[W:2 * W, 0, 0:S], ACT.Copy).then_inc(M["xb_q2_done"], 1)

            def probabilities(n, u):
                m = n * NU + u
                act.wait_ge(M["xb_s_psum"], m + 1)
                if m >= 2:
                    act.wait_ge(M["xb_pv_done"], m - 1)
                act.activation(xb_p[:, m % 2, :, :], ps[:, 5 + m % 2, :].rearrange("p (c s) -> p c s", c=4),
                               ACT.Exp).then_inc(M["xb_p_done"], 1)

            for b in range(B):
                if b == 1:
                    for g in range(4):
                        context_copy(1, g)
                    k_squares(1, 0, NC // 2)
                for g in range(2):
                    act.wait_ge(M["xb_q1_psum"], 2 * b + g + 1)
                    act.activation(xb_qT1[:, 4 * g:4 * g + 4, :], ps[:, 1 + g, :], ACT.Copy).then_inc(M["xb_q1_done"], 1)
                if b == 1:
                    k_high(b * PAIRS)
                first = b * PAIRS
                for slot in range(-6, UNITS + 9):
                    if 0 <= slot - 8 < UNITS:
                        probabilities(first + (slot - 8) // 8, slot % 8)
                    if 0 <= slot + 6 < UNITS and slot % 2 == 0:
                        k_copy(first + (slot + 6) // 8, (slot + 6) % 8 // 2)
                    if (slot + 13) % 8 == 0 and slot + 13 < UNITS:
                        k_high(first + (slot + 13) // 8)
                    if slot % 8 == 7 and 0 <= slot < UNITS:
                        q_copy(first + slot // 8)
                    if b == 0 and (slot + 5) % 3 == 0:
                        last_rows((slot + 5) // 3)
            for b in range(B):
                act.wait_ge(M["xb_oT_psum"], b + 1)
                act.activation(xb_qfT[:, :, b * S:(b + 1) * S],
                               ps[:, 1 + b, 0:D].rearrange("p (k s) -> p k s", k=KC), ACT.Copy).then_inc(M["xb_oT_done"], 1)
            if upto < 5:
                return

            act.wait_ge(M["sb_psum"], 1)
            act.activation(sb_hT[:, :, :], ps[:, 0, :], ACT.Copy).then_inc(M["sb_act"], 1)
            act.wait_ge(M["sb_psum"], 2)
            act.activation(sb_qT[:, :, :], ps[:, 1, :], ACT.Copy).then_inc(M["sb_act"], 1)
            act.activation(sb_kT[:, :, :], ps[:, 2, :], ACT.Copy).then_inc(M["sb_act"], 1)
            act.wait_ge(M["sb_psum"], 3)
            act.activation(sb_v[:, :, :], ps[:, 3, :], ACT.Copy).then_inc(M["sb_act"], 1)
            act.wait_ge(M["sb_dve"], 2)
            act.activation(sb_s[:, :, :], sb_s[:, :, :], ACT.Exp, scale=float(D) ** -0.5).then_inc(M["sb_act"], 1)
            act.wait_ge(M["sb_psum"], 5)
            act.activation(sb_pT[:, :, :], ps[:, 5, 0:B * S], ACT.Copy).then_inc(M["sb_act"], 1)
            act.wait_ge(M["sb_psum"], 6)
            act.activation(sb_oT[:, :, :], ps[:, 6, :], ACT.Copy).then_inc(M["sb_act"], 1)
            if upto < 6:
                return

            xnT_copy(3)
            act.wait_ge(M["mo_psum"], 1)
            act.activation(mo_rT[:, :, :], ps[:, 1, 0:KC * E], ACT.Copy).then_inc(M["mo_act"], 1)
            act.wait_ge(M["mo_centred"], 1)
            act.activation(mo_s[:, :, :], mo_s[:, :, :], ACT.Exp).then_inc(M["mo_act"], 1)
            for e in range(E):
                act.wait_ge(M["mo_gu_psum"], e + 1)
                if e >= 2:
                    act.wait_ge(M["mo_a_done"], e - 1)
                act.activation(mo_sg[:, e % 2, :, :], ps[0:IP, 3 + 2 * (e % 2), :], ACT.Silu).then_inc(M["mo_silu"], 1)

        @block.vector
        def _(dve):
            links = [0]

            def chained(ins):
                links[0] += 1
                ins.then_inc(M["dve_chain"], 1)
                dve.wait_ge(M["dve_chain"], links[0])

            def layernorm(k):
                for b in range(B):
                    if k > 0:
                        dve.wait_ge(M["x_updated"], B * (k - 1) + b + 1)
                    chained(dve.bn_stats(stats[:, b, :], x_sb[:, b, :]))
                    dve.bn_aggr(meanvar[:, b, :], stats[:, b, :]).then_inc(M["ln_var"], 1)
                dve.wait_ge(M["ln_var"], B * (k + 1))
                dve.wait_ge(M["ln_rstd"], k + 1)
                for b in range(B):
                    dve.tensor_scalar(xn[:, b, :], x_sb[:, b, :], meanvar[:, b, 0:1], rstd[:, b:b + 1],
                                      ALU.subtract, ALU.mult).then_inc(M["xn_ready"], 1)

            dve.wait_ge(M["x_loaded"], 16)
            layernorm(0)

            def context_low(j):
                dve.wait_ge(M["ctxT_hi_done"], j + 1)
                dve.tensor_tensor(ctxT_lo[:, 4 * j:4 * j + 4, :], ps[:, 4 + j % 4, :].rearrange("p (c k) -> p c k", c=4),
                                  ctxT_hi[:, 4 * j:4 * j + 4, :].bitcast(F32), ALU.subtract).then_inc(M["ctxT_lo_done"], 1)

            def query_part(c):
                if 1 <= c < 9:
                    b, g = (c - 1) // NG, (c - 1) % NG
                    dve.wait_ge(M["q_rstd_done"], c)
                    dve.tensor_tensor(qn[:, b, G * g:G * g + G, :], ps[:, 4 + (c - 1) % 4, :].rearrange("p (h d) -> p h d", h=G),
                                      q_rstd[:, b, G * g:G * g + G].unsqueeze(2).to_broadcast([P, G, HD0]),
                                      ALU.mult).then_inc(M["qn_done"], 1)
                if c < 8:
                    b, g = c // NG, c % NG
                    dve.wait_ge(M["q_squared"], c + 1)
                    dve.tensor_reduce(q_ss[:, b, G * g:G * g + G], q_sq[:, c % 2, :].rearrange("p (h d) -> p h d", h=G),
                                      AX.X, ALU.add).then_inc(M["q_ss_done"], 1)
                elif c < 12:
                    context_low(c - 4)
                elif 18 <= c < 26:
                    j = c - 18
                    dve.wait_ge(M["q3_hi_done"], j + 1)
                    dve.tensor_tensor(q3_lo[:, :, 2 * j:2 * j + 2, :].rearrange("p b h s -> p h b s"),
                                      ps[:, 6 + j % 2, :].rearrange("p (h b s) -> p h b s", h=2, b=B),
                                      q3_hi[:, :, 2 * j:2 * j + 2, :].bitcast(F32).rearrange("p b h s -> p h b s"),
                                      ALU.subtract).then_inc(M["q3_lo_done"], 1)

            dve.wait_ge(M["wk_loaded"], 16)
            chained(dve.tensor_copy(wk_hi[:, :], wk[:, :]))
            dve.tensor_tensor(wk_lo[:, :], wk[:, :], wk_hi[:, :].bitcast(F32), ALU.subtract).then_inc(M["wk_split"], 1)
            for j in range(4):
                context_low(j)
            dve.wait_ge(M["gains_loaded"], 32)
            dve.tensor_scalar(gqk[:, :], gains[:, 0:1], gains[:, 1:2], float(HD0) ** -0.5, ALU.mult, ALU.mult).then_inc(M["gqk_done"], 1)
            chained(dve.memset(shift[:, :], 0.0))
            for c in range(B * NC):
                for g in range(NG):
                    i = c * NG + g
                    dve.wait_ge(M["k_squared"], i + 1)
                    dve.tensor_reduce(k_ss[:, c, G * g:G * g + G], sq[:, i % 2, :].rearrange("p (h d) -> p h d", h=G),
                                      AX.X, ALU.add).then_inc(M["k_ss_done"], 1)
                query_part(c)
            ROUND = 1.5 * 2.0 ** 23

            def ternary(step):
                i, w = step // 3, (w1, w2)[step // 3]
                if step == 0:
                    dve.wait_ge(M["wabs_psum"], 1)
                    chained(dve.tensor_scalar(w_mean[:, :], ps[:, 7, 0:2], 1.0 / (FI * D), 1e-5, ALU.mult, ALU.max))
                    dve.reciprocal(w_scale[:, :], w_mean[:, :]).then_inc(M["wq_quant"], 1)
                dve.wait_ge(M["wq_quant"], step + 1)
                ins = (lambda: dve.tensor_scalar(w[:, :, :], w[:, :, :], w_scale[:, i:i + 1], ROUND, ALU.mult, ALU.add),
                       lambda: dve.tensor_scalar(w[:, :, :], w[:, :, :], -ROUND, 1.0, ALU.add, ALU.min),
                       lambda: dve.tensor_scalar(w[:, :, :], w[:, :, :], -1.0, None, ALU.max))[step % 3]()
                ins.then_inc(M["wq_quant"], 1)

            for b in range(B):
                dve.wait_ge(M["k_rstd_done"], b + 1)
                for g in range(NG):
                    for c2 in range(NC // 2):
                        i = (b * NG + g) * (NC // 2) + c2
                        if i % 2 == 1 and i // 2 < 6:
                            ternary(i // 2)
                        c = b * NC + 2 * c2
                        dve.wait_ge(M["s_psum"], i + 1)
                        if i >= 2:
                            dve.wait_ge(M["p_done"], i - 1)
                        dve.tensor_tensor(s_sb[:, i % 2, :, :].rearrange("p c (h s) -> p c h s", h=G),
                                          ps[:, 2 * (i % 2):2 * (i % 2) + 2, :].rearrange("p c (h s) -> p c h s", h=G),
                                          k_rstd[:, c:c + 2, G * g:G * g + G].unsqueeze(3).to_broadcast([P, 2, G, S]),
                                          ALU.mult).then_inc(M["s_scaled"], 1)
                    j = b * NG + g
                    o = ps[:, 4 + 2 * (j % 2):6 + 2 * (j % 2), 0:2 * (C + 2)].rearrange("p k (h c) -> p k h c", h=2)
                    dve.wait_ge(M["o_psum"], j + 1)
                    chained(dve.reciprocal(o_den[:, j, :].rearrange("p (k h) -> p k h", k=2), o[:, :, :, C]))
                    dve.tensor_tensor(o_n[:, b, G * g:G * g + G, :].rearrange("p (k h) c -> p k h c", k=2), o[:, :, :, 0:C],
                                      o_den[:, j, :].rearrange("p (k h) -> p k h", k=2).unsqueeze(3).to_broadcast([P, 2, 2, C]),
                                      ALU.mult).then_inc(M["o_done"], 1)
            for b in range(B):
                dve.wait_ge(M["y_psum"], b + 1)
                dve.tensor_tensor(x_sb[:, b, :], x_sb[:, b, :], ps[:, 4 + b, 0:D], ALU.add).then_inc(M["x_updated"], 1)
            if upto < 2:
                return
            layernorm(1)
            dve.memset(sa_v[:, :, :, HD:HD + 2], 1.0).then_inc(M["sa_v_done"], 1)
            dve.wait_ge(M["mask_ready"], 1)
            dve.wait_ge(M["sa_qkT"], 2 * KC)
            for b in range(B):
                for j in range(KC):
                    i = b * KC + j
                    if i >= 2:
                        dve.wait_ge(M["sa_s_psum"], i - 1)
                    dve.tensor_tensor(sa_km[:, i % 2, :, :], sa_kT[:, j, b * S:(b + 1) * S].unsqueeze(1).to_broadcast([P, 8, S]),
                                      head_mask[:, :].unsqueeze(2).to_broadcast([P, 8, S]), ALU.mult).then_inc(M["sa_km_done"], 1)
            for b in range(B):
                for j in range(KC):
                    dve.wait_ge(M["sa_s_psum"], b * KC + j + 1)
                    bank = 4 * (1 - b) + 2 * j
                    dve.tensor_tensor(sa_s[:, b, 8 * j:8 * j + 8, :], ps[:, bank:bank + 2, :].rearrange("p k (h s) -> p (k h) s", s=S),
                                      causal[:, :].unsqueeze(1).to_broadcast([P, 8, S]), ALU.add).then_inc(M["sa_s_masked"], 1)
                dve.wait_ge(M["sa_s_masked"], KC * (b + 1))
                chained(dve.tensor_reduce(sa_max[:, b, :], sa_s[:, b, :, :], AX.X, ALU.max))
                dve.tensor_tensor(sa_s[:, b, :, :], sa_s[:, b, :, :], sa_max[:, b, :].unsqueeze(2).to_broadcast([P, H, S]),
                                  ALU.subtract).then_inc(M["sa_centred"], 1)
            def heads(ap):
                return ap.rearrange("p (h d) -> p h d", d=HD)

            def per_head(ap, n):
                return ap.unsqueeze(2).to_broadcast([P, n, HD])

            if upto >= 4:
                dve.wait_ge(M["xb_wkv_loaded"], 64)
                for j, w in enumerate((xb_wkv, xb_bkv)):
                    wv32 = w[:, :].rearrange("p (h d) -> p h d", d=2 * HD)
                    chained(dve.tensor_reduce(xb_s32[:, j, 0:H], wv32[:, :, 0:HD], AX.X, ALU.add))
                    chained(dve.tensor_scalar(xb_s32[:, j, 0:H], xb_s32[:, j, 0:H], 1.0 / HD, None, ALU.mult))
                    dve.tensor_tensor(wv32[:, :, 0:HD], wv32[:, :, 0:HD], per_head(xb_s32[:, j, 0:H], H), ALU.subtract).then_inc(M["xb_centred"], 1)
            for b in range(B):
                dve.wait_ge(M["sa_o_psum"], b + 1)
                o = ps[:, 4 * (1 - b), 0:H * (HD + 2)].rearrange("p (h d) -> p h d", h=H)
                chained(dve.reciprocal(sa_den[:, b, :], o[:, :, HD]))
                dve.tensor_tensor(sa_o[:, b, :].rearrange("p (h d) -> p h d", h=H), o[:, :, 0:HD],
                                  sa_den[:, b, :].unsqueeze(2).to_broadcast([P, H, HD]), ALU.mult).then_inc(M["sa_o_done"], 1)
            for b in range(B):
                dve.wait_ge(M["y_psum"], B + b + 1)
                dve.tensor_tensor(x_sb[:, b, :], x_sb[:, b, :], ps[:, 4 * (1 - b) + 2, 0:D], ALU.add).then_inc(M["x_updated"], 1)
            if upto < 3:
                return
            layernorm(2)
            dve.wait_ge(M["xn_ready"], 3 * B)

            def quantise(i, src, dst):
                for b in range(B):
                    chained(dve.tensor_reduce(ff_max[:, i, b:b + 1], src[:, b, :], AX.X, ALU.max, apply_absolute_value=True))
                dve.wait_ge(M["ff_r_done"], i + 1)
                chained(dve.tensor_tensor(ff_max[:, i, :], ff_max[:, i, :], ff_r[:, i, :], ALU.mult))
                chained(dve.tensor_scalar(ff_max[:, i, :], ff_max[:, i, :], 1e-5, 1.0 / 127.0, ALU.max, ALU.mult))
                chained(dve.reciprocal(ff_s[:, i, :], ff_max[:, i, :]))
                chained(dve.tensor_scalar(ff_dq[:, i, :], ff_max[:, i, :], w_mean[:, i:i + 1], None, ALU.mult))
                for b in range(B):
                    chained(dve.tensor_scalar(dst[:, b, :], src[:, b, :], ff_r[:, i, b:b + 1], ff_s[:, i, b:b + 1], ALU.mult, ALU.mult))
                    chained(dve.tensor_scalar(dst[:, b, :], dst[:, b, :], ROUND, -ROUND, ALU.add, ALU.add))
                    dve.tensor_scalar(dst[:, b, :], dst[:, b, :], 127.0, -128.0, ALU.min, ALU.max).then_inc(M["ff_q_done"], 1)

            for b in range(B):
                dve.scalar_tensor_tensor(out=ff_sq[:, b, 0:D], in0=xn[:, b, :], scalar=1.0, in1=xn[:, b, :], op0=ALU.mult, op1=ALU.mult,
                                         accum_out=ff_ss[:, 0, b:b + 1]).then_inc(M["ff_ss_done"], 1)
            quantise(0, xn, ff_q1)
            dve.wait_ge(M["ffb_loaded"], 64)
            def key_sums(b, t):
                n = b * (NC // 2) + t
                dve.wait_ge(M["xb_k_sq"], n + 1)
                dve.tensor_reduce(xb_ss[:, 2 * t:2 * t + 2, :], sq[:, n % 2, :].rearrange("p (c h d) -> p c h d", c=2, h=H),
                                  AX.X, ALU.add).then_inc(M["xb_k_ss"], 1)

            for b in range(B):
                dve.wait_ge(M["ff_h_psum"], b + 1)
                dve.scalar_tensor_tensor(out=ff_h[:, b, :], in0=ps[:, 4 + 2 * b:6 + 2 * b, :].rearrange("p k n -> p (k n)"), scalar=ff_dq[:, 0, b:b + 1],
                                         in1=b1_all[:, :], op0=ALU.mult, op1=ALU.add).then_inc(M["ff_h_done"], 1)
            if upto >= 4:
                key_sums(0, 0)
                key_sums(0, 1)
            for b in range(B):
                dve.wait_ge(M["ff_gelu"], b + 1)
                for t in range(2):
                    chained(dve.bn_stats(ff_stats[:, b, t, :], ff_h[:, b, t * 512:(t + 1) * 512]))
                dve.bn_aggr(ff_mv[:, b, :], ff_stats[:, b, :, :]).then_inc(M["ff_lnvar"], 1)
            dve.wait_ge(M["ff_lnvar"], B)
            dve.wait_ge(M["ff_lnrstd"], 1)
            for b in range(B):
                chained(dve.tensor_scalar(ff_h2[:, b, :], ff_h[:, b, :], ff_mv[:, b, 0:1], ff_rstd[:, b:b + 1], ALU.subtract, ALU.mult))
                chained(dve.tensor_tensor(ff_h2[:, b, :], ff_h2[:, b, :], lng_all[:, :], ALU.mult))
                chained(dve.tensor_tensor(ff_h2[:, b, :], ff_h2[:, b, :], lnb_all[:, :], ALU.add))
                dve.scalar_tensor_tensor(out=ff_sq[:, b, :], in0=ff_h2[:, b, :], scalar=1.0, in1=ff_h2[:, b, :], op0=ALU.mult, op1=ALU.mult,
                                         accum_out=ff_ss[:, 1, b:b + 1]).then_inc(M["ff_ss_done"], 1)
            quantise(1, ff_h2, ff_h)
            if upto >= 4:
                for t in range(2, NC // 2):
                    key_sums(0, t)
            for b in range(B):
                dve.wait_ge(M["y_psum"], 2 * B + b + 1)
                chained(dve.tensor_tensor(x_sb[:, b, :], x_sb[:, b, :], b2_all[:, :], ALU.add))
                dve.scalar_tensor_tensor(out=x_sb[:, b, :], in0=ps[:, 1 + b, 0:D], scalar=ff_dq[:, 1, b:b + 1], in1=x_sb[:, b, :],
                                         op0=ALU.mult, op1=ALU.add).then_inc(M["x_updated"], 1)
            if upto < 4:
                return

            def key_rows(b):
                for c in range(NC):
                    n = b * NC + c
                    dve.wait_ge(M["xb_kv_psum"], n + 1)
                    dve.tensor_tensor(xb_kv[:, c, :, 0:2 * HD], ps[:, 1 + c % 4, :].rearrange("p (h d) -> p h d", h=H),
                                      xb_bkv[:, :].rearrange("p (h d) -> p h d", h=H), ALU.add).then_inc(M["xb_kv_done"], 1)
                    if c % 2 == 1 and c >= 3:
                        key_sums(b, c // 2 - 1)
                key_sums(b, NC // 2 - 1)

            def key_rstd(b):
                dve.wait_ge(M["xb_k_sqrt"], b + 1)
                dve.reciprocal(xb_rk[:, :, :], xb_rk[:, :, :]).then_inc(M["xb_kr_done"], 1)

            def head_norm(dst, tmp, sums, n):
                chained(dve.tensor_reduce(sums[:, 0, 0:n], heads(dst), AX.X, ALU.add))
                chained(dve.tensor_scalar(sums[:, 0, 0:n], sums[:, 0, 0:n], 1.0 / HD, None, ALU.mult))
                chained(dve.tensor_tensor(heads(dst), heads(dst), per_head(sums[:, 0, 0:n], n), ALU.subtract))
                chained(dve.tensor_tensor(tmp, dst, dst, ALU.mult))

            def k_full(n):
                i = n % PAIRS
                if n >= 1:
                    dve.wait_ge(M["xb_klo"], n)
                    dve.wait_ge(M["xb_khi"], n)
                dve.tensor_tensor(xb_kt[:, :, :, :], xb_kv[:, :, 2 * i:2 * i + 2, 0:HD], xb_rk[:, :, 2 * i:2 * i + 2].unsqueeze(3).to_broadcast([P, NC, 2, HD]),
                                  ALU.mult).then_inc(M["xb_kt_done"], 1)

            def k_low(n):
                dve.wait_ge(M["xb_khi"], n + 1)
                dve.tensor_tensor(xb_kn[n % 2][:, :, :, HD:2 * HD].rearrange("p c h d -> p (c h) d"), xb_kt[:, :, :, :].rearrange("p c h d -> p (c h) d"),
                                  xb_kn[n % 2][:, :, :, 0:HD].bitcast(F32).rearrange("p c h d -> p (c h) d"), ALU.subtract).then_inc(M["xb_klo"], 1)

            layernorm(3)
            key_rstd(0)
            dve.wait_ge(M["xb_kr_done"], 1)
            k_full(0)
            k_low(0)
            q_all = xb_q[:, :, :].rearrange("p b d -> p (b d)")
            t_all = xb_t[:, :, :].rearrange("p b d -> p (b d)")
            qk_all = xb_qk[:, :, :].rearrange("p b d -> p (b d)")
            vec = lambda j, n: xb_vec[:, j, :].unsqueeze(1).to_broadcast([P, n, HD])
            dve.wait_ge(M["xb_w_loaded"], 13 * 16)
            dve.wait_ge(M["xb_q_psum"], 1)
            chained(dve.tensor_tensor(xb_q[:, :, :], ps[:, 0, :].rearrange("p (b d) -> p b d", b=B), xb_bq[:, :].unsqueeze(1).to_broadcast([P, B, D]), ALU.add))
            head_norm(q_all, t_all, xb_s32, B * H)
            dve.tensor_reduce(xb_s32[:, 1, :], heads(t_all), AX.X, ALU.add).then_inc(M["xb_q_ss"], 1)
            dve.wait_ge(M["xb_q_sqrt"], 1)
            chained(dve.reciprocal(xb_s32[:, 3, :], xb_s32[:, 2, :]))
            chained(dve.tensor_tensor(heads(q_all), heads(q_all), per_head(xb_s32[:, 3, :], B * H), ALU.mult))
            chained(dve.tensor_tensor(heads(q_all), heads(q_all), vec(0, B * H), ALU.mult))
            dve.tensor_tensor(heads(q_all), heads(q_all), vec(1, B * H), ALU.add).then_inc(M["xb_q_done"], 1)
            dve.wait_ge(M["xb_q_done"], 1)
            chained(dve.scalar_tensor_tensor(out=heads(qk_all), in0=heads(q_all), scalar=SC, in1=vec(2, B * H), op0=ALU.mult, op1=ALU.mult))
            chained(dve.scalar_tensor_tensor(out=heads(t_all), in0=heads(q_all), scalar=SC, in1=vec(3, B * H), op0=ALU.mult, op1=ALU.mult))
            chained(dve.tensor_reduce(xb_qb[:, :], heads(t_all), AX.X, ALU.add))


            def last_rows(stage):
                if stage in (1, 2):
                    b = stage - 1
                    dve.wait_ge(M["xb_last_psum"], 1 + stage)
                    dve.tensor_tensor(xb_kd[:, b, :], ps[:, 3, :], xb_bd[:, :], ALU.add).then_inc(M["xb_kd_read"], 1)
                elif stage in (3, 4):
                    b = stage - 3
                    if b == 0:
                        dve.wait_ge(M["xb_kd_read"], 2)
                    half = xb_d32[:, :, b * H:(b + 1) * H]
                    head_norm(xb_kd[:, b, 0:D], t_all[:, 0:D], half, H)
                    chained(dve.tensor_reduce(half[:, 1, :], heads(t_all[:, 0:D]), AX.X, ALU.add))
                    if b == 1:
                        dve.engine_nop().then_inc(M["xb_kd_ss"], 1)
                elif stage == 5:
                    dve.wait_ge(M["xb_kd_rstd"], 1)
                    for b in range(B):
                        k = heads(xb_kd[:, b, 0:D])
                        chained(dve.tensor_tensor(k, k, per_head(xb_d32[:, 3, b * H:(b + 1) * H], H), ALU.mult))
                        chained(dve.tensor_tensor(k, k, vec(4, H), ALU.mult))
                        chained(dve.tensor_tensor(k, k, vec(5, H), ALU.add))
                        dve.tensor_tensor(xb_kdm[b].rearrange("p (v h d) -> p v h d", h=8, d=HD), xb_kd[:, b, :].rearrange("p (v h d) -> p v h d", h=8, d=HD),
                                          head_mask[:, :].unsqueeze(1).unsqueeze(3).to_broadcast([P, 4, 8, HD]), ALU.mult).then_inc(M["xb_kdm_done"], 1)
                elif stage == 8:
                    dve.wait_ge(M["xb_last_psum"], 6)
                    sd = ps[:, 3, :].rearrange("p (h k) -> p h k", k=DCA)
                    chained(dve.tensor_reduce(xb_d32[:, 0, :], sd, AX.X, ALU.max))
                    dve.tensor_tensor(pd, sd, per_head(xb_d32[:, 0, :], B * H), ALU.subtract).then_inc(M["xb_sd_centred"], 1)
                elif stage == 10:
                    dve.wait_ge(M["xb_last_act"], 4)
                    chained(dve.tensor_reduce(xb_d32[:, 1, :], pd, AX.X, ALU.add))
                    chained(dve.reciprocal(xb_d32[:, 2, :], xb_d32[:, 1, :]))
                    dve.tensor_tensor(pd, pd, per_head(xb_d32[:, 2, :], B * H), ALU.mult).then_inc(M["xb_pd_done"], 1)
                elif stage == 12:
                    dve.wait_ge(M["xb_last_psum"], 8)
                    dve.tensor_copy(xb_o[:, :, :], ps[:, 3, :]).then_inc(M["xb_od_done"], 1)

            pd = xb_pd[:, :, :].rearrange("p b (h k) -> p (b h) k", k=DCA)

            def q_rows(b, h, n, value):
                chained(dve.tensor_copy(xb_qn[:, h:h + n, 3 * HD], value))
                return dve.tensor_tensor(xb_qn[:, h:h + n, 3 * HD + 1], value, xb_qn[:, h:h + n, 3 * HD].bitcast(F32), ALU.subtract)

            for b in range(B):
                if b == 1:
                    dve.wait_ge(M["xb_pv_done"], PAIRS * NU)
                    key_rows(1)
                    key_rstd(1)
                qk = heads(xb_qk[:, b, :])
                chained(dve.tensor_copy(xb_qn[:, :, 0:HD], qk))
                chained(dve.tensor_copy(xb_qn[:, :, HD:2 * HD], qk))
                chained(dve.tensor_tensor(xb_qn[:, :, 2 * HD:3 * HD], qk, xb_qn[:, :, 0:HD].bitcast(F32), ALU.subtract))
                q_rows(b, 0, H, xb_qb[:, b * H:(b + 1) * H]).then_inc(M["xb_qn_done"], 1)
                dve.wait_ge(M["xb_qn_done"], b + 1)
                dve.wait_ge(M["xb_q1_done"], 2 * (b + 1))
                if b == 1:
                    dve.wait_ge(M["xb_kr_done"], b + 1)
                    k_full(b * PAIRS)
                    k_low(b * PAIRS)
                first = b * PAIRS
                for slot in range(-6, UNITS + 9):
                    if 0 <= slot + 4 < UNITS:
                        n, m = first + (slot + 4) // 8, (slot + 4) % 8
                        dve.wait_ge(M["xb_m_psum"], 8 * n + m + 1)
                        dve.tensor_reduce(xb_pm[:, n % 2, 4 * (m % 2) + m // 2:4 * (m % 2) + m // 2 + 1],
                                          ps[:, 1 + m % 2, :].rearrange("p (c k) -> p c k", k=P)[:, :, 0:P - 1],
                                          AX.XY, ALU.max).then_inc(M["xb_m_done"], 1)
                        if m == 7:
                            i = n % PAIRS
                            dve.wait_ge(M["xb_m_done"], 8 * n + 8)
                            chained(dve.tensor_reduce(xb_m[:, n % 2, :], xb_pm[:, n % 2, :].rearrange("p (h u) -> p h u", h=2), AX.X, ALU.max))
                            chained(dve.tensor_tensor(xb_m[:, n % 2, :], xb_qb[:, b * H + 2 * i:b * H + 2 * i + 2], xb_m[:, n % 2, :], ALU.subtract))
                            q_rows(b, 2 * i, 2, xb_m[:, n % 2, :]).then_inc(M["xb_row_done"], 1)
                    if (slot + 14) % 8 == 0 and slot + 14 < UNITS:
                        k_full(first + (slot + 14) // 8)
                    if (slot + 11) % 8 == 0 and slot + 11 < UNITS:
                        k_low(first + (slot + 11) // 8)
                    if b == 0 and (slot + 5) % 3 == 0:
                        last_rows((slot + 5) // 3)
                dve.wait_ge(M["xb_o_psum"], b + 1)
                dve.tensor_copy(xb_oh[:, :], ps[:, 7, :]).then_inc(M["xb_oh_done"], 1)
                dve.wait_ge(M["xb_ohT_psum"], b + 1)
                o = ps[:, 5, :].rearrange("p (h d) -> p h d", h=H)
                chained(dve.reciprocal(xb_den[:, b, :], o[:, :, 2 * HD - 1]))
                chained(dve.tensor_tensor(heads(xb_t[:, b, :]), o[:, :, HD - 1:2 * HD - 1], per_head(xb_den[:, b, :], H), ALU.mult))
                if b == 0:
                    dve.wait_ge(M["xb_od_done"], 1)
                dve.tensor_tensor(xb_o[:, b, :], xb_o[:, b, :], xb_t[:, b, :], ALU.add).then_inc(M["xb_o_done"], 1)
            for b in range(B):
                dve.wait_ge(M["y_psum"], 3 * B + b + 1)
                dve.tensor_tensor(x_sb[:, b, :], x_sb[:, b, :], ps[:, 3 + b, 0:D], ALU.add).then_inc(M["x_updated"], 1)
            if upto < 5:
                return

            layernorm(4)
            dve.wait_ge(M["xn_ready"], 5 * B)
            for b in range(B):
                chained(dve.bn_stats(stats[:, b, :], xn[:, b, :]))
                dve.bn_aggr(sb_mv[:, b, :], stats[:, b, :]).then_inc(M["sb_var"], 1)
            dve.wait_ge(M["sb_var"], B)
            dve.wait_ge(M["sb_rstd_done"], 1)
            dve.wait_ge(M["sb_w_loaded"], 64)
            for b in range(B):
                chained(dve.tensor_scalar(sb_h[:, b, :], xn[:, b, :], sb_mv[:, b, 0:1], sb_rstd[:, b:b + 1], ALU.subtract, ALU.mult))
            chained(dve.tensor_tensor(sb_h[:, :, :], sb_h[:, :, :], sb_g[:, 0, :].unsqueeze(1).to_broadcast([P, B, D]), ALU.mult))
            dve.tensor_tensor(sb_h[:, :, :], sb_h[:, :, :], sb_g[:, 1, :].unsqueeze(1).to_broadcast([P, B, D]), ALU.add).then_inc(M["sb_dve"], 1)
            dve.wait_ge(M["sb_psum"], 4)
            dve.wait_ge(M["sb_masks"], 2)
            chained(dve.tensor_tensor(sb_s[:, :, :], ps[:, 4, 0:B * S].rearrange("p (b s) -> p b s", b=B), causal2[:, :].unsqueeze(1).to_broadcast([P, B, S]), ALU.add))
            chained(dve.tensor_reduce(sb_m[:, 0, :], sb_s[:, :, :], AX.X, ALU.max))
            dve.tensor_tensor(sb_s[:, :, :], sb_s[:, :, :], sb_m[:, 0, :].unsqueeze(2).to_broadcast([P, B, S]), ALU.subtract).then_inc(M["sb_dve"], 1)
            dve.wait_ge(M["sb_act"], 5)
            chained(dve.tensor_reduce(sb_m[:, 1, :], sb_s[:, :, :], AX.X, ALU.add))
            chained(dve.reciprocal(sb_m[:, 2, :], sb_m[:, 1, :]))
            dve.tensor_tensor(sb_s[:, :, :], sb_s[:, :, :], sb_m[:, 2, :].unsqueeze(2).to_broadcast([P, B, S]), ALU.mult).then_inc(M["sb_dve"], 1)
            for b in range(B):
                chained(dve.tensor_tensor(x_sb[:, b, :], x_sb[:, b, :], xn[:, b, :], ALU.add))
            for b in range(B):
                dve.wait_ge(M["y_psum"], 5 * B)
                dve.tensor_tensor(x_sb[:, b, :], x_sb[:, b, :], ps[:, 7, b * D:(b + 1) * D], ALU.add).then_inc(M["x_updated"], 1)
            if upto < 6:
                return

            layernorm(5)
            dve.wait_ge(M["mo_r_loaded"], 32)
            dve.wait_ge(M["mo_psum"], 2)
            chained(dve.tensor_tensor(mo_s[:, :, :], ps[:, 2, 0:B * E].rearrange("p (b e) -> p b e", b=B), mo_bias[:, :].unsqueeze(1).to_broadcast([P, B, E]), ALU.add))
            chained(dve.tensor_reduce(mo_m[:, 0, :], mo_s[:, :, :], AX.X, ALU.max))
            dve.tensor_tensor(mo_s[:, :, :], mo_s[:, :, :], mo_m[:, 0, :].unsqueeze(2).to_broadcast([P, B, E]), ALU.subtract).then_inc(M["mo_centred"], 1)
            dve.wait_ge(M["mo_act"], 2)
            chained(dve.tensor_reduce(mo_m[:, 1, :], mo_s[:, :, :], AX.X, ALU.add))
            chained(dve.reciprocal(mo_m[:, 2, :], mo_m[:, 1, :]))
            chained(dve.tensor_tensor(mo_s[:, :, :], mo_s[:, :, :], mo_m[:, 2, :].unsqueeze(2).to_broadcast([P, B, E]), ALU.mult))
            for b in range(B):
                mine = mo_s[:, b, :].unsqueeze(2).to_broadcast([P, E, E])
                other = mo_s[:, b, :].unsqueeze(1).to_broadcast([P, E, E])
                chained(dve.tensor_tensor(mo_gt[:, b, :, :], other, mine, ALU.is_gt))
                chained(dve.tensor_tensor(mo_eq[:, b, :, :], other, mine, ALU.is_equal))
                chained(dve.tensor_tensor(mo_eq[:, b, :, :], mo_eq[:, b, :, :], mo_first[:, :, :], ALU.mult))
                chained(dve.tensor_tensor(mo_gt[:, b, :, :], mo_gt[:, b, :, :], mo_eq[:, b, :, :], ALU.add))
                chained(dve.tensor_reduce(mo_rank[:, b, :], mo_gt[:, b, :, :], AX.X, ALU.add))
            chained(dve.scalar_tensor_tensor(out=mo_s[:, :, :], in0=mo_rank[:, :, :], scalar=TOP - 0.5, in1=mo_s[:, :, :], op0=ALU.is_lt, op1=ALU.mult))
            chained(dve.tensor_reduce(mo_m[:, 1, :], mo_s[:, :, :], AX.X, ALU.add))
            chained(dve.reciprocal(mo_m[:, 2, :], mo_m[:, 1, :]))
            chained(dve.tensor_tensor(mo_s[:, :, :], mo_s[:, :, :], mo_m[:, 2, :].unsqueeze(2).to_broadcast([P, B, E]), ALU.mult))

            def add_expert(e):
                dve.wait_ge(M["mo_y_psum"], e + 1)
                if e >= 1:
                    dve.wait_ge(M["mo_y_done"], B * e)
                for b in range(B):
                    ins = dve.scalar_tensor_tensor(out=x_sb[:, b, :], in0=ps[:, 0 + 7 * (e % 2), b * D:(b + 1) * D], scalar=mo_s[:, b, e:e + 1], in1=x_sb[:, b, :],
                                                   op0=ALU.mult, op1=ALU.add)
                    ins.then_inc(M["x_updated"] if e == E - 1 else M["mo_y_done"], 1)

            for e in range(E):
                dve.wait_ge(M["mo_silu"], e + 1)
                if e >= 2:
                    dve.wait_ge(M["mo_y_psum"], e - 1)
                dve.tensor_tensor(mo_a[:, e % 2, :, :].rearrange("p i s -> p (i s)"), ps[0:IP, 4 + 2 * (e % 2), :], mo_sg[:, e % 2, :, :].rearrange("p i s -> p (i s)"),
                                  ALU.mult).then_inc(M["mo_a_done"], 1)
                if e >= 1:
                    add_expert(e - 1)
            add_expert(E - 1)

        @block.tensor
        def _(pe):
            def xn_transposes(k):
                pe.wait_ge(M["xn_ready"], B * (k + 1))
                for kc in range(KC):
                    for b in range(B):
                        last = pe.transpose(ps[:, 0, (kc * B + b) * P:(kc * B + b + 1) * P], xn[:, b, kc * P:(kc + 1) * P], ident[:, :])
                last.then_inc(M["xT_psum"], 1)

            pe.wait_ge(M["ident_ready"], 1)
            xn_transposes(0)

            def context_transposes(j):
                if j >= 4:
                    pe.wait_ge(M["qn_done"], j + 1)
                for t in range(4):
                    last = pe.transpose(ps[:, 4 + j % 4, t * P:(t + 1) * P], ctx_nat[:, 4 * j + t, 0:C], ident[:, :])
                last.then_inc(M["ctxT_psum"], 1)

            def query_part(c):
                if c < 8:
                    b, g = c // NG, c % NG
                    if c == 0:
                        pe.wait_ge(M["wq_loaded"], 16)
                    if c < 4:
                        pe.wait_ge(M["ctxT_lo_done"], c + 1)
                    else:
                        pe.wait_ge(M["qn_done"], c - 3)
                    for kc in range(KC):
                        last = pe.matmul(ps[:, 4 + c % 4, :], xnT[:, kc, b * S:(b + 1) * S],
                                         wq[:, kc, g * 512:(g + 1) * 512], start=(kc == 0), stop=(kc == KC - 1))
                    last.then_inc(M["q_psum"], 1)
                elif c < 12:
                    if c == 8:
                        pe.wait_ge(M["ctx1_loaded"], 16)
                    context_transposes(c - 4)
                elif c < 14:
                    for j in (2 * (c - 12), 2 * (c - 12) + 1):
                        pe.wait_ge(M["ctxT_lo_done"], j + 5)
                        for t in range(4):
                            h = 4 * j + t
                            last = pe.transpose(ps[:, 4 + j, t * P:(t + 1) * P], wk[:, h * P:(h + 1) * P], ident[:, :])
                        last.then_inc(M["wkT_psum"], 1)
                elif c < 18:
                    for j in (2 * (c - 14), 2 * (c - 14) + 1):
                        if j >= 2:
                            pe.wait_ge(M["qT_done"], j - 1)
                        else:
                            pe.wait_ge(M["wkT_done"], H // 4)
                        for t in range(2):
                            for b in range(B):
                                last = pe.transpose(ps[:, 4 + j % 2, (t * B + b) * P:(t * B + b + 1) * P], qn[:, b, 2 * j + t, :], ident[:, :])
                        last.then_inc(M["qT_psum"], 1)
                elif c < 26:
                    j = c - 18
                    pe.wait_ge(M["qT_done"], j + 1)
                    if j >= 2:
                        pe.wait_ge(M["q3_lo_done"], j - 1)
                    for t in range(2):
                        h = 2 * j + t
                        last = pe.matmul(ps[:, 6 + j % 2, t * B * S:(t + 1) * B * S], wkT[:, h, :], qT[:, h, :], start=True, stop=True)
                    last.then_inc(M["q3_psum"], 1)

            pe.wait_ge(M["ctx_loaded"], 16)
            for j in range(4):
                context_transposes(j)
            pe.wait_ge(M["wk_split"], 1)
            pe.wait_ge(M["xnT_ready"], 1)
            for c in range(B * NC):
                if c % 4 == 0:
                    pe.wait_ge(M["ctxT_lo_done"], c // 4 + 1)
                for g in range(NG):
                    i = c * NG + g
                    if i >= 4:
                        pe.wait_ge(M["k_squared"], i - 3)
                    r = slice(g * 512, (g + 1) * 512)
                    pe.matmul(ps[:, i % 4, :], ctxT_hi[:, c, :], wk_hi[:, r], start=True, stop=False)
                    pe.matmul(ps[:, i % 4, :], ctxT_hi[:, c, :], wk_lo[:, r], start=False, stop=False)
                    pe.matmul(ps[:, i % 4, :], ctxT_lo[:, c, :], wk_hi[:, r], start=False, stop=True).then_inc(M["k_psum"], 1)
                query_part(c)
            pe.wait_ge(M["q3_lo_done"], H // 2)
            pe.wait_ge(M["wabs_done"], 2)
            pe.matmul(ps[:, 7, 0:2], ones[:, :], w_abs[:, :], start=True, stop=True).then_inc(M["wabs_psum"], 1)
            pe.wait_ge(M["k_squared"], B * NC * NG)

            STEPS = B * NG * (NC // 2)

            def scores(i):
                b, g, c2 = i // (NG * NC // 2), i // (NC // 2) % NG, i % (NC // 2)
                if i >= 2:
                    pe.wait_ge(M["s_scaled"], i - 1)
                for t in range(2):
                    c = b * NC + 2 * c2 + t
                    bank = 2 * (i % 2) + t
                    q_hi = q3_hi[:, b, G * g:G * g + G, :]
                    q_lo = q3_lo[:, b, G * g:G * g + G, :]
                    pe.matmul(ps[:, bank, :], ctxT_hi[:, c, :], q_hi, start=True, stop=False)
                    pe.matmul(ps[:, bank, :], ctxT_hi[:, c, :], q_lo, start=False, stop=False)
                    last = pe.matmul(ps[:, bank, :], ctxT_lo[:, c, :], q_hi, start=False, stop=True)
                last.then_inc(M["s_psum"], 1)

            def weighted_sums(i):
                b, g, c2 = i // (NG * NC // 2), i // (NC // 2) % NG, i % (NC // 2)
                j = b * NG + g
                pe.wait_ge(M["p_done"], i + 1)
                if c2 == 0 and j == 1:
                    pe.wait_ge(M["wq_quant"], 1)
                if c2 == 0 and j >= 2:
                    pe.wait_ge(M["o_done"], j - 1)
                for t in range(2):
                    c = b * NC + 2 * c2 + t
                    for h in range(G):
                        at = ps[:, 4 + 2 * (j % 2) + h // 2, (h % 2) * (C + 2):(h % 2) * (C + 2) + C + 1]
                        first = c2 == 0 and t == 0
                        last = pe.matmul(at, p_sb[:, i % 2, t, h * S:(h + 1) * S], ctx_nat[:, c, 0:C + 1],
                                         start=first and h % 2 == 0, stop=(c2 == NC // 2 - 1 and t == 1), skip_group_check=True)
                last.then_inc(M["pv_chunk"], 1)
                if c2 == NC // 2 - 1:
                    pe.wait_ge(M["pv_chunk"], i + 1)
                    pe.nop().then_inc(M["o_psum"], 1)

            for i in range(STEPS + 1):
                if i < STEPS:
                    scores(i)
                if i >= 1:
                    weighted_sums(i - 1)
            pe.wait_ge(M["o_done"], B * NG)
            pe.wait_ge(M["wv_loaded"], 16)
            pe.wait_ge(M["wo_loaded"], 16)
            for j in range(H // 2):
                if j >= 2:
                    pe.wait_ge(M["oT_done"], j - 1)
                for t in range(2):
                    for b in range(B):
                        last = pe.transpose(ps[:, j % 2, (t * B + b) * P:(t * B + b + 1) * P], o_n[:, b, 2 * j + t, :], ident[:, :])
                last.then_inc(M["oT_psum"], 1)
            for j in range(H // 2):
                pe.wait_ge(M["oT_done"], j + 1)
                if j >= 2:
                    pe.wait_ge(M["aT_done"], j - 1)
                for t in range(2):
                    h = 2 * j + t
                    last = pe.matmul(ps[:, 2 + j % 2, t * B * S:(t + 1) * B * S], wv[:, h, :], oT[:, h, :], start=True, stop=True)
                last.then_inc(M["aT_psum"], 1)
            pe.wait_ge(M["aT_done"], H // 2)
            for b in range(B):
                for h in range(H):
                    last = pe.matmul(ps[:, 4 + b, 0:D], aT[:, h, b * S:(b + 1) * S], wo[:, h, :], start=(h == 0), stop=(h == H - 1))
                last.then_inc(M["y_psum"], 1)

            if upto < 2:
                return
            def weight_transposes(i):
                pe.wait_ge(M["wq_quant"], 4 + 3 * (i // 4))
                pe.wait_ge(M["sa_s_masked"], KC * (i // 4 + 1))
                for t in range(4):
                    if i < 4:
                        src = w1[:, 4 * (i % 2) + t, (i // 2) * P:(i // 2 + 1) * P]
                    else:
                        ic, o = 2 * (i - 4) + t // 2, t % 2
                        src = w2[:, o, ic * P:(ic + 1) * P]
                    last = pe.transpose(ps[:, (4 + i) % 8, t * P:(t + 1) * P], src, ident[:, :])
                last.then_inc(M["wqT_psum"], 1)

            xn_transposes(1)
            pe.wait_ge(M["xnT_ready"], 2)
            pe.wait_ge(M["sa_w_loaded"], 128)
            for t in range(2):
                for j in range(KC):
                    for kc in range(KC):
                        last = pe.matmul(ps[:, 1 + t, j * B * S:(j + 1) * B * S], w_in[:, kc, t * D + j * P:t * D + (j + 1) * P],
                                         xnT[:, kc, :], start=(kc == 0), stop=(kc == KC - 1))
            last.then_inc(M["sa_q_psum"], 1)
            for b in range(B):
                for kc in range(KC):
                    pe.matmul(ps[:, 3, b * D:(b + 1) * D], xnT[:, kc, b * S:(b + 1) * S], w_in[:, kc, 2 * D:3 * D], start=(kc == 0), stop=False)
                last = pe.matmul(ps[:, 3, b * D:(b + 1) * D], ones[0:1, :], b_in_row[:, 2 * D:3 * D], start=False, stop=True)
            last.then_inc(M["sa_v_psum"], 1)
            for b in range(B):
                if b == 1:
                    pe.wait_ge(M["sa_v_done"], 2)
                    pe.wait_ge(M["sa_qkT"], 2 * KC)
                for j in range(KC):
                    i = b * KC + j
                    pe.wait_ge(M["sa_km_done"], i + 1)
                    for t in range(2):
                        last = pe.matmul(ps[:, 4 * (1 - b) + 2 * j + t, :], sa_qT[:, j, b * S:(b + 1) * S],
                                         sa_km[:, i % 2, 4 * t:4 * t + 4, :], start=True, stop=True)
                    last.then_inc(M["sa_s_psum"], 1)
            for i in range(8):
                weight_transposes(i)
            for b in range(B):
                pe.wait_ge(M["sa_p_done"], b + 1)
                pe.wait_ge(M["wqT_done"], 4 * (b + 1))
                for g in range(4):
                    for t in range(4):
                        last = pe.transpose(ps[:, 4 * (1 - b) + g, t * P:(t + 1) * P], sa_s[:, b, 4 * g + t, :], ident[:, :])
                    last.then_inc(M["sa_pT_psum"], 1)
            def context_transposes_2(b, g):
                if b == 0:
                    pe.wait_ge(M["sa_pT_done"], 4 if g == 0 else 8)
                    if g >= 2:
                        pe.wait_ge(M["xb_cT_done"], g - 1)
                bank = 1 + g if b == 1 else 7 - 4 * (g % 2)
                for t in range(4):
                    last = pe.transpose(ps[:, bank, t * P:(t + 1) * P], ctx_nat[:, b * NC + 4 * g + t, 0:C], ident[:, :])
                last.then_inc(M["xb_cT_psum"], 1)

            def key_products(first, last):
                if first == 0:
                    pe.wait_ge(M["xb_cT_done"], 4)
                    pe.wait_ge(M["xb_centred"], 2)
                for c in range(first, last):
                    if c >= 2:
                        pe.wait_ge(M["xb_kv_done"], c if c == NC // 2 else c - 1)
                    pe.matmul(ps[:, KEY_BANKS[c], :], xb_cT[0][:, c, :], xb_wkv[:, :], start=True, stop=False)
                    pe.matmul(ps[:, KEY_BANKS[c], :], ones[0:1, :], xb_bkv[0:1, :], start=False, stop=True).then_inc(M["xb_kv_psum"], 1)

            if upto >= 4:
                for g in range(4):
                    context_transposes_2(0, g)
            for b in range(B):
                pe.wait_ge(M["sa_pT_done"], 4 * b + 4)
                for h in range(H):
                    last = pe.matmul(ps[:, 4 * (1 - b), h * (HD + 2):h * (HD + 2) + HD + 1], sa_pT[:, b, h, :], sa_v[:, b, h, 0:HD + 1],
                                     start=True, stop=True)
                last.then_inc(M["sa_o_psum"], 1)
            if upto >= 4:
                key_products(0, 2)
            for b in range(B):
                pe.wait_ge(M["sa_o_done"], b + 1)
                for kc in range(KC):
                    last = pe.transpose(ps[:, 4 * (1 - b) + 1, kc * S:(kc + 1) * S], sa_o[:, b, kc * P:(kc + 1) * P], ident[:, :])
                last.then_inc(M["sa_oT_psum"], 1)
            for b in range(B):
                pe.wait_ge(M["sa_oT_done"], b + 1)
                y = ps[:, 4 * (1 - b) + 2, 0:D]
                for kc in range(KC):
                    pe.matmul(y, sa_oT[:, kc, b * S:(b + 1) * S], w_out[:, kc, :], start=(kc == 0), stop=False)
                pe.matmul(y, ones[0:1, :], b_out_row[:, :], start=False, stop=True).then_inc(M["y_psum"], 1)
            if upto >= 4:
                key_products(2, 8)
            if upto < 3:
                return
            pe.wait_ge(M["ff_q_done"], B)
            for kc in range(KC):
                for b in range(B):
                    last = pe.transpose(ps[:, 0, (kc * B + b) * P:(kc * B + b + 1) * P], ff_q1[:, b, kc * P:(kc + 1) * P], ident[:, :])
            last.then_inc(M["ff_qT_psum"], 1)
            pe.wait_ge(M["ff_qT_done"], 1)
            if upto >= 4:
                pe.wait_ge(M["xb_kv_done"], 7)
            pe.wait_ge(M["wqT_done"], 8)
            for b in range(B):
                for t in range(2):
                    for kc in range(KC):
                        last = pe.matmul(ps[:, 4 + 2 * b + t, :], ff_qT1[:, kc, b * S:(b + 1) * S], w1qT[:, kc, t * 512:(t + 1) * 512],
                                         start=(kc == 0), stop=(kc == KC - 1))
                last.then_inc(M["ff_h_psum"], 1)
            if upto >= 4:
                key_products(8, NC)
            for b in range(B):
                pe.wait_ge(M["ff_q_done"], B + b + 1)
                for g in range(2):
                    for t in range(4):
                        last = pe.transpose(ps[:, 4 + 2 * b + g, t * P:(t + 1) * P], ff_h[:, b, (4 * g + t) * P:(4 * g + t + 1) * P], ident[:, :])
                    last.then_inc(M["ff_qT_psum"], 1)
            for b in range(B):
                pe.wait_ge(M["ff_qT_done"], 1 + 2 * (b + 1))
                for ic in range(FC):
                    last = pe.matmul(ps[:, 1 + b, 0:D], ff_qT2[:, ic, b * S:(b + 1) * S], w2qT[:, ic, :], start=(ic == 0), stop=(ic == FC - 1))
                last.then_inc(M["y_psum"], 1)
            if upto < 4:
                return

            xn_transposes(3)
            pe.wait_ge(M["xnT_ready"], 3)
            pe.wait_ge(M["xb_w_loaded"], 13 * 16)
            for b in range(B):
                for kc in range(KC):
                    last = pe.matmul(ps[:, 0, b * D:(b + 1) * D], xnT[:, kc, b * S:(b + 1) * S], xb_wq[:, kc, :], start=(kc == 0), stop=(kc == KC - 1))
            last.then_inc(M["xb_q_psum"], 1)

            def last_rows(stage):
                if stage == 0:
                    for b in range(B):
                        last = pe.transpose(ps[:, 3, b * DCA:(b + 1) * DCA], xb_yd[:, b, :], ident[0:DCA, 0:DCA])
                elif stage in (1, 2):
                    b = stage - 1
                    if b == 0:
                        pe.wait_ge(M["xb_last_act"], 1)
                    else:
                        pe.wait_ge(M["xb_kd_read"], 1)
                    last = pe.matmul(ps[:, 3, :], xb_ydT[:, b, :, :].rearrange("p r k -> p (r k)"), xb_wd[:, :], start=True, stop=True)
                elif stage == 6:
                    pe.wait_ge(M["xb_kdm_done"], B)
                    for b in range(B):
                        for kc in range(KC):
                            last = pe.transpose(ps[:, 3, (b * KC + kc) * P:(b * KC + kc + 1) * P], xb_kdm[b][:, kc * P:(kc + 1) * P], ident[:, :])
                elif stage == 7:
                    pe.wait_ge(M["xb_last_act"], 2)
                    for kc in range(KC):
                        for b in range(B):
                            last = pe.transpose(ps[:, 3, (kc * B + b) * S:(kc * B + b + 1) * S], xb_q[:, b, kc * P:(kc + 1) * P], ident[:, :])
                elif stage == 8:
                    pe.wait_ge(M["xb_last_act"], 3)
                    for b in range(B):
                        for kc in range(KC):
                            last = pe.matmul(ps[:, 3, b * D + kc * P:b * D + (kc + 1) * P], xb_qfT[:, kc, b * S:(b + 1) * S], xb_kdT[:, b, kc, :], start=True, stop=True)
                elif stage == 11:
                    pe.wait_ge(M["xb_pd_done"], 1)
                    for kc in range(KC):
                        for b in range(B):
                            last = pe.transpose(ps[:, 3, (kc * B + b) * S:(kc * B + b + 1) * S], xb_pd[:, b, kc * P:(kc + 1) * P], ident[:, :])
                elif stage == 12:
                    pe.wait_ge(M["xb_last_act"], 5)
                    for b in range(B):
                        for kc in range(KC):
                            last = pe.matmul(ps[:, 3, b * D + kc * P:b * D + (kc + 1) * P], xb_pdT[:, kc, b * S:(b + 1) * S],
                                             xb_kdm[b][:, D + kc * P:D + (kc + 1) * P], start=True, stop=True)
                else:
                    return
                last.then_inc(M["xb_last_psum"], 1)

            def k_transposes(n, g):
                pe.wait_ge(M["xb_klo"], n + 1)
                if 4 * n + g >= 2:
                    pe.wait_ge(M["xb_kT_done"], 4 * n + g - 1)
                for t in range(4):
                    last = pe.transpose(ps[:, 4 * (g % 2), t * P:(t + 1) * P],
                                        xb_kn[n % 2][:, 4 * g + t, :, :].bitcast(F32).rearrange("p h w -> p (h w)"), ident[:, :])
                last.then_inc(M["xb_kT_psum"], 1)

            def maxima(n, m):
                pe.wait_ge(M["xb_kT_done"], 4 * n + m // 2 + 1)
                if 8 * n + m >= 2:
                    pe.wait_ge(M["xb_m_done"], 8 * n + m - 1)
                r = slice(W * (m % 2), W * (m % 2) + W)
                pe.matmul(ps[:, 1 + m % 2, :], xb_qT1[r, n % PAIRS, :], xb_kT[r, n % 2, 4 * (m // 2):4 * (m // 2) + 4, :],
                          start=True, stop=True).then_inc(M["xb_m_psum"], 1)

            def q_transpose(n):
                i = n % PAIRS
                pe.wait_ge(M["xb_row_done"], n + 1)
                pe.wait_ge(M["xb_kT_done"], min(4 * n + 7, 4 * PAIRS * (n // PAIRS + 1)))
                pe.transpose(ps[:, 0, 0:S], xb_qn[:, 2 * i:2 * i + 2, :].bitcast(F32).rearrange("p h w -> p (h w)"), ident[:, :]).then_inc(M["xb_q2_psum"], 1)

            def scores_t(n, u):
                m = n * NU + u
                pe.wait_ge(M["xb_q2_done"], n + 1)
                if m >= 2:
                    pe.wait_ge(M["xb_p_done"], m - 1)
                for t in range(2):
                    last = pe.matmul(ps[:, 5 + u % 2, t * 2 * S:(t + 1) * 2 * S], xb_kT[:, n % 2, 2 * u + t, :], xb_qT2[:, n % 2, :],
                                     start=True, stop=True)
                last.then_inc(M["xb_s_psum"], 1)

            def head_sums(n, u):
                m, i = n * NU + u, n % PAIRS
                pe.wait_ge(M["xb_p_done"], m + 1)
                for t in range(2):
                    c = 2 * u + t
                    for h in (2 * i, 2 * i + 1):
                        last = pe.matmul(ps[32 * (h % 4):32 * (h % 4) + 32, 7, (h // 4) * S:(h // 4 + 1) * S], xb_kv[0:P - 1, c, h, 1:2 * HD + 1],
                                         xb_p[0:P - 1, m % 2, 2 * t + h % 2, :], start=(c == 0), stop=(c == NC - 1), skip_group_check=True)
                last.then_inc(M["xb_pv_done"], 1)

            for b in range(B):
                if b == 1:
                    pe.wait_ge(M["xb_od_done"], 1)
                    pe.wait_ge(M["xb_m_done"], 8 * PAIRS)
                    for g in range(4):
                        context_transposes_2(1, g)
                    pe.wait_ge(M["xb_cT_done"], 8)
                    for c in range(NC):
                        if c >= 4:
                            pe.wait_ge(M["xb_kv_done"], NC + c - 3)
                        pe.matmul(ps[:, 1 + c % 4, :], xb_cT[1][:, c, :], xb_wkv[:, :], start=True, stop=True).then_inc(M["xb_kv_psum"], 1)
                pe.wait_ge(M["xb_qn_done"], b + 1)
                pe.wait_ge(M["xb_kv_done"], (b + 1) * NC)
                for g in range(2):
                    for t in range(4):
                        j = 4 * g + t
                        last = pe.transpose(ps[:, 1 + g, t * P:(t + 1) * P], xb_qn[:, 2 * j:2 * j + 2, :].bitcast(F32).rearrange("p h w -> p (h w)"), ident[:, :])
                    last.then_inc(M["xb_q1_psum"], 1)
                pe.wait_ge(M["xb_q1_done"], 2 * (b + 1))
                pe.wait_ge(M["xb_const"], 7 + 2 * b)
                if b == 1:
                    pe.wait_ge(M["xb_o_done"], 1)
                first = b * PAIRS
                for slot in range(-6, UNITS + 9):
                    if 0 <= slot - 8 < UNITS:
                        scores_t(first + (slot - 8) // 8, slot % 8)
                    if 0 <= slot + 4 < UNITS:
                        maxima(first + (slot + 4) // 8, (slot + 4) % 8)
                    if 0 <= slot + 6 < UNITS and slot % 2 == 0:
                        k_transposes(first + (slot + 6) // 8, (slot + 6) % 8 // 2)
                    if slot % 8 == 7 and 0 <= slot < UNITS:
                        q_transpose(first + slot // 8)
                    if 0 <= slot - 9 < UNITS:
                        head_sums(first + (slot - 9) // 8, (slot - 9) % 8)
                    if b == 0 and (slot + 5) % 3 == 0:
                        last_rows((slot + 5) // 3)
                pe.wait_ge(M["xb_pv_done"], (b + 1) * PAIRS * NU)
                pe.nop().then_inc(M["xb_o_psum"], 1)
                pe.wait_ge(M["xb_oh_done"], b + 1)
                pe.wait_ge(M["xb_p_done"], (b + 1) * PAIRS * NU)
                for g in range(4):
                    last = pe.transpose(ps[:, 5, g * S:(g + 1) * S], xb_oh[:, g * S:(g + 1) * S], ident[:, :])
                last.then_inc(M["xb_ohT_psum"], 1)
            for b in range(B):
                pe.wait_ge(M["xb_o_done"], b + 1)
                for kc in range(KC):
                    last = pe.transpose(ps[:, 1 + b, kc * S:(kc + 1) * S], xb_o[:, b, kc * P:(kc + 1) * P], ident[:, :])
                last.then_inc(M["xb_oT_psum"], 1)
            for b in range(B):
                pe.wait_ge(M["xb_oT_done"], b + 1)
                for kc in range(KC):
                    pe.matmul(ps[:, 3 + b, 0:D], xb_qfT[:, kc, b * S:(b + 1) * S], xb_wo[:, kc, :], start=(kc == 0), stop=False)
                pe.matmul(ps[:, 3 + b, 0:D], ones[0:1, :], xb_wo_row[:, :], start=False, stop=True).then_inc(M["y_psum"], 1)
            if upto < 5:
                return

            pe.wait_ge(M["sb_dve"], 1)
            for kc in range(KC):
                for b in range(B):
                    last = pe.transpose(ps[:, 0, (kc * B + b) * P:(kc * B + b + 1) * P], sb_h[:, b, kc * P:(kc + 1) * P], ident[:, :])
            last.then_inc(M["sb_psum"], 1)
            pe.wait_ge(M["sb_act"], 1)
            for t in range(2):
                for j in range(KC):
                    for kc in range(KC):
                        last = pe.matmul(ps[:, 1 + t, j * B * S:(j + 1) * B * S], sb_w[:, kc, t * D + j * P:t * D + (j + 1) * P], sb_hT[:, kc, :],
                                         start=(kc == 0), stop=(kc == KC - 1))
            last.then_inc(M["sb_psum"], 1)
            pe.wait_ge(M["x_updated"], 4 * B)
            for b in range(B):
                for kc in range(KC):
                    last = pe.matmul(ps[:, 3, b * D:(b + 1) * D], sb_hT[:, kc, b * S:(b + 1) * S], sb_w[:, kc, 2 * D:3 * D], start=(kc == 0), stop=(kc == KC - 1))
            last.then_inc(M["sb_psum"], 1)
            pe.wait_ge(M["sb_act"], 3)
            for b in range(B):
                for kc in range(KC):
                    last = pe.matmul(ps[:, 4, b * S:(b + 1) * S], sb_qT[:, kc, b * S:(b + 1) * S], sb_kT[:, kc, b * S:(b + 1) * S], start=(kc == 0), stop=(kc == KC - 1))
            last.then_inc(M["sb_psum"], 1)
            pe.wait_ge(M["sb_dve"], 3)
            for b in range(B):
                last = pe.transpose(ps[:, 5, b * S:(b + 1) * S], sb_s[:, b, :], ident[:, :])
            last.then_inc(M["sb_psum"], 1)
            pe.wait_ge(M["sb_act"], 6)
            pe.wait_ge(M["sb_act"], 4)
            for kc in range(KC):
                for b in range(B):
                    last = pe.matmul(ps[:, 6, (kc * B + b) * S:(kc * B + b + 1) * S], sb_v[:, b, kc * P:(kc + 1) * P], sb_pT[:, b, :], start=True, stop=True)
            last.then_inc(M["sb_psum"], 1)
            pe.wait_ge(M["sb_act"], 7)
            for b in range(B):
                for kc in range(KC):
                    last = pe.matmul(ps[:, 7, b * D:(b + 1) * D], sb_oT[:, kc, b * S:(b + 1) * S], sb_wo[:, kc, :], start=(kc == 0), stop=(kc == KC - 1))
                last.then_inc(M["y_psum"], 1)
            if upto < 6:
                return

            pe.wait_ge(M["mo_r_loaded"], 32)
            for kc in range(KC):
                last = pe.transpose(ps[:, 1, kc * E:(kc + 1) * E], mo_r[:, kc * P:(kc + 1) * P], ident[0:E, 0:E])
            last.then_inc(M["mo_psum"], 1)
            xn_transposes(5)
            pe.wait_ge(M["xnT_ready"], 4)
            pe.wait_ge(M["mo_act"], 1)
            for b in range(B):
                for kc in range(KC):
                    last = pe.matmul(ps[:, 2, b * E:(b + 1) * E], xnT[:, kc, b * S:(b + 1) * S], mo_rT[:, kc, :], start=(kc == 0), stop=(kc == KC - 1))
            last.then_inc(M["mo_psum"], 1)
            pe.wait_ge(M["mo_w_loaded"], 16 * 16)
            pe.wait_ge(M["mo_down_loaded"], 8 * 16)
            for e in range(E + 1):
                if e < E:
                    if e >= 2:
                        pe.wait_ge(M["mo_a_done"], e - 1)
                    for t, w in ((0, mo_gate), (1, mo_up)):
                        for ic in range(IC):
                            for kc in range(KC):
                                last = pe.matmul(ps[0:IP, 3 + 2 * (e % 2) + t, ic * B * S:(ic + 1) * B * S], w[:, e, kc, ic * IP:(ic + 1) * IP], xnT[:, kc, :],
                                                 start=(kc == 0), stop=(kc == KC - 1))
                    last.then_inc(M["mo_gu_psum"], 1)
                if e >= 1:
                    f = e - 1
                    pe.wait_ge(M["mo_a_done"], f + 1)
                    if f == 1:
                        pe.wait_ge(M["x_updated"], 5 * B)
                    if f >= 2:
                        pe.wait_ge(M["mo_y_done"], B * (f - 1))
                    for b in range(B):
                        for ic in range(IC):
                            last = pe.matmul(ps[:, 7 * (f % 2), b * D:(b + 1) * D], mo_a[:, f % 2, ic, b * S:(b + 1) * S], mo_down[:, f, ic, :],
                                             start=(ic == 0), stop=(ic == IC - 1))
                    last.then_inc(M["mo_y_psum"], 1)


def kernel(**inputs):
    import concourse.bacc as bacc
    from concourse.bass_utils import run_bass_kernel_spmd

    nc = bacc.Bacc("TRN2", target_bir_lowering=False, num_devices=1)
    arrays, args = {}, {}
    for name, value in inputs.items():
        value = np.ascontiguousarray(value)
        arrays[f"in_{name}"] = value
        args[name] = nc.dram_tensor(f"in_{name}", value.shape, mybir.dt.from_np(value.dtype), kind="ExternalInput").ap()
    out = nc.dram_tensor("out", inputs["x"].shape, F32, kind="ExternalOutput").ap()
    build(nc, args, out)
    return run_bass_kernel_spmd(nc, [arrays], core_ids=[0]).results[0]["out"]
```

```python
from contextlib import ExitStack

import numpy as np
import concourse.bass as bass
from concourse import mybir

F32 = mybir.dt.float32
F32R = mybir.dt.float32r
BF16 = mybir.dt.bfloat16
ALU = mybir.AluOpType
ACT = mybir.ActivationFunctionType
AX = mybir.AxisListType

P = 128
EPS = 1e-5


def build(nc, a, out):
    B, S, D = a["x"].shape
    KV = a["ctx_1024"].shape[1]
    C = a["ctx_1024"].shape[2]
    H = 16
    HD0 = a["L0_xattn_gq"].shape[0]
    NC = KV // P
    KC = D // P
    G = 4
    NG = H // G
    assert S == P and C == P and HD0 == P

    ctx = ExitStack()
    with ctx:
        def sb(name, shape, dt=F32):
            return ctx.enter_context(nc.sbuf_tensor(name, shape, dt))

        def sem(name):
            return ctx.enter_context(nc.semaphore(name))

        ps = ctx.enter_context(nc.psum_tensor("ps", [P, 8, 512], F32))

        ident = sb("ident", [P, P])
        ones = sb("ones", [P, P])
        neg_half = sb("neg_half", [P, 32])
        x_sb = sb("x_sb", [P, B, D])
        stats = sb("stats", [P, B, 6])
        meanvar = sb("meanvar", [P, B, 2])
        veps = sb("veps", [P, B])
        rstd = sb("rstd", [P, B])
        xn = sb("xn", [P, B, D])
        xnT = sb("xnT", [P, KC, B * S])
        ctx_nat = sb("ctx_nat", [P, B * NC, C + 2])
        KB = 1024
        ARENA = 168 * KB
        arena_start = nc.sbuf_base
        arena = sb("arena", [P, ARENA // 4])
        base = -(-arena_start // 32) * 32

        def at(name, offset, shape, dt=F32):
            size = int(np.prod(shape[1:])) * mybir.dt.size(dt)
            assert offset + size <= ARENA
            return nc.alloc_sbuf_tensor_at(name, shape, dt, offset=base + offset)

        ctxT_hi = at("ctxT_hi", 0, [P, B * NC, P], F32R)
        ctxT_lo = at("ctxT_lo", 16 * KB, [P, B * NC, P], F32R)
        wk_hi = at("wk_hi", 32 * KB, [P, H * HD0], F32R)
        wk_lo = at("wk_lo", 40 * KB, [P, H * HD0], F32R)
        wk = at("wk", 48 * KB, [P, H * HD0])
        s_sb = at("s_sb", 48 * KB, [P, 2, 2, 512])
        wkT = at("wkT", 56 * KB, [P, H, C])
        p_sb = at("p_sb", 56 * KB, [P, 2, 2, 512])
        q3_hi = at("q3_hi", 64 * KB, [P, B, H, S], F32R)
        q3_lo = at("q3_lo", 80 * KB, [P, B, H, S], F32R)
        wq = at("wq", 96 * KB, [P, KC, H * HD0])
        wv = at("wv", 112 * KB, [P, H, HD0])
        wo = at("wo", 120 * KB, [P, H, D])
        qn = at("qn", 136 * KB, [P, B, H, HD0])
        qT = at("qT", 152 * KB, [P, H, B * S])
        gains = sb("gains", [P, 2])
        gqk = sb("gqk", [P, 1])
        sq = sb("sq", [P, 2, 512])
        q_sq = at("q_sq", 64 * KB, [P, 2, 512])
        q_ss = sb("q_ss", [P, B, H])
        q_rstd = sb("q_rstd", [P, B, H])
        k_stats = sb("k_stats", [P, 2, B * NC, H])
        k_ss, k_rstd = k_stats[:, 0, :, :], k_stats[:, 1, :, :]
        shift = sb("shift", [P, 1])
        gain_max = sb("gain_max", [1, 1])
        o_den = sb("o_den", [P, B * NG, G])
        o_n = qn
        oT = qT
        aT = at("aT", 64 * KB, [P, H, B * S])

        HD = D // H
        w_in = at("w_in", 0, [P, KC, 3 * D])
        w_out = at("w_out", 6 * KB, [P, KC, D])
        bqk = sb("bqk", [P, 2 * KC])
        b_in_row = at("b_in_row", 16 * KB, [1, 3 * D])
        b_out_row = at("b_out_row", 19 * KB, [1, D])
        head_mask = sb("head_mask", [P, 8])
        causal = at("causal", 28 * KB, [P, S])
        sa_s = at("sa_s", 152 * KB, [P, B, H, S])
        sa_qT = at("sa_qT", 120 * KB, [P, KC, B * S])
        sa_kT = at("sa_kT", 122 * KB, [P, KC, B * S])
        sa_km = at("sa_km", 124 * KB, [P, 2, 8, S])
        sa_v = at("sa_v", 132 * KB, [P, B, H, HD + 2])
        sa_o = at("sa_o", 135 * KB, [P, B, D])
        sa_oT = at("sa_oT", 137 * KB, [P, KC, B * S])
        sa_pT = at("sa_pT", 48 * KB, [P, B, H, S])
        sa_max = sb("sa_max", [P, B, H])
        sa_den = sb("sa_den", [P, B, H])
        FI = a["L0_ffn_w1"].shape[0]
        FC = FI // P
        w1 = at("w1", 96 * KB, [P, FC, D])
        w2 = at("w2", 104 * KB, [P, KC, FI])
        w1qT = at("w1qT", 139 * KB, [P, KC, FI], BF16)
        w2qT = at("w2qT", 143 * KB, [P, FC, D], BF16)
        b1_all = at("b1_all", 8 * KB, [P, FI])
        lng_all = at("lng_all", 12 * KB, [P, FI])
        lnb_all = at("lnb_all", 24 * KB, [P, FI])
        b2_all = at("b2_all", 20 * KB, [P, D])
        w_sizes = at("w_sizes", 136 * KB, [P, FC * D])
        w_abs = sb("w_abs", [P, 2])
        w_mean = sb("w_mean", [P, 2])
        w_scale = sb("w_scale", [P, 2])
        ff_ss = sb("ff_ss", [P, 2, B])
        ff_r = sb("ff_r", [P, 2, B])
        ff_max = sb("ff_max", [P, 2, B])
        ff_s = sb("ff_s", [P, 2, B])
        ff_dq = sb("ff_dq", [P, 2, B])
        ff_q1 = at("ff_q1", 128 * KB, [P, B, D])
        ff_sq = at("ff_sq", 152 * KB, [P, B, FI])
        ff_qT1 = at("ff_qT1", 130 * KB, [P, KC, B * S], BF16)
        ff_h = at("ff_h", 48 * KB, [P, B, FI])
        ff_h2 = at("ff_h2", 56 * KB, [P, B, FI])
        ff_qT2 = at("ff_qT2", 124 * KB, [P, FC, B * S], BF16)
        ff_stats = sb("ff_stats", [P, B, 2, 6])
        ff_mv = sb("ff_mv", [P, B, 2])
        ff_rstd = sb("ff_rstd", [P, B])

        DCA = 16
        assert DCA == NC
        PAIRS = H // 2
        W = 64
        NU = NC // 2
        EPS2 = 1e-6
        SC = float(HD) ** -0.5
        UNITS = PAIRS * NU
        OFFSET = UNITS + 8
        LAST_SLOTS = {-5: 0, -2: 1, 1: 2, 4: 3, 7: 4, 17: 5, 19: 13, 20: 6, 22: 7, 24: 8, 26: 9, 28: 10, 31: 11, 34: 12}

        def v_heads(c):
            return xb_v[:, c, HD - 1:HD - 1 + H * VW].rearrange("p (h d) -> p h d", d=VW)[:, :, 0:HD]

        def unit_at(slot, lead):
            for b in range(B):
                k = slot - OFFSET * b + lead
                if 0 <= k < UNITS:
                    return b * PAIRS + k // NU, k % NU
            return None

        KEY_BANKS = [7, 3] * (NC // 4) + [3, 0] * (NC // 4)
        xb_cT = [[at(f"xb_cT{b}{g}", k * KB, [P, 4, P]) for g, k in enumerate(ks)] for b, ks in enumerate(((112, 114, 116, 118), (40, 44, 46, 133)))]
        xb_kn = [at("xb_kn_even", 0, [P, NC, 2, W], F32R), at("xb_kn_odd", 141 * KB, [P, NC, 2, W], F32R)]
        xb_k = at("xb_k", 64 * KB, [P, NC, H, HD])
        VW = HD + 1
        xb_v = at("xb_v", 80 * KB, [P, NC, HD + H * VW])
        xb_p = at("xb_p", 126 * KB, [P, 2, 4, S])
        xb_qn = at("xb_qn", 48 * KB, [P, H, W], F32R)
        xb_qT1 = at("xb_qT1", 52 * KB, [P, PAIRS, S], F32R)
        xb_qT2 = at("xb_qT2", 130 * KB, [P, 2, 2 * S], F32R)
        xb_kt = at("xb_kt", 56 * KB, [P, NC, 2, HD])
        xb_oh = at("xb_oh", 126 * KB, [P, 4 * S])
        xb_kT = at("xb_kT", 152 * KB, [P, 2, NC, P], F32R)
        xb_wkv = at("xb_wkv", 36 * KB, [P, 2 * D])
        xb_bkv_split = at("xb_bkv_split", 32 * KB, [1, 2, 2 * D], F32R)
        xb_bkv = at("xb_bkv", 38 * KB, [P, 2 * D])
        xb_wq = at("xb_wq", 40 * KB, [P, KC, D])
        xb_wo = at("xb_wo", 42 * KB, [P, KC, D])
        xb_wd = at("xb_wd", 44 * KB, [P, 2 * D])
        xb_bd = at("xb_bd", 46 * KB, [P, 2 * D])
        xb_bq = at("xb_bq", 30 * KB, [P, D])
        xb_q = at("xb_q", 133 * KB, [P, B, D])
        xb_qk = at("xb_qk", 135 * KB, [P, B, D])
        xb_t = at("xb_t", 137 * KB, [P, B, D])
        xb_qfT = at("xb_qfT", 139 * KB, [P, KC, B * S])
        xb_kd = k_stats[:, :, :, :].rearrange("p b n h -> p b (n h)")
        xb_kdm = [xn[:, :, :].rearrange("p b d -> p (b d)"), xnT[:, :, :].rearrange("p k s -> p (k s)")]
        xb_kdT = at("xb_kdT", 149 * KB, [P, B, KC, P])
        xb_wo_row = at("xb_wo_row", 151 * KB, [1, D])
        xb_yd = sb("xb_yd", [DCA, B, C])
        xb_ydT = sb("xb_ydT", [P, B, 8, DCA])
        xb_pd = at("xb_pd", 58 * KB, [P, B, D])
        xb_pdT = at("xb_pdT", 60 * KB, [P, KC, B * S])
        xb_o = at("xb_o", 62 * KB, [P, B, D])
        eps2 = sb("eps2", [P, 1])
        xb_vec = sb("xb_vec", [P, 6, HD])
        xb_ss = sb("xb_ss", [P, NC, H])
        xb_rk = sb("xb_rk", [P, NC, H])
        xb_s32 = sb("xb_s32", [P, 4, B * H])
        xb_d32 = sb("xb_d32", [P, 4, B * H])
        xb_qb = sb("xb_qb", [P, B * H])
        xb_pm = sb("xb_pm", [P, 2, 8])
        xb_m = sb("xb_m", [P, 2, 2])
        xb_den = sb("xb_den", [P, B, H])

        sb_w = at("sb_w", 70 * KB, [P, KC, 3 * D])
        sb_wo = at("sb_wo", 76 * KB, [P, KC, D])
        sb_g = at("sb_g", 78 * KB, [P, 2, D])
        sb_h = at("sb_h", 136 * KB, [P, B, D])
        sb_hT = at("sb_hT", 138 * KB, [P, KC, B * S])
        sb_qT = at("sb_qT", 140 * KB, [P, KC, B * S])
        sb_kT = at("sb_kT", 142 * KB, [P, KC, B * S])
        sb_v = at("sb_v", 144 * KB, [P, B, D])
        sb_s = at("sb_s", 146 * KB, [P, B, S])
        sb_pT = at("sb_pT", 147 * KB, [P, B, S])
        sb_oT = at("sb_oT", 148 * KB, [P, KC, B * S])
        causal2 = at("causal2", 150 * KB, [P, S])
        sb_mv = sb("sb_mv", [P, B, 2])
        sb_rstd = sb("sb_rstd", [P, B])
        sb_m = sb("sb_m", [P, 3, B])
        E = a["L1_ffn_router_w"].shape[0]
        TOP = 4
        EI = a["L1_ffn_gate_proj"].shape[2]
        IC = 2
        IP = EI // IC
        mo_gate = at("mo_gate", 8 * KB, [P, E, KC, EI])
        mo_up = at("mo_up", 98 * KB, [P, E, KC, EI])
        mo_down = at("mo_down", 36 * KB, [IP, E, IC, D])
        mo_r = at("mo_r", 126 * KB, [E, D])
        mo_rT = at("mo_rT", 127 * KB, [P, KC, E])
        mo_bias = at("mo_bias", 128 * KB, [P, E])
        mo_s = at("mo_s", 129 * KB, [P, B, E])
        mo_gt = at("mo_gt", 130 * KB, [P, B, E, E])
        mo_eq = at("mo_eq", 132 * KB, [P, B, E, E])
        mo_rank = at("mo_rank", 134 * KB, [P, B, E])
        mo_first = at("mo_first", 135 * KB, [P, E, E])
        mo_m = sb("mo_m", [P, 3, B])
        mo_sg = at("mo_sg", 136 * KB, [IP, 2, IC, B * S])
        mo_a = at("mo_a", 140 * KB, [IP, 2, IC, B * S])
        mo_x_hi = at("mo_x_hi", 163 * KB, [P, KC, B * S], F32R)
        mo_x_lo = at("mo_x_lo", 165 * KB, [P, KC, B * S], F32R)
        mo_w_hi = at("mo_w_hi", 80 * KB, [P, 3, 2, KC, EI], F32R)
        mo_w_lo = at("mo_w_lo", 152 * KB, [P, 3, 2, KC, EI], F32R)
        mo_a_hi = at("mo_a_hi", 0 * KB, [IP, 3, IC, B * S], F32R)
        mo_a_lo = at("mo_a_lo", 144 * KB, [IP, 3, IC, B * S], F32R)
        mo_d_hi = at("mo_d_hi", 91 * KB, [IP, 2, IC, D], F32R)
        mo_d_lo = [at(f"mo_d_lo{k}", o * KB, [IP, IC, D], F32R) for k, o in enumerate((6, 150))]
        Y_BANKS = (0, 7, 1, 2)

        semaphores = {
            "x_loaded": "DMA: x",
            "ctx_loaded": "DMA: the first sequence's context",
            "ctx1_loaded": "DMA: the second sequence's context",
            "wk_loaded": "DMA: Wk",
            "wq_loaded": "DMA: Wq",
            "wv_loaded": "DMA: Wv",
            "wo_loaded": "DMA: Wo",
            "gains_loaded": "DMA: the gains of q and k",
            "out_done": "DMA: the output is in DRAM",
            "const_made": "Pool: constants",
            "ident_ready": "Pool: the identity",
            "pool_chain": "Pool: its own last result",
            "dve_chain": "DVE: its own last result",
            "ln_var": "DVE: a sequence's mean and variance",
            "ln_rstd": "Pool: 1/deviation of the layernorm",
            "xn_ready": "DVE: a sequence normalised",
            "xT_psum": "TensorE: the normalised stream transposed, in bank 0",
            "xnT_ready": "ACT: it in SBUF",
            "x_updated": "DVE: a block added to a sequence of the stream",
            "y_psum": "TensorE: what a block adds to a sequence",
            "ctxT_psum": "TensorE: four context chunks transposed",
            "ctxT_hi_done": "ACT: their high part",
            "ctxT_lo_done": "DVE: their low part, the bank is read",
            "wk_split": "DVE: Wk in high and low parts",
            "wkT_psum": "TensorE: four heads of Wk transposed",
            "wkT_done": "ACT: them in SBUF",
            "q_psum": "TensorE: a group of q",
            "q_squared": "ACT: its squares",
            "q_ss_done": "DVE: their sums, q_sq is read",
            "q_rstd_done": "Pool: 1/RMS of a group of q",
            "qn_done": "DVE: the group over its RMS, the bank is read",
            "qT_psum": "TensorE: two heads of q transposed",
            "qT_done": "ACT: them in SBUF with the gains",
            "gains_done": "DVE: the gains' product, their largest, the shift of the scores",
            "q3_psum": "TensorE: two heads of q3",
            "q3_hi_done": "ACT: their high part",
            "q3_lo_done": "DVE: their low part, the bank is read",
            "k_psum": "TensorE: a group of k",
            "k_squared": "ACT: its squares, the bank is read",
            "k_ss_done": "DVE: their sums, half of sq is read",
            "k_rstd_done": "Pool: 1/RMS of a sequence's k",
            "s_psum": "TensorE: a step's scores",
            "s_scaled": "DVE: them times k's 1/RMS, the banks are read",
            "p_done": "ACT: their exponentials, s_sb is read",
            "pv_chunk": "TensorE: a step's sums, p_sb is read",
            "o_done": "DVE: a group of heads divided by its sums, the banks are read",
            "oT_psum": "TensorE: two heads transposed",
            "oT_done": "ACT: them in SBUF",
            "aT_psum": "TensorE: two heads' values",
            "aT_done": "ACT: them in SBUF",
            "sa_w_loaded": "DMA: the self attention's weights",
            "mask_ready": "Pool: the masks",
            "sa_q_psum": "TensorE: q and k, transposed",
            "sa_qkT": "ACT: a part of them with its bias",
            "sa_v_psum": "TensorE: v",
            "sa_v_done": "ACT and DVE: v and its ones",
            "sa_km_done": "DVE: k with the other heads masked out",
            "sa_s_psum": "TensorE: eight heads' scores, the masked k is read",
            "sa_s_masked": "DVE: them with the causal mask, the banks are read",
            "sa_centred": "DVE: a sequence's scores less their maxima",
            "sa_p_done": "ACT: its exponentials",
            "sa_pT_psum": "TensorE: four heads of them transposed",
            "sa_pT_done": "ACT: those in SBUF, the bank is read",
            "sa_o_psum": "TensorE: a sequence's sums",
            "sa_o_done": "DVE: them divided",
            "sa_oT_psum": "TensorE: them transposed",
            "sa_oT_done": "ACT: those in SBUF",
            "ffw_loaded": "DMA: the feed forward's weights",
            "ffb_loaded": "DMA: its biases and gains",
            "wabs_done": "ACT: a weight matrix's sizes summed in each partition",
            "small_psum": "TensorE: the gains in a row, their largest everywhere, the mean sizes everywhere",
            "wq_quant": "DVE: the scales, then each third of a matrix's rounding",
            "wqT_psum": "TensorE: an eighth of the ternary weights transposed",
            "wqT_done": "ACT: it in bf16, the bank is read",
            "ff_ss_done": "DVE, then ACT: a sequence's squares summed",
            "ff_r_done": "Pool: 1/RMS of what is quantised",
            "ff_q_done": "DVE: a sequence quantised",
            "ff_qT_psum": "TensorE: a part of it transposed",
            "ff_qT_done": "ACT: it in bf16",
            "ff_h_psum": "TensorE: a sequence's inner products",
            "ff_h_done": "DVE: them scaled, with their bias",
            "ff_silu": "ACT: their silu",
            "ff_gelu": "ACT: their gelu",
            "ff_lnvar": "DVE: mean and variance of the inner layernorm",
            "ff_lnrstd": "Pool: its 1/deviation",
            "ff_normed": "DVE: a sequence through the inner layernorm",
            "xb_w_loaded": "DMA: the second cross attention's other weights",
            "xb_wkv_loaded": "DMA: its weights and biases of k and v",
            "xb_centred": "DVE: a weight or bias less its mean over a head",
            "xb_cT_psum": "TensorE: four context chunks transposed",
            "xb_cT_done": "ACT: them in SBUF, the bank is read",
            "xb_kv_psum": "TensorE: a chunk's k and v",
            "xb_kv_done": "ACT or DVE: it in SBUF, the bank is read",
            "xb_k_sq": "ACT: two chunks' squares of k",
            "xb_k_ss": "DVE: their sums, half of sq is read",
            "xb_k_sqrt": "ACT: k's deviations",
            "xb_kr_done": "DVE: their reciprocals",
            "xb_kt_done": "DVE: a pair's k over its deviation",
            "xb_khi": "ACT: its high part, twice",
            "xb_klo": "DVE: its low part",
            "xb_kT_psum": "TensorE: a quarter of the pair's stacked k transposed",
            "xb_kT_done": "ACT: it in SBUF, the bank is read",
            "xb_q_psum": "TensorE: q of both sequences",
            "xb_q_ss": "DVE: a sequence's squares of q summed",
            "xb_q_sqrt": "ACT (first) and Pool (second sequence): from them the deviations",
            "xb_q_done": "DVE: a sequence's q normalised",
            "xb_qn_done": "DVE: its stacked q",
            "xb_q1_psum": "TensorE: four pairs of it transposed",
            "xb_q1_done": "ACT: them in SBUF, the bank is read",
            "xb_row_done": "DVE: a pair's maxima taken off its stacked q",
            "xb_q2_psum": "TensorE: the pair's q transposed again",
            "xb_q2_done": "ACT: it in SBUF, bank 0 is read",
            "xb_m_psum": "TensorE: scores for a maximum",
            "xb_m_done": "DVE: the maximum, the bank is read",
            "xb_s_psum": "TensorE: a unit's scores",
            "xb_p_done": "ACT: their exponentials, the bank is read",
            "xb_pv_done": "TensorE: the unit's sums, xb_p is read",
            "xb_const": "Pool: the constants in the stacked operands and v",
            "xb_oh_done": "DVE: a sequence's sums in SBUF, bank 7 is read",
            "xb_ohT_psum": "TensorE: them transposed",
            "xb_o_done": "DVE: them divided, the last rows' added, bank 5 is read",
            "xb_oT_psum": "TensorE: a sequence's heads transposed",
            "xb_oT_done": "ACT: them in SBUF",
            "xb_last_psum": "TensorE: the next step for the last rows, in bank 3",
            "xb_last_act": "ACT: its next result for them",
            "xb_kd_read": "DVE: their k and v with bias, bank 3 is read",
            "xb_kd_ss": "DVE: their squares of k summed",
            "xb_kd_rstd": "Pool: 1/deviation of their k",
            "xb_kdm_done": "DVE: their k and v masked head by head",
            "xb_sd_centred": "DVE: their scores less the maxima, bank 3 is read",
            "xb_pd_done": "DVE: their probabilities",
            "xb_od_done": "DVE: their part of the heads, bank 3 is read",
            "sb_w_loaded": "DMA: the single-headed attention's weights",
            "sb_masks": "Pool: its mask and the order of the experts",
            "sb_var": "DVE: mean and variance of its layernorm",
            "sb_rstd_done": "Pool: its 1/deviation",
            "sb_psum": "TensorE: its next product",
            "sb_act": "ACT: its next result",
            "sb_dve": "DVE: its next result",
            "mo_w_loaded": "DMA: the experts' gates and ups",
            "mo_down_loaded": "DMA: the experts' downs",
            "mo_r_loaded": "DMA: the router",
            "mo_psum": "TensorE: the router transposed, then its scores",
            "mo_act": "ACT: the router's weights, then its exponentials",
            "mo_centred": "DVE: the router's scores less their maxima",
            "mo_x_split": "ACT, DVE: high and low part of the stream",
            "mo_w_split": "ACT: high part of an expert's gate, then up",
            "mo_w_low": "DVE: their low parts",
            "mo_d_split": "ACT: high part of an expert's down",
            "mo_d_low": "DVE: its low part",
            "mo_gu_psum": "TensorE: an expert's gate and up",
            "mo_silu": "ACT: silu of the gate",
            "mo_a_done": "DVE: times up, the banks are read",
            "mo_a_hi_done": "ACT: its high part",
            "mo_a_lo_done": "DVE: its low part",
            "mo_y_psum": "TensorE: an expert's output",
            "mo_y_done": "DVE: a sequence of it added, weighted",
        }
        M = {name: sem(name) for name in semaphores}

        block = ctx.enter_context(nc.Block())

        @block.sync
        def _(sp):
            sp.dma_start(x_sb[:, :, :], a["x"].rearrange("b s d -> s b d")).then_inc(M["x_loaded"], 16)
            def load_context(b):
                sp.dma_start(ctx_nat[:, b * NC:(b + 1) * NC, 0:C],
                             a["ctx_1024"][b].rearrange("(p c) d -> p c d", c=NC)).then_inc(M["ctx_loaded"] if b == 0 else M["ctx1_loaded"], 16)

            sp.dma_start(wk[:, :], a["L0_xattn_Wk"]).then_inc(M["wk_loaded"], 16)
            load_context(0)
            sp.dma_start(wq[:, :, :], a["L0_xattn_Wq"].rearrange("(k p) n -> p k n", p=P)).then_inc(M["wq_loaded"], 16)
            load_context(1)
            sp.dma_start(gains[:, 0:1], a["L0_xattn_gq"].rearrange("(p o) -> p o", o=1)).then_inc(M["gains_loaded"], 16)
            sp.dma_start(gains[:, 1:2], a["L0_xattn_gk"].rearrange("(p o) -> p o", o=1)).then_inc(M["gains_loaded"], 16)
            sp.dma_start(wv[:, :, :], a["L0_xattn_Wv"].rearrange("p (h d) -> p h d", h=H)).then_inc(M["wv_loaded"], 16)
            sp.dma_start(wo[:, :, :], a["L0_xattn_Wo"].rearrange("(h p) n -> p h n", p=P)).then_inc(M["wo_loaded"], 16)
            sp.wait_ge(M["q_psum"], B * NG)
            sp.dma_start(w1[:, :, :], a["L0_ffn_w1"].rearrange("(o p) d -> p o d", p=P)).then_inc(M["ffw_loaded"], 16)
            sp.dma_start(w2[:, :, :], a["L0_ffn_w2"].rearrange("(o p) d -> p o d", p=P)).then_inc(M["ffw_loaded"], 16)
            sp.wait_ge(M["pv_chunk"], NG * NC // 2)
            sp.dma_start(w_in[:, :, :], a["L0_attn_w_in"].rearrange("(k p) n -> p k n", p=P)).then_inc(M["sa_w_loaded"], 16)
            sp.dma_start(w_out[:, :, :], a["L0_attn_w_out"].rearrange("(k p) n -> p k n", p=P)).then_inc(M["sa_w_loaded"], 16)
            for j in range(2 * KC):
                sp.dma_start(bqk[:, j:j + 1], a["L0_attn_b_in"][j * P:(j + 1) * P].rearrange("(p o) -> p o", o=1)).then_inc(M["sa_w_loaded"], 16)
            sp.dma_start(b_in_row[:, :], a["L0_attn_b_in"].rearrange("(o n) -> o n", o=1)).then_inc(M["sa_w_loaded"], 16)
            sp.dma_start(b_out_row[:, :], a["L0_attn_b_out"].rearrange("(o n) -> o n", o=1)).then_inc(M["sa_w_loaded"], 16)
            sp.wait_ge(M["pv_chunk"], B * NG * NC // 2)
            for t, name in ((b1_all, "L0_ffn_b1"), (lng_all, "L0_ffn_ln_g"), (lnb_all, "L0_ffn_ln_b"), (b2_all, "L0_ffn_b2")):
                sp.dma_start(t[:, :], a[name].rearrange("(o n) -> o n", o=1).to_broadcast([P, a[name].shape[0]])).then_inc(M["ffb_loaded"], 16)
            wkv = M["xb_wkv_loaded"]
            sp.dma_start(xb_wkv[:, 0:D], a["L1_xattn_Wk"]).then_inc(wkv, 16)
            sp.dma_start(xb_wkv[:, D:2 * D], a["L1_xattn_Wv"]).then_inc(wkv, 16)
            everywhere = ((xb_bkv[:, 0:D], "L1_xattn_bk"), (xb_bkv[:, D:2 * D], "L1_xattn_bv"))
            for dst, name in everywhere:
                sp.dma_start(dst, a[name].rearrange("(o n) -> o n", o=1).to_broadcast([P, D])).then_inc(wkv, 16)
            xw = M["xb_w_loaded"]
            sp.wait_ge(M["y_psum"], B)
            sp.dma_start(xb_wq[:, :, :], a["L1_xattn_Wq"].rearrange("(k p) n -> p k n", p=P)).then_inc(xw, 16)
            sp.dma_start(xb_wo[:, :, :], a["L1_xattn_Wo"].rearrange("(k p) n -> p k n", p=P)).then_inc(xw, 16)
            sp.dma_start(xb_wd[:, :], a["L1_xattn_Wkv_dca"]).then_inc(xw, 16)
            sp.dma_start(xb_bd[:, :], a["L1_xattn_bkv_dca"].rearrange("(o n) -> o n", o=1).to_broadcast([P, 2 * D])).then_inc(xw, 16)
            sp.dma_start(xb_bq[:, :], a["L1_xattn_bq"].rearrange("(o n) -> o n", o=1).to_broadcast([P, D])).then_inc(xw, 16)
            sp.dma_start(xb_wo_row[:, :], a["L1_xattn_bo"].rearrange("(o n) -> o n", o=1)).then_inc(xw, 16)
            sp.dma_start(xb_yd[:, :, :], a["ctx_1024"][:, KV - DCA:KV, :].rearrange("b k c -> k b c")).then_inc(xw, 16)
            for j, name in enumerate(("qn_w", "qn_b", "kn_w", "kn_b", "kn_dca_w", "kn_dca_b")):
                sp.dma_start(xb_vec[:, j, :], a["L1_xattn_" + name].rearrange("(o n) -> o n", o=1).to_broadcast([P, HD])).then_inc(xw, 16)
            sp.wait_ge(M["x_updated"], 3 * B)
            sp.wait_ge(M["xb_q_done"], 1)
            for t, name in ((mo_gate, "L1_ffn_gate_proj"), (mo_up, "L1_ffn_up_proj")):
                for e in range(0, E, 4):
                    for kc in range(KC):
                        sp.dma_start(t[:, e:e + 4, kc, :], a[name][e:e + 4, kc * P:(kc + 1) * P, :].rearrange("e p i -> p e i")).then_inc(M["mo_w_loaded"], 16)
            sp.wait_ge(M["xb_kt_done"], B * PAIRS)
            lw = M["sb_w_loaded"]
            sp.dma_start(sb_w[:, :, :], a["L1_attn_qkv"].rearrange("(k p) n -> p k n", p=P)).then_inc(lw, 16)
            sp.dma_start(sb_wo[:, :, :], a["L1_attn_o_proj"].rearrange("(k p) n -> p k n", p=P)).then_inc(lw, 16)
            sp.dma_start(sb_g[:, 0, :], a["L1_attn_gamma"].rearrange("(o n) -> o n", o=1).to_broadcast([P, D])).then_inc(lw, 16)
            sp.dma_start(sb_g[:, 1, :], a["L1_attn_beta"].rearrange("(o n) -> o n", o=1).to_broadcast([P, D])).then_inc(lw, 16)
            sp.wait_ge(M["xb_ohT_psum"], B)
            sp.dma_start(mo_r[:, :], a["L1_ffn_router_w"]).then_inc(M["mo_r_loaded"], 16)
            sp.dma_start(mo_bias[:, :], a["L1_ffn_expert_bias"].rearrange("(o n) -> o n", o=1).to_broadcast([P, E])).then_inc(M["mo_r_loaded"], 16)
            sp.wait_ge(M["y_psum"], 4 * B)
            for e in range(0, E, 4):
                for ic in range(IC):
                    sp.dma_start(mo_down[:, e:e + 4, ic, :], a["L1_ffn_down_proj"][e:e + 4, ic * IP:(ic + 1) * IP, :].rearrange("e p n -> p e n")).then_inc(M["mo_down_loaded"], 16)
            sp.wait_ge(M["x_updated"], B * 6)
            sp.dma_start(out.rearrange("b s d -> s b d"), x_sb[:, :, :]).then_inc(M["out_done"], 16)
            sp.wait_ge(M["out_done"], 16)

        @block.gpsimd
        def _(pool):
            links = [0]

            def chained(ins):
                links[0] += 1
                ins.then_inc(M["pool_chain"], 1)
                pool.wait_ge(M["pool_chain"], links[0])

            pool.memset(neg_half[:, :], -0.5).then_inc(M["const_made"], 1)
            pool.memset(ones[:, :], 1.0).then_inc(M["const_made"], 1)
            pool.memset(ctx_nat[:, :, C:C + 2], 1.0).then_inc(M["const_made"], 1)
            pool.memset(eps2[:, :], EPS2).then_inc(M["const_made"], 1)
            chained(pool.memset(ident[:, :], 0.0))
            pool.affine_select(out=ident[:, :], in_=ident[:, :], compare_op=ALU.not_equal, fill=1.0,
                               base=0, pattern=[[-1, P]], channel_multiplier=1).then_inc(M["ident_ready"], 1)
            pool.wait_ge(M["const_made"], 3)

            def ln_rstd(k):
                pool.wait_ge(M["ln_var"], B * (k + 1))
                chained(pool.tensor_scalar(veps[:, :], meanvar[:, :, 1], EPS, None, ALU.add))
                pool.tensor_tensor(rstd[:, :], veps[:, :], neg_half[:, 0:B], ALU.pow).then_inc(M["ln_rstd"], 1)

            ln_rstd(0)
            for b in range(B):
                for g in range(NG):
                    pool.wait_ge(M["q_ss_done"], NG * b + g + 1)
                    r = slice(G * g, G * g + G)
                    chained(pool.tensor_scalar(q_ss[:, b, r], q_ss[:, b, r], 1.0 / HD0, EPS, ALU.mult, ALU.add))
                    pool.tensor_tensor(q_rstd[:, b, r], q_ss[:, b, r], neg_half[:, 0:G], ALU.pow).then_inc(M["q_rstd_done"], 1)
            for b in range(B):
                pool.wait_ge(M["k_ss_done"], NG * NC * (b + 1))
                r = slice(b * NC, (b + 1) * NC)
                chained(pool.tensor_scalar(k_ss[:, r, :], k_ss[:, r, :], 1.0 / HD0, EPS, ALU.mult, ALU.add))
                pool.tensor_tensor(k_rstd[:, r, :], k_ss[:, r, :],
                                   neg_half[:, 0:1].unsqueeze(1).to_broadcast([P, NC, H]), ALU.pow).then_inc(M["k_rstd_done"], 1)

            pool.wait_ge(M["pv_chunk"], B * NG * NC // 2)
            chained(pool.memset(causal[:, :], 0.0))
            chained(pool.affine_select(out=causal[:, :], in_=causal[:, :], compare_op=ALU.is_ge, fill=-1e30,
                                       base=0, pattern=[[-1, S]], channel_multiplier=1))
            chained(pool.memset(head_mask[:, :], 1.0))
            chained(pool.affine_select(out=head_mask[:, :], in_=head_mask[:, :], compare_op=ALU.is_ge, fill=0.0,
                                       base=0, pattern=[[-HD, 8]], channel_multiplier=1))
            pool.affine_select(out=head_mask[:, :], in_=head_mask[:, :], compare_op=ALU.is_ge, fill=0.0,
                               base=HD - 1, pattern=[[HD, 8]], channel_multiplier=-1).then_inc(M["mask_ready"], 1)
            ln_rstd(1)
            pool.wait_ge(M["wqT_psum"], 8)
            pool.memset(xb_v[:, :, 0:HD - 1], 0.0).then_inc(M["xb_const"], 1)
            pool.memset(xb_v[:, :, HD - 1:HD - 1 + H * VW].rearrange("p c (h d) -> p c h d", d=VW)[:, :, :, HD:VW], 1.0).then_inc(M["xb_const"], 1)
            ln_rstd(2)

            def rms(i, n):
                pool.wait_ge(M["ff_ss_done"], B * (i + 1))
                chained(pool.tensor_scalar(ff_ss[:, i, :], ff_ss[:, i, :], 1.0 / n, EPS, ALU.mult, ALU.add))
                pool.tensor_tensor(ff_r[:, i, :], ff_ss[:, i, :], neg_half[:, 0:B], ALU.pow).then_inc(M["ff_r_done"], 1)

            rms(0, D)
            pool.wait_ge(M["ff_lnvar"], B)
            chained(pool.tensor_scalar(ff_rstd[:, :], ff_mv[:, :, 1], EPS, None, ALU.add))
            pool.tensor_tensor(ff_rstd[:, :], ff_rstd[:, :], neg_half[:, 0:B], ALU.pow).then_inc(M["ff_lnrstd"], 1)
            rms(1, FI)
            pool.wait_ge(M["y_psum"], 3 * B)
            for kn in xb_kn:
                pool.memset(kn[:, :, :, 3 * HD:3 * HD + 2].bitcast(F32), 1.0).then_inc(M["xb_const"], 1)
                pool.memset(kn[:, :, :, 3 * HD + 2:W].bitcast(F32), 0.0).then_inc(M["xb_const"], 1)
            pool.memset(xb_qn[:, :, 3 * HD + 2:W].bitcast(F32), 0.0).then_inc(M["xb_const"], 1)
            pool.memset(xb_qT2[:, :, :].bitcast(F32), 0.0).then_inc(M["xb_const"], 1)
            ln_rstd(3)
            pool.wait_ge(M["xb_q_ss"], 2)
            chained(pool.tensor_scalar(xb_s32[:, 1, H:2 * H], xb_s32[:, 1, H:2 * H], 1.0 / HD, EPS2, ALU.mult, ALU.add))
            pool.tensor_tensor(xb_s32[:, 3, H:2 * H], xb_s32[:, 1, H:2 * H], neg_half[:, 0:H], ALU.pow).then_inc(M["xb_q_sqrt"], 1)
            pool.wait_ge(M["xb_kd_ss"], 1)
            chained(pool.tensor_scalar(xb_d32[:, 1, :], xb_d32[:, 1, :], 1.0 / HD, EPS2, ALU.mult, ALU.add))
            pool.tensor_tensor(xb_d32[:, 3, :], xb_d32[:, 1, :], neg_half[:, 0:B * H], ALU.pow).then_inc(M["xb_kd_rstd"], 1)
            pool.wait_ge(M["xb_pv_done"], B * UNITS)
            chained(pool.memset(causal2[:, :], 0.0))
            pool.affine_select(out=causal2[:, :], in_=causal2[:, :], compare_op=ALU.is_ge, fill=-1e30,
                               base=0, pattern=[[-1, S]], channel_multiplier=1).then_inc(M["sb_masks"], 1)
            chained(pool.memset(mo_first[:, :, :], 1.0))
            pool.affine_select(out=mo_first[:, :, :], in_=mo_first[:, :, :], compare_op=ALU.is_gt, fill=0.0,
                               base=0, pattern=[[1, E], [-1, E]], channel_multiplier=0).then_inc(M["sb_masks"], 1)
            ln_rstd(4)
            pool.wait_ge(M["sb_var"], B)
            chained(pool.tensor_scalar(sb_rstd[:, :], sb_mv[:, :, 1], EPS, None, ALU.add))
            pool.tensor_tensor(sb_rstd[:, :], sb_rstd[:, :], neg_half[:, 0:B], ALU.pow).then_inc(M["sb_rstd_done"], 1)
            ln_rstd(5)
        @block.scalar
        def _(act):
            def xnT_copy(k):
                act.wait_ge(M["xT_psum"], k + 1)
                act.activation(xnT[:, :, :], ps[:, 0, :], ACT.Copy).then_inc(M["xnT_ready"], 1)

            xnT_copy(0)
            def context_high(j):
                act.wait_ge(M["ctxT_psum"], j + 1)
                act.activation(ctxT_hi[:, 4 * j:4 * j + 4, :], ps[:, 4 + j % 4, :], ACT.Copy).then_inc(M["ctxT_hi_done"], 1)

            def query_part(c):
                if c < 8:
                    act.wait_ge(M["q_psum"], c + 1)
                    if c >= 2:
                        act.wait_ge(M["q_ss_done"], c - 1)
                    act.activation(q_sq[:, c % 2, :], ps[:, 4 + c % 4, :], ACT.Square).then_inc(M["q_squared"], 1)
                elif c < 12:
                    context_high(c - 4)
                elif c < 14:
                    for j in (2 * (c - 12), 2 * (c - 12) + 1):
                        act.wait_ge(M["wkT_psum"], j + 1)
                        act.activation(wkT[:, 4 * j:4 * j + 4, :], ps[:, 4 + j, :], ACT.Copy).then_inc(M["wkT_done"], 1)
                elif c < 18:
                    if c == 14:
                        act.wait_ge(M["gains_done"], 1)
                    for j in (2 * (c - 14), 2 * (c - 14) + 1):
                        act.wait_ge(M["qT_psum"], j + 1)
                        act.activation(qT[:, 2 * j:2 * j + 2, :], ps[:, 4 + j % 2, :], ACT.Copy, scale=gqk[:, 0:1]).then_inc(M["qT_done"], 1)
                elif c < 26:
                    j = c - 18
                    act.wait_ge(M["q3_psum"], j + 1)
                    if j == 0:
                        act.wait_ge(M["q_ss_done"], B * NG)
                    act.activation(q3_hi[:, :, 2 * j:2 * j + 2, :].rearrange("p b h s -> p h b s"),
                                   ps[:, 6 + j % 2, :].rearrange("p (h b s) -> p h b s", h=2, b=B),
                                   ACT.Copy).then_inc(M["q3_hi_done"], 1)
                elif c < 28:
                    if c == 26:
                        act.wait_ge(M["ffw_loaded"], 32)
                        act.wait_ge(M["qT_psum"], H // 2)
                    act.activation(w_sizes[:, :], (w1, w2)[c - 26][:, :, :].rearrange("p k n -> p (k n)"), ACT.Abs,
                                   accum_out=w_abs[:, c - 26:c - 25]).then_inc(M["wabs_done"], 1)

            for j in range(4):
                context_high(j)
            for c in range(B * NC):
                for g in range(NG):
                    i = c * NG + g
                    act.wait_ge(M["k_psum"], i + 1)
                    if i >= 2:
                        act.wait_ge(M["k_ss_done"], i - 1)
                    act.activation(sq[:, i % 2, :], ps[:, i % 4, :], ACT.Square).then_inc(M["k_squared"], 1)
                query_part(c)
            act.wait_ge(M["gains_done"], 3)
            for i in range(B * NG * NC // 2):
                act.wait_ge(M["s_scaled"], i + 1)
                if i >= 2:
                    act.wait_ge(M["pv_chunk"], i - 1)
                act.activation(p_sb[:, i % 2, :, :], s_sb[:, i % 2, :, :], ACT.Exp, bias=shift[:, 0:1]).then_inc(M["p_done"], 1)
            for j in range(H // 2):
                act.wait_ge(M["oT_psum"], j + 1)
                act.activation(oT[:, 2 * j:2 * j + 2, :], ps[:, j % 2, :], ACT.Copy).then_inc(M["oT_done"], 1)
            for j in range(H // 2):
                act.wait_ge(M["aT_psum"], j + 1)
                act.activation(aT[:, 2 * j:2 * j + 2, :], ps[:, 2 + j % 2, :], ACT.Copy).then_inc(M["aT_done"], 1)
            xnT_copy(1)
            act.wait_ge(M["sa_w_loaded"], 128)
            act.wait_ge(M["sa_q_psum"], 1)
            for j in range(KC):
                act.activation(sa_qT[:, j, :], ps[:, 1, j * B * S:(j + 1) * B * S], ACT.Identity, bias=bqk[:, j:j + 1]).then_inc(M["sa_qkT"], 1)
            for j in range(KC):
                act.activation(sa_kT[:, j, :], ps[:, 2, j * B * S:(j + 1) * B * S], ACT.Identity, bias=bqk[:, KC + j:KC + j + 1]).then_inc(M["sa_qkT"], 1)
            act.wait_ge(M["sa_v_psum"], 1)
            act.activation(sa_v[:, :, :, 0:HD], ps[:, 3, :].rearrange("p (b h d) -> p b h d", b=B, h=H), ACT.Copy).then_inc(M["sa_v_done"], 1)
            def weight_copies(first):
                for i in range(first, first + 4):
                    act.wait_ge(M["wqT_psum"], i + 1)
                    if i < 4:
                        dst = w1qT[:, i // 2, (i % 2) * 512:(i % 2) * 512 + 512]
                    else:
                        dst = w2qT[:, 2 * (i - 4):2 * (i - 4) + 2, :]
                    act.activation(dst, ps[:, (4 + i) % 8, :], ACT.Copy).then_inc(M["wqT_done"], 1)

            def context_copy(b, g):
                act.wait_ge(M["xb_cT_psum"], 4 * b + g + 1)
                bank = 3 if b == 1 else 7 - 4 * (g % 2)
                act.activation(xb_cT[b][g][:, :, :], ps[:, bank, :], ACT.Copy).then_inc(M["xb_cT_done"], 1)

            def key_copies(first, last):
                for c in range(first, last):
                    if c == 0:
                        act.wait_ge(M["y_psum"], B)
                    act.wait_ge(M["xb_kv_psum"], c + 1)
                    kv = ps[:, KEY_BANKS[c], :].rearrange("p (h v d) -> p h v d", h=H, v=2)
                    act.activation(xb_k[:, c, :, :], kv[:, :, 0, :], ACT.Copy)
                    act.activation(v_heads(c), kv[:, :, 1, :], ACT.Copy).then_inc(M["xb_kv_done"], 1)

            def k_square(b, t):
                n = b * (NC // 2) + t
                act.wait_ge(M["xb_kv_done"], b * NC + 2 * t + 2)
                if n >= 2:
                    act.wait_ge(M["xb_k_ss"], n - 1)
                act.activation(sq[:, n % 2, :].rearrange("p (c h d) -> p c h d", c=2, h=H), xb_k[:, 2 * t:2 * t + 2, :, :],
                               ACT.Square).then_inc(M["xb_k_sq"], 1)

            def k_deviation(b):
                act.wait_ge(M["xb_k_ss"], (b + 1) * (NC // 2))
                act.activation(xb_rk[:, :, :], xb_ss[:, :, :], ACT.Sqrt, scale=1.0 / HD, bias=eps2[:, 0:1]).then_inc(M["xb_k_sqrt"], 1)

            for b in range(B):
                weight_copies(4 * b)
                act.wait_ge(M["sa_centred"], b + 1)
                act.activation(sa_s[:, b, :, :], sa_s[:, b, :, :], ACT.Exp, scale=float(HD) ** -0.5).then_inc(M["sa_p_done"], 1)
            for b in range(B):
                for g in range(4):
                    act.wait_ge(M["sa_pT_psum"], b * 4 + g + 1)
                    act.activation(sa_pT[:, b, 4 * g:4 * g + 4, :], ps[:, 4 * (1 - b) + g, :], ACT.Copy).then_inc(M["sa_pT_done"], 1)
            for g in range(4):
                context_copy(0, g)
            key_copies(0, 2)
            for b in range(B):
                act.wait_ge(M["sa_oT_psum"], b + 1)
                act.activation(sa_oT[:, :, b * S:(b + 1) * S], ps[:, 4 * (1 - b) + 1, 0:D].rearrange("p (k s) -> p k s", k=KC),
                               ACT.Copy).then_inc(M["sa_oT_done"], 1)
            key_copies(2, 8)
            k_square(0, 0)
            k_square(0, 1)
            act.wait_ge(M["ff_qT_psum"], 1)
            act.activation(ff_qT1[:, :, :], ps[:, 0, :], ACT.Copy).then_inc(M["ff_qT_done"], 1)
            for b in range(B):
                act.wait_ge(M["ff_h_done"], b + 1)
                act.activation(ff_h2[:, b, :], ff_h[:, b, :], ACT.Silu).then_inc(M["ff_silu"], 1)
            for b in range(B):
                act.wait_ge(M["ff_silu"], b + 1)
                act.activation(ff_h[:, b, :], ff_h2[:, b, :], ACT.Gelu).then_inc(M["ff_gelu"], 1)
            key_copies(8, 13)
            for b in range(B):
                if b == 1:
                    key_copies(13, NC)
                act.wait_ge(M["ff_normed"], b + 1)
                act.activation(ff_sq[:, b, :], ff_h2[:, b, :], ACT.Square, accum_out=ff_ss[:, 1, b:b + 1]).then_inc(M["ff_ss_done"], 1)
            k_square(0, 2)
            k_square(0, 3)
            for b in range(B):
                for g in range(2):
                    act.wait_ge(M["ff_qT_psum"], 2 + 2 * b + g)
                    act.activation(ff_qT2[:, 4 * g:4 * g + 4, b * S:(b + 1) * S], ps[:, 4 + 2 * b + g, :], ACT.Copy).then_inc(M["ff_qT_done"], 1)

            def k_high(n):
                act.wait_ge(M["xb_kt_done"], n + 1)
                if n < 2:
                    act.wait_ge(M["y_psum"], 3 * B)
                if n >= 2:
                    act.wait_ge(M["xb_kT_psum"], 4 * (n - 1))
                src = xb_kt[:, :, :, :].rearrange("p c h d -> p (c h) d").unsqueeze(2).to_broadcast([P, 2 * NC, 2, HD])
                dst = xb_kn[n % 2][:, :, :, 0:4 * HD].rearrange("p c h (r t d) -> p (c h) r t d", r=2, t=2)[:, :, :, 0, :]
                act.activation(dst, src, ACT.Copy).then_inc(M["xb_khi"], 1)

            for t in range(4, NC // 2):
                k_square(0, t)
            k_deviation(0)
            xnT_copy(2)
            k_high(0)
            act.wait_ge(M["xb_q_ss"], 1)
            act.activation(xb_s32[:, 2, 0:H], xb_s32[:, 1, 0:H], ACT.Sqrt, scale=1.0 / HD, bias=eps2[:, 0:1]).then_inc(M["xb_q_sqrt"], 1)

            def last_rows(stage):
                if stage == 0:
                    act.wait_ge(M["xb_last_psum"], 1)
                    act.activation(xb_ydT[:, :, :, :], ps[:, 3, 0:B * DCA].rearrange("p (b k) -> p b k", b=B).unsqueeze(2).to_broadcast([P, B, 8, DCA]),
                                   ACT.Copy).then_inc(M["xb_last_act"], 1)
                elif stage == 6:
                    act.wait_ge(M["xb_last_psum"], 4)
                    act.activation(xb_kdT[:, :, :, :], ps[:, 3, :], ACT.Copy).then_inc(M["xb_last_act"], 1)
                elif stage == 7:
                    act.wait_ge(M["xb_last_psum"], 5)
                    act.activation(xb_qfT[:, :, :], ps[:, 3, :], ACT.Copy).then_inc(M["xb_last_act"], 1)
                elif stage == 9:
                    act.wait_ge(M["xb_sd_centred"], 1)
                    act.activation(xb_pd[:, :, :], xb_pd[:, :, :], ACT.Exp, scale=SC).then_inc(M["xb_last_act"], 1)
                elif stage == 11:
                    act.wait_ge(M["xb_last_psum"], 7)
                    act.activation(xb_pdT[:, :, :], ps[:, 3, :], ACT.Copy).then_inc(M["xb_last_act"], 1)

            def k_copy(n, g):
                act.wait_ge(M["xb_kT_psum"], 4 * n + g + 1)
                act.activation(xb_kT[:, n % 2, 4 * g:4 * g + 4, :], ps[:, 4 * (g % 2), :], ACT.Copy).then_inc(M["xb_kT_done"], 1)

            def q_copy(n):
                act.wait_ge(M["xb_q2_psum"], n + 1)
                if n == 0:
                    act.wait_ge(M["xb_const"], 8)
                act.activation(xb_qT2[0:W, n % 2, 0:S], ps[0:W, 0, 0:S], ACT.Copy)
                act.activation(xb_qT2[W:2 * W, n % 2, S:2 * S], ps[W:2 * W, 0, 0:S], ACT.Copy).then_inc(M["xb_q2_done"], 1)

            def probabilities(n, u):
                m = n * NU + u
                act.wait_ge(M["xb_s_psum"], m + 1)
                if m >= 2:
                    act.wait_ge(M["xb_pv_done"], m - 1)
                act.activation(xb_p[:, m % 2, :, :], ps[:, 5 + m % 2, :].rearrange("p (c s) -> p c s", c=4),
                               ACT.Exp).then_inc(M["xb_p_done"], 1)

            def queries_1(b):
                for g in range(2):
                    act.wait_ge(M["xb_q1_psum"], 2 * b + g + 1)
                    act.activation(xb_qT1[:, 4 * g:4 * g + 4, :], ps[:, 1 + g, :], ACT.Copy).then_inc(M["xb_q1_done"], 1)

            queries_1(0)
            for slot in range(-6, B * OFFSET + 4):
                if unit_at(slot, -8):
                    probabilities(*unit_at(slot, -8))
                if slot % 2 == 0 and unit_at(slot, 6):
                    n, u = unit_at(slot, 6)
                    k_copy(n, u // 2)
                n, u = unit_at(slot, 13) or (0, 0)
                if u == 0 and n % PAIRS > 0:
                    k_high(n)
                if slot % 8 == 5 and unit_at(slot, 0):
                    q_copy(unit_at(slot, 0)[0])
                if slot in LAST_SLOTS:
                    last_rows(LAST_SLOTS[slot])
                if 41 <= slot < 45:
                    context_copy(1, slot - 41)
                if 48 <= slot < 64 and slot % 2 == 0:
                    k_square(1, (slot - 48) // 2)
                if slot == 63:
                    k_deviation(1)
                if slot == 65:
                    k_high(PAIRS)
                if slot == 66:
                    queries_1(1)
            for b in range(B):
                act.wait_ge(M["xb_oT_psum"], b + 1)
                act.activation(xb_qfT[:, :, b * S:(b + 1) * S],
                               ps[:, 1 + b, 0:D].rearrange("p (k s) -> p k s", k=KC), ACT.Copy).then_inc(M["xb_oT_done"], 1)

            act.wait_ge(M["sb_psum"], 1)
            act.activation(sb_hT[:, :, :], ps[:, 0, :], ACT.Copy).then_inc(M["sb_act"], 1)
            act.wait_ge(M["sb_psum"], 2)
            act.activation(sb_qT[:, :, :], ps[:, 1, :], ACT.Copy).then_inc(M["sb_act"], 1)
            act.activation(sb_kT[:, :, :], ps[:, 2, :], ACT.Copy).then_inc(M["sb_act"], 1)
            act.wait_ge(M["sb_psum"], 3)
            act.activation(sb_v[:, :, :], ps[:, 3, :], ACT.Copy).then_inc(M["sb_act"], 1)

            def weights_high(e):
                if e == 0:
                    act.wait_ge(M["mo_w_loaded"], 16 * 16)
                if e >= 3:
                    act.wait_ge(M["mo_gu_psum"], e - 2)
                act.activation(mo_w_hi[:, e % 3, 0, :, :], mo_gate[:, e, :, :], ACT.Copy).then_inc(M["mo_w_split"], 1)
                act.activation(mo_w_hi[:, e % 3, 1, :, :], mo_up[:, e, :, :], ACT.Copy).then_inc(M["mo_w_split"], 1)

            act.wait_ge(M["sb_dve"], 2)
            act.activation(sb_s[:, :, :], sb_s[:, :, :], ACT.Exp, scale=float(D) ** -0.5).then_inc(M["sb_act"], 1)
            weights_high(0)
            act.wait_ge(M["sb_psum"], 5)
            act.activation(sb_pT[:, :, :], ps[:, 5, 0:B * S], ACT.Copy).then_inc(M["sb_act"], 1)
            weights_high(1)
            act.wait_ge(M["sb_psum"], 6)
            act.activation(sb_oT[:, :, :], ps[:, 6, :], ACT.Copy).then_inc(M["sb_act"], 1)

            def down_high(e):
                if e == 0:
                    act.wait_ge(M["mo_down_loaded"], 8 * 16)
                if e >= 2:
                    act.wait_ge(M["mo_y_psum"], e - 1)
                act.activation(mo_d_hi[:, e % 2, :, :], mo_down[:, e, :, :], ACT.Copy).then_inc(M["mo_d_split"], 1)

            def products_high(e):
                act.wait_ge(M["mo_a_done"], e + 1)
                if e >= 3:
                    act.wait_ge(M["mo_y_psum"], e - 2)
                act.activation(mo_a_hi[:, e % 3, :, :], mo_a[:, e % 2, :, :], ACT.Copy).then_inc(M["mo_a_hi_done"], 1)

            xnT_copy(3)
            act.activation(mo_x_hi[:, :, :], ps[:, 0, :], ACT.Copy).then_inc(M["mo_x_split"], 1)
            act.wait_ge(M["mo_psum"], 1)
            act.activation(mo_rT[:, :, :], ps[:, 1, 0:KC * E], ACT.Copy).then_inc(M["mo_act"], 1)
            act.wait_ge(M["mo_centred"], 1)
            act.activation(mo_s[:, :, :], mo_s[:, :, :], ACT.Exp).then_inc(M["mo_act"], 1)
            for e in range(E):
                if e + 2 < E:
                    weights_high(e + 2)
                act.wait_ge(M["mo_gu_psum"], e + 1)
                if e >= 2:
                    act.wait_ge(M["mo_a_done"], e - 1)
                act.activation(mo_sg[:, e % 2, :, :], ps[0:IP, 3 + 2 * (e % 2), :], ACT.Silu).then_inc(M["mo_silu"], 1)
                if e >= 1:
                    down_high(e - 1)
                products_high(e)
            down_high(E - 1)

        @block.vector
        def _(dve):
            links = [0]

            def chained(ins):
                links[0] += 1
                ins.then_inc(M["dve_chain"], 1)
                dve.wait_ge(M["dve_chain"], links[0])

            def layernorm(k):
                for b in range(B):
                    if k > 0:
                        dve.wait_ge(M["x_updated"], B * (k - 1) + b + 1)
                    chained(dve.bn_stats(stats[:, b, :], x_sb[:, b, :]))
                    dve.bn_aggr(meanvar[:, b, :], stats[:, b, :]).then_inc(M["ln_var"], 1)
                dve.wait_ge(M["ln_var"], B * (k + 1))
                dve.wait_ge(M["ln_rstd"], k + 1)
                for b in range(B):
                    dve.tensor_scalar(xn[:, b, :], x_sb[:, b, :], meanvar[:, b, 0:1], rstd[:, b:b + 1],
                                      ALU.subtract, ALU.mult).then_inc(M["xn_ready"], 1)

            dve.wait_ge(M["x_loaded"], 16)
            layernorm(0)

            def context_low(j):
                dve.wait_ge(M["ctxT_hi_done"], j + 1)
                dve.tensor_tensor(ctxT_lo[:, 4 * j:4 * j + 4, :], ps[:, 4 + j % 4, :].rearrange("p (c k) -> p c k", c=4),
                                  ctxT_hi[:, 4 * j:4 * j + 4, :].bitcast(F32), ALU.subtract).then_inc(M["ctxT_lo_done"], 1)

            def query_part(c):
                if 1 <= c < 9:
                    b, g = (c - 1) // NG, (c - 1) % NG
                    dve.wait_ge(M["q_rstd_done"], c)
                    dve.tensor_tensor(qn[:, b, G * g:G * g + G, :], ps[:, 4 + (c - 1) % 4, :].rearrange("p (h d) -> p h d", h=G),
                                      q_rstd[:, b, G * g:G * g + G].unsqueeze(2).to_broadcast([P, G, HD0]),
                                      ALU.mult).then_inc(M["qn_done"], 1)
                if c < 8:
                    b, g = c // NG, c % NG
                    dve.wait_ge(M["q_squared"], c + 1)
                    dve.tensor_reduce(q_ss[:, b, G * g:G * g + G], q_sq[:, c % 2, :].rearrange("p (h d) -> p h d", h=G),
                                      AX.X, ALU.add).then_inc(M["q_ss_done"], 1)
                elif c < 12:
                    context_low(c - 4)
                elif 18 <= c < 26:
                    j = c - 18
                    dve.wait_ge(M["q3_hi_done"], j + 1)
                    dve.tensor_tensor(q3_lo[:, :, 2 * j:2 * j + 2, :].rearrange("p b h s -> p h b s"),
                                      ps[:, 6 + j % 2, :].rearrange("p (h b s) -> p h b s", h=2, b=B),
                                      q3_hi[:, :, 2 * j:2 * j + 2, :].bitcast(F32).rearrange("p b h s -> p h b s"),
                                      ALU.subtract).then_inc(M["q3_lo_done"], 1)
                elif c == 26:
                    dve.wait_ge(M["small_psum"], 1)
                    dve.tensor_reduce(gain_max[:, :], ps[0:1, 4, 0:P], AX.X, ALU.max, apply_absolute_value=True).then_inc(M["gains_done"], 1)
                elif c == 28:
                    dve.wait_ge(M["small_psum"], 2)
                    chained(dve.tensor_scalar(shift[:, :], ps[:, 5, 0:1], -float(HD0), 75.0, ALU.mult, ALU.add))
                    dve.tensor_scalar(shift[:, :], shift[:, :], 0.0, None, ALU.min).then_inc(M["gains_done"], 1)

            dve.wait_ge(M["wk_loaded"], 16)
            chained(dve.tensor_copy(wk_hi[:, :], wk[:, :]))
            dve.tensor_tensor(wk_lo[:, :], wk[:, :], wk_hi[:, :].bitcast(F32), ALU.subtract).then_inc(M["wk_split"], 1)
            for j in range(4):
                context_low(j)
            dve.wait_ge(M["gains_loaded"], 32)
            dve.tensor_scalar(gqk[:, :], gains[:, 0:1], gains[:, 1:2], float(HD0) ** -0.5, ALU.mult, ALU.mult).then_inc(M["gains_done"], 1)
            for c in range(B * NC):
                for g in range(NG):
                    i = c * NG + g
                    dve.wait_ge(M["k_squared"], i + 1)
                    dve.tensor_reduce(k_ss[:, c, G * g:G * g + G], sq[:, i % 2, :].rearrange("p (h d) -> p h d", h=G),
                                      AX.X, ALU.add).then_inc(M["k_ss_done"], 1)
                query_part(c)
            ROUND = 1.5 * 2.0 ** 23

            def ternary(step):
                i, w = step // 3, (w1, w2)[step // 3]
                if step == 0:
                    dve.wait_ge(M["small_psum"], 3)
                    chained(dve.tensor_scalar(w_mean[:, :], ps[:, 7, 0:2], 1.0 / (FI * D), 1e-5, ALU.mult, ALU.max))
                    dve.reciprocal(w_scale[:, :], w_mean[:, :]).then_inc(M["wq_quant"], 1)
                dve.wait_ge(M["wq_quant"], step + 1)
                if step % 3 == 0:
                    dve.tensor_scalar(w[:, :, :], w[:, :, :], w_scale[:, i:i + 1], ROUND, ALU.mult, ALU.add).then_inc(M["wq_quant"], 1)
                elif step % 3 == 1:
                    dve.tensor_scalar(w[:, :, :], w[:, :, :], -ROUND, 1.0, ALU.add, ALU.min).then_inc(M["wq_quant"], 1)
                else:
                    dve.tensor_scalar(w[:, :, :], w[:, :, :], -1.0, None, ALU.max).then_inc(M["wq_quant"], 1)

            def normalise(j):
                b, g = j // NG, j % NG
                o = ps[:, 4 + 2 * (j % 2):6 + 2 * (j % 2), 0:2 * (C + 2)].rearrange("p k (h c) -> p k h c", h=2)
                dve.wait_ge(M["pv_chunk"], (j + 1) * (NC // 2))
                chained(dve.reciprocal(o_den[:, j, :].rearrange("p (k h) -> p k h", k=2), o[:, :, :, C]))
                dve.tensor_tensor(o_n[:, b, G * g:G * g + G, :].rearrange("p (k h) c -> p k h c", k=2), o[:, :, :, 0:C],
                                  o_den[:, j, :].rearrange("p (k h) -> p k h", k=2).unsqueeze(3).to_broadcast([P, 2, 2, C]),
                                  ALU.mult).then_inc(M["o_done"], 1)

            for b in range(B):
                dve.wait_ge(M["k_rstd_done"], b + 1)
                for g in range(NG):
                    for c2 in range(NC // 2):
                        i = (b * NG + g) * (NC // 2) + c2
                        if i % 2 == 1 and i // 2 < 6:
                            ternary(i // 2)
                        c = b * NC + 2 * c2
                        dve.wait_ge(M["s_psum"], i + 1)
                        if i >= 2:
                            dve.wait_ge(M["p_done"], i - 1)
                        dve.tensor_tensor(s_sb[:, i % 2, :, :].rearrange("p c (h s) -> p c h s", h=G),
                                          ps[:, 2 * (i % 2):2 * (i % 2) + 2, :].rearrange("p c (h s) -> p c h s", h=G),
                                          k_rstd[:, c:c + 2, G * g:G * g + G].unsqueeze(3).to_broadcast([P, 2, G, S]),
                                          ALU.mult).then_inc(M["s_scaled"], 1)
                        if c2 == 1 and i > 1:
                            normalise(b * NG + g - 1)
            normalise(B * NG - 1)
            for b in range(B):
                dve.wait_ge(M["y_psum"], b + 1)
                dve.tensor_tensor(x_sb[:, b, :], x_sb[:, b, :], ps[:, 4 + b, 0:D], ALU.add).then_inc(M["x_updated"], 1)
            layernorm(1)
            dve.memset(sa_v[:, :, :, HD:HD + 2], 1.0).then_inc(M["sa_v_done"], 1)
            dve.wait_ge(M["mask_ready"], 1)
            dve.wait_ge(M["sa_qkT"], 2 * KC)
            for b in range(B):
                for j in range(KC):
                    i = b * KC + j
                    if i >= 2:
                        dve.wait_ge(M["sa_s_psum"], i - 1)
                    dve.tensor_tensor(sa_km[:, i % 2, :, :], sa_kT[:, j, b * S:(b + 1) * S].unsqueeze(1).to_broadcast([P, 8, S]),
                                      head_mask[:, :].unsqueeze(2).to_broadcast([P, 8, S]), ALU.mult).then_inc(M["sa_km_done"], 1)
            for b in range(B):
                for j in range(KC):
                    dve.wait_ge(M["sa_s_psum"], b * KC + j + 1)
                    bank = 4 * (1 - b) + 2 * j
                    dve.tensor_tensor(sa_s[:, b, 8 * j:8 * j + 8, :], ps[:, bank:bank + 2, :].rearrange("p k (h s) -> p (k h) s", s=S),
                                      causal[:, :].unsqueeze(1).to_broadcast([P, 8, S]), ALU.add).then_inc(M["sa_s_masked"], 1)
                dve.wait_ge(M["sa_s_masked"], KC * (b + 1))
                chained(dve.tensor_reduce(sa_max[:, b, :], sa_s[:, b, :, :], AX.X, ALU.max))
                dve.tensor_tensor(sa_s[:, b, :, :], sa_s[:, b, :, :], sa_max[:, b, :].unsqueeze(2).to_broadcast([P, H, S]),
                                  ALU.subtract).then_inc(M["sa_centred"], 1)
            def heads(ap):
                return ap.rearrange("p (h d) -> p h d", d=HD)

            def per_head(ap, n):
                return ap.unsqueeze(2).to_broadcast([P, n, HD])

            dve.wait_ge(M["xb_wkv_loaded"], 64)
            for j, w in enumerate((xb_wkv, xb_bkv)):
                wv32 = w[:, :].rearrange("p (h d) -> p h d", d=2 * HD)
                chained(dve.tensor_reduce(xb_s32[:, j, 0:H], wv32[:, :, 0:HD], AX.X, ALU.add))
                chained(dve.tensor_scalar(xb_s32[:, j, 0:H], xb_s32[:, j, 0:H], 1.0 / HD, None, ALU.mult))
                dve.tensor_tensor(wv32[:, :, 0:HD], wv32[:, :, 0:HD], per_head(xb_s32[:, j, 0:H], H), ALU.subtract).then_inc(M["xb_centred"], 1)
            dve.wait_ge(M["xb_w_loaded"], 13 * 16)
            for j, w in ((2, xb_wq[:, :, :].rearrange("p k (h d) -> p (k h) d", d=HD)), (3, xb_bq[:, :].rearrange("p (h d) -> p h d", d=HD))):
                n = KC * H if j == 2 else H
                chained(dve.tensor_reduce(xb_s32[:, j, 0:n], w, AX.X, ALU.add))
                chained(dve.tensor_scalar(xb_s32[:, j, 0:n], xb_s32[:, j, 0:n], 1.0 / HD, None, ALU.mult))
                dve.tensor_tensor(w, w, per_head(xb_s32[:, j, 0:n], n), ALU.subtract).then_inc(M["xb_centred"], 1)
            dve.wait_ge(M["xb_centred"], 4)
            chained(dve.tensor_copy(xb_bkv_split[:, 0, :], xb_bkv[0:1, :]))
            dve.tensor_tensor(xb_bkv_split[:, 1, :], xb_bkv[0:1, :], xb_bkv_split[:, 0, :].bitcast(F32), ALU.subtract).then_inc(M["xb_centred"], 1)
            for b in range(B):
                dve.wait_ge(M["sa_o_psum"], b + 1)
                o = ps[:, 4 * (1 - b), 0:H * (HD + 2)].rearrange("p (h d) -> p h d", h=H)
                chained(dve.reciprocal(sa_den[:, b, :], o[:, :, HD]))
                dve.tensor_tensor(sa_o[:, b, :].rearrange("p (h d) -> p h d", h=H), o[:, :, 0:HD],
                                  sa_den[:, b, :].unsqueeze(2).to_broadcast([P, H, HD]), ALU.mult).then_inc(M["sa_o_done"], 1)
            for b in range(B):
                dve.wait_ge(M["y_psum"], B + b + 1)
                dve.tensor_tensor(x_sb[:, b, :], x_sb[:, b, :], ps[:, 4 * (1 - b) + 2, 0:D], ALU.add).then_inc(M["x_updated"], 1)
            layernorm(2)
            dve.wait_ge(M["xn_ready"], 3 * B)

            def quantise(i, src, dst):
                for b in range(B):
                    chained(dve.tensor_reduce(ff_max[:, i, b:b + 1], src[:, b, :], AX.X, ALU.max, apply_absolute_value=True))
                dve.wait_ge(M["ff_r_done"], i + 1)
                chained(dve.tensor_tensor(ff_max[:, i, :], ff_max[:, i, :], ff_r[:, i, :], ALU.mult))
                chained(dve.tensor_scalar(ff_max[:, i, :], ff_max[:, i, :], 1e-5, 1.0 / 127.0, ALU.max, ALU.mult))
                chained(dve.reciprocal(ff_s[:, i, :], ff_max[:, i, :]))
                chained(dve.tensor_scalar(ff_dq[:, i, :], ff_max[:, i, :], w_mean[:, i:i + 1], None, ALU.mult))
                for b in range(B):
                    chained(dve.tensor_scalar(dst[:, b, :], src[:, b, :], ff_r[:, i, b:b + 1], ff_s[:, i, b:b + 1], ALU.mult, ALU.mult))
                    chained(dve.tensor_scalar(dst[:, b, :], dst[:, b, :], ROUND, -ROUND, ALU.add, ALU.add))
                    dve.tensor_scalar(dst[:, b, :], dst[:, b, :], 127.0, -128.0, ALU.min, ALU.max).then_inc(M["ff_q_done"], 1)

            for b in range(B):
                dve.scalar_tensor_tensor(out=ff_sq[:, b, 0:D], in0=xn[:, b, :], scalar=1.0, in1=xn[:, b, :], op0=ALU.mult, op1=ALU.mult,
                                         accum_out=ff_ss[:, 0, b:b + 1]).then_inc(M["ff_ss_done"], 1)
            quantise(0, xn, ff_q1)
            dve.wait_ge(M["ffb_loaded"], 64)
            def key_sums(b, t):
                n = b * (NC // 2) + t
                dve.wait_ge(M["xb_k_sq"], n + 1)
                dve.tensor_reduce(xb_ss[:, 2 * t:2 * t + 2, :], sq[:, n % 2, :].rearrange("p (c h d) -> p c h d", c=2, h=H),
                                  AX.X, ALU.add).then_inc(M["xb_k_ss"], 1)

            for b in range(B):
                dve.wait_ge(M["ff_h_psum"], b + 1)
                dve.scalar_tensor_tensor(out=ff_h[:, b, :], in0=ps[:, 4 + 2 * b:6 + 2 * b, :].rearrange("p k n -> p (k n)"), scalar=ff_dq[:, 0, b:b + 1],
                                         in1=b1_all[:, :], op0=ALU.mult, op1=ALU.add).then_inc(M["ff_h_done"], 1)
            key_sums(0, 0)
            key_sums(0, 1)
            for b in range(B):
                dve.wait_ge(M["ff_gelu"], b + 1)
                for t in range(2):
                    chained(dve.bn_stats(ff_stats[:, b, t, :], ff_h[:, b, t * 512:(t + 1) * 512]))
                dve.bn_aggr(ff_mv[:, b, :], ff_stats[:, b, :, :]).then_inc(M["ff_lnvar"], 1)
            dve.wait_ge(M["ff_lnvar"], B)
            dve.wait_ge(M["ff_lnrstd"], 1)
            for b in range(B):
                chained(dve.tensor_scalar(ff_h2[:, b, :], ff_h[:, b, :], ff_mv[:, b, 0:1], ff_rstd[:, b:b + 1], ALU.subtract, ALU.mult))
                chained(dve.tensor_tensor(ff_h2[:, b, :], ff_h2[:, b, :], lng_all[:, :], ALU.mult))
                dve.tensor_tensor(ff_h2[:, b, :], ff_h2[:, b, :], lnb_all[:, :], ALU.add).then_inc(M["ff_normed"], 1)
            dve.wait_ge(M["ff_normed"], B)
            quantise(1, ff_h2, ff_h)
            for t in range(2, NC // 2):
                key_sums(0, t)
            for b in range(B):
                dve.wait_ge(M["y_psum"], 2 * B + b + 1)
                chained(dve.tensor_tensor(x_sb[:, b, :], x_sb[:, b, :], b2_all[:, :], ALU.add))
                dve.scalar_tensor_tensor(out=x_sb[:, b, :], in0=ps[:, 1 + b, 0:D], scalar=ff_dq[:, 1, b:b + 1], in1=x_sb[:, b, :],
                                         op0=ALU.mult, op1=ALU.add).then_inc(M["x_updated"], 1)

            def second_keys(c):
                dve.wait_ge(M["xb_kv_psum"], NC + c + 1)
                dve.tensor_tensor(xb_k[:, c, :, :], ps[:, 3, 0:D].rearrange("p (h d) -> p h d", h=H),
                                  xb_bkv[:, :].rearrange("p (h v d) -> p h v d", h=H, v=2)[:, :, 0, :], ALU.add).then_inc(M["xb_kv_done"], 1)

            def second_values(c):
                if c == 0:
                    dve.wait_ge(M["xb_pv_done"], UNITS)
                dve.wait_ge(M["xb_kv_psum"], 2 * NC + c + 1)
                dve.tensor_tensor(v_heads(c), ps[:, 3 + 3 * (c % 2), 0:D].rearrange("p (h d) -> p h d", h=H),
                                  xb_bkv[:, :].rearrange("p (h v d) -> p h v d", h=H, v=2)[:, :, 1, :], ALU.add).then_inc(M["xb_kv_done"], 1)

            def key_rstd(b):
                dve.wait_ge(M["xb_k_sqrt"], b + 1)
                dve.reciprocal(xb_rk[:, :, :], xb_rk[:, :, :]).then_inc(M["xb_kr_done"], 1)

            def head_norm(dst, tmp, sums, n):
                chained(dve.tensor_reduce(sums[:, 0, 0:n], heads(dst), AX.X, ALU.add))
                chained(dve.tensor_scalar(sums[:, 0, 0:n], sums[:, 0, 0:n], 1.0 / HD, None, ALU.mult))
                chained(dve.tensor_tensor(heads(dst), heads(dst), per_head(sums[:, 0, 0:n], n), ALU.subtract))
                chained(dve.tensor_tensor(tmp, dst, dst, ALU.mult))

            def k_full(n):
                i = n % PAIRS
                if n >= 1:
                    dve.wait_ge(M["xb_klo"], n)
                    dve.wait_ge(M["xb_khi"], n)
                dve.tensor_tensor(xb_kt[:, :, :, :], xb_k[:, :, 2 * i:2 * i + 2, :], xb_rk[:, :, 2 * i:2 * i + 2].unsqueeze(3).to_broadcast([P, NC, 2, HD]),
                                  ALU.mult).then_inc(M["xb_kt_done"], 1)

            def k_low(n):
                dve.wait_ge(M["xb_khi"], n + 1)
                dve.tensor_tensor(xb_kn[n % 2][:, :, :, HD:2 * HD].rearrange("p c h d -> p (c h) d"), xb_kt[:, :, :, :].rearrange("p c h d -> p (c h) d"),
                                  xb_kn[n % 2][:, :, :, 0:HD].bitcast(F32).rearrange("p c h d -> p (c h) d"), ALU.subtract).then_inc(M["xb_klo"], 1)

            layernorm(3)
            key_rstd(0)
            dve.wait_ge(M["xb_kr_done"], 1)
            k_full(0)
            q_all = xb_q[:, :, :].rearrange("p b d -> p (b d)")
            t_all = xb_t[:, :, :].rearrange("p b d -> p (b d)")
            qk_all = xb_qk[:, :, :].rearrange("p b d -> p (b d)")
            vec = lambda j, n: xb_vec[:, j, :].unsqueeze(1).to_broadcast([P, n, HD])
            dve.wait_ge(M["xb_w_loaded"], 13 * 16)
            dve.wait_ge(M["xb_q_psum"], 1)
            chained(dve.tensor_tensor(xb_q[:, :, :], ps[:, 0, :].rearrange("p (b d) -> p b d", b=B), xb_bq[:, :].unsqueeze(1).to_broadcast([P, B, D]), ALU.add))

            def queries(b, part):
                q_b, t_b, qk_b = q_all[:, b * D:(b + 1) * D], t_all[:, b * D:(b + 1) * D], qk_all[:, b * D:(b + 1) * D]
                half = xb_s32[:, :, b * H:(b + 1) * H]
                if part == 0:
                    chained(dve.tensor_tensor(t_b, q_b, q_b, ALU.mult))
                    dve.tensor_reduce(half[:, 1, :], heads(t_b), AX.X, ALU.add).then_inc(M["xb_q_ss"], 1)
                elif part == 1:
                    dve.wait_ge(M["xb_q_sqrt"], b + 1)
                    if b == 0:
                        chained(dve.reciprocal(half[:, 3, :], half[:, 2, :]))
                    chained(dve.tensor_tensor(heads(q_b), heads(q_b), per_head(half[:, 3, :], H), ALU.mult))
                    chained(dve.tensor_tensor(heads(q_b), heads(q_b), vec(0, H), ALU.mult))
                    dve.tensor_tensor(heads(q_b), heads(q_b), vec(1, H), ALU.add).then_inc(M["xb_q_done"], 1)
                    dve.wait_ge(M["xb_q_done"], b + 1)
                else:
                    chained(dve.scalar_tensor_tensor(out=heads(qk_b), in0=heads(q_b), scalar=SC, in1=vec(2, H), op0=ALU.mult, op1=ALU.mult))
                    chained(dve.scalar_tensor_tensor(out=heads(t_b), in0=heads(q_b), scalar=SC, in1=vec(3, H), op0=ALU.mult, op1=ALU.mult))
                    chained(dve.tensor_reduce(xb_qb[:, b * H:(b + 1) * H], heads(t_b), AX.X, ALU.add))

            for part in range(3):
                queries(0, part)
                if part == 0:
                    k_low(0)

            def last_rows(stage):
                if stage in (1, 2):
                    b = stage - 1
                    dve.wait_ge(M["xb_last_psum"], 1 + stage)
                    dve.tensor_tensor(xb_kd[:, b, :], ps[:, 3, :], xb_bd[:, :], ALU.add).then_inc(M["xb_kd_read"], 1)
                elif stage in (3, 4):
                    b = stage - 3
                    if b == 0:
                        dve.wait_ge(M["xb_kd_read"], 2)
                    half = xb_d32[:, :, b * H:(b + 1) * H]
                    head_norm(xb_kd[:, b, 0:D], t_all[:, 0:D], half, H)
                    chained(dve.tensor_reduce(half[:, 1, :], heads(t_all[:, 0:D]), AX.X, ALU.add))
                    if b == 1:
                        dve.engine_nop().then_inc(M["xb_kd_ss"], 1)
                elif stage in (5, 13):
                    if stage == 5:
                        dve.wait_ge(M["xb_kd_rstd"], 1)
                    for b in (0,) if stage == 5 else (1,):
                        k = heads(xb_kd[:, b, 0:D])
                        chained(dve.tensor_tensor(k, k, per_head(xb_d32[:, 3, b * H:(b + 1) * H], H), ALU.mult))
                        chained(dve.tensor_tensor(k, k, vec(4, H), ALU.mult))
                        chained(dve.tensor_tensor(k, k, vec(5, H), ALU.add))
                        dve.tensor_tensor(xb_kdm[b].rearrange("p (v h d) -> p v h d", h=8, d=HD), xb_kd[:, b, :].rearrange("p (v h d) -> p v h d", h=8, d=HD),
                                          head_mask[:, :].unsqueeze(1).unsqueeze(3).to_broadcast([P, 4, 8, HD]), ALU.mult).then_inc(M["xb_kdm_done"], 1)
                elif stage == 8:
                    dve.wait_ge(M["xb_last_psum"], 6)
                    sd = ps[:, 3, :].rearrange("p (h k) -> p h k", k=DCA)
                    chained(dve.tensor_reduce(xb_d32[:, 0, :], sd, AX.X, ALU.max))
                    dve.tensor_tensor(pd, sd, per_head(xb_d32[:, 0, :], B * H), ALU.subtract).then_inc(M["xb_sd_centred"], 1)
                elif stage == 10:
                    dve.wait_ge(M["xb_last_act"], 4)
                    chained(dve.tensor_reduce(xb_d32[:, 1, :], pd, AX.X, ALU.add))
                    chained(dve.reciprocal(xb_d32[:, 2, :], xb_d32[:, 1, :]))
                    dve.tensor_tensor(pd, pd, per_head(xb_d32[:, 2, :], B * H), ALU.mult).then_inc(M["xb_pd_done"], 1)
                elif stage == 12:
                    dve.wait_ge(M["xb_last_psum"], 8)
                    dve.tensor_copy(xb_o[:, :, :], ps[:, 3, :]).then_inc(M["xb_od_done"], 1)

            pd = xb_pd[:, :, :].rearrange("p b (h k) -> p (b h) k", k=DCA)

            def q_rows(b, h, n, value):
                chained(dve.tensor_copy(xb_qn[:, h:h + n, 3 * HD], value))
                return dve.tensor_tensor(xb_qn[:, h:h + n, 3 * HD + 1], value, xb_qn[:, h:h + n, 3 * HD].bitcast(F32), ALU.subtract)

            def stacked_queries(b):
                if b == 1:
                    dve.wait_ge(M["xb_q2_psum"], PAIRS)
                qk = heads(xb_qk[:, b, :])
                chained(dve.tensor_copy(xb_qn[:, :, 0:HD], qk))
                chained(dve.tensor_copy(xb_qn[:, :, HD:2 * HD], qk))
                chained(dve.tensor_tensor(xb_qn[:, :, 2 * HD:3 * HD], qk, xb_qn[:, :, 0:HD].bitcast(F32), ALU.subtract))
                q_rows(b, 0, H, xb_qb[:, b * H:(b + 1) * H]).then_inc(M["xb_qn_done"], 1)
                dve.wait_ge(M["xb_qn_done"], b + 1)

            def maximum(n, m):
                dve.wait_ge(M["xb_m_psum"], 8 * n + m + 1)
                dve.tensor_reduce(xb_pm[:, n % 2, 4 * (m % 2) + m // 2:4 * (m % 2) + m // 2 + 1],
                                  ps[:, 1 + m % 2, :].rearrange("p (c k) -> p c k", k=P)[:, :, 0:P - 1],
                                  AX.XY, ALU.max).then_inc(M["xb_m_done"], 1)

            def addends(n):
                b, i = n // PAIRS, n % PAIRS
                dve.wait_ge(M["xb_m_done"], 8 * n + 8)
                dve.wait_ge(M["xb_q1_done"], 2 * (b + 1))
                chained(dve.tensor_reduce(xb_m[:, n % 2, :], xb_pm[:, n % 2, :].rearrange("p (h u) -> p h u", h=2), AX.X, ALU.max))
                chained(dve.tensor_tensor(xb_m[:, n % 2, :], xb_qb[:, b * H + 2 * i:b * H + 2 * i + 2], xb_m[:, n % 2, :], ALU.subtract))
                q_rows(b, 2 * i, 2, xb_m[:, n % 2, :]).then_inc(M["xb_row_done"], 1)

            def sums_copy(b):
                dve.wait_ge(M["xb_pv_done"], (b + 1) * UNITS)
                dve.tensor_copy(xb_oh[:, :], ps[:, 7, :]).then_inc(M["xb_oh_done"], 1)

            def outputs(b):
                dve.wait_ge(M["xb_ohT_psum"], b + 1)
                o = ps[:, 5, :].rearrange("p (h d) -> p h d", h=H)
                chained(dve.reciprocal(xb_den[:, b, :], o[:, :, 2 * HD - 1]))
                chained(dve.tensor_tensor(heads(xb_t[:, b, :]), o[:, :, HD - 1:2 * HD - 1], per_head(xb_den[:, b, :], H), ALU.mult))
                dve.tensor_tensor(xb_o[:, b, :], xb_o[:, b, :], xb_t[:, b, :], ALU.add).then_inc(M["xb_o_done"], 1)

            stacked_queries(0)
            for slot in range(-6, B * OFFSET + 4):
                if unit_at(slot, 4):
                    n, m = unit_at(slot, 4)
                    maximum(n, m)
                    if m == 7:
                        addends(n)
                n, u = unit_at(slot, 14) or (0, 0)
                if u == 0 and n % PAIRS > 0:
                    k_full(n)
                n, u = unit_at(slot, 11) or (0, 0)
                if u == 0 and n % PAIRS > 0:
                    k_low(n)
                if slot in LAST_SLOTS:
                    last_rows(LAST_SLOTS[slot])
                if slot in (9, 13, 15):
                    queries(1, (9, 13, 15).index(slot))
                if 45 <= slot < 61:
                    second_keys(slot - 45)
                if 49 <= slot < 65 and slot % 2 == 1:
                    key_sums(1, (slot - 49) // 2)
                if slot == 64:
                    key_rstd(1)
                    dve.wait_ge(M["xb_kr_done"], 2)
                    k_full(PAIRS)
                    stacked_queries(1)
                if slot == 65:
                    k_low(PAIRS)
                for b in range(B):
                    if slot == OFFSET * (b + 1):
                        sums_copy(b)
                    if slot == OFFSET * (b + 1) + 3:
                        outputs(b)
                if OFFSET <= slot < OFFSET + 8:
                    second_values(2 * (slot - OFFSET))
                    second_values(2 * (slot - OFFSET) + 1)
            for b in range(B):
                dve.wait_ge(M["y_psum"], 3 * B + b + 1)
                dve.tensor_tensor(x_sb[:, b, :], x_sb[:, b, :], ps[:, 3 + b, 0:D], ALU.add).then_inc(M["x_updated"], 1)

            layernorm(4)
            dve.wait_ge(M["xn_ready"], 5 * B)
            for b in range(B):
                chained(dve.bn_stats(stats[:, b, :], xn[:, b, :]))
                dve.bn_aggr(sb_mv[:, b, :], stats[:, b, :]).then_inc(M["sb_var"], 1)
            dve.wait_ge(M["sb_var"], B)
            dve.wait_ge(M["sb_rstd_done"], 1)
            dve.wait_ge(M["sb_w_loaded"], 64)
            for b in range(B):
                chained(dve.tensor_scalar(sb_h[:, b, :], xn[:, b, :], sb_mv[:, b, 0:1], sb_rstd[:, b:b + 1], ALU.subtract, ALU.mult))
            chained(dve.tensor_tensor(sb_h[:, :, :], sb_h[:, :, :], sb_g[:, 0, :].unsqueeze(1).to_broadcast([P, B, D]), ALU.mult))
            dve.tensor_tensor(sb_h[:, :, :], sb_h[:, :, :], sb_g[:, 1, :].unsqueeze(1).to_broadcast([P, B, D]), ALU.add).then_inc(M["sb_dve"], 1)
            def weights_low(e):
                dve.wait_ge(M["mo_w_split"], 2 * (e + 1))
                for t, w in ((0, mo_gate), (1, mo_up)):
                    dve.tensor_tensor(mo_w_lo[:, e % 3, t, :, :], w[:, e, :, :], mo_w_hi[:, e % 3, t, :, :].bitcast(F32), ALU.subtract).then_inc(M["mo_w_low"], 1)

            dve.wait_ge(M["sb_psum"], 4)
            dve.wait_ge(M["sb_masks"], 2)
            chained(dve.tensor_tensor(sb_s[:, :, :], ps[:, 4, 0:B * S].rearrange("p (b s) -> p b s", b=B), causal2[:, :].unsqueeze(1).to_broadcast([P, B, S]), ALU.add))
            chained(dve.tensor_reduce(sb_m[:, 0, :], sb_s[:, :, :], AX.X, ALU.max))
            dve.tensor_tensor(sb_s[:, :, :], sb_s[:, :, :], sb_m[:, 0, :].unsqueeze(2).to_broadcast([P, B, S]), ALU.subtract).then_inc(M["sb_dve"], 1)
            dve.wait_ge(M["sb_act"], 5)
            chained(dve.tensor_reduce(sb_m[:, 1, :], sb_s[:, :, :], AX.X, ALU.add))
            chained(dve.reciprocal(sb_m[:, 2, :], sb_m[:, 1, :]))
            dve.tensor_tensor(sb_s[:, :, :], sb_s[:, :, :], sb_m[:, 2, :].unsqueeze(2).to_broadcast([P, B, S]), ALU.mult).then_inc(M["sb_dve"], 1)
            for b in range(B):
                chained(dve.tensor_tensor(x_sb[:, b, :], x_sb[:, b, :], xn[:, b, :], ALU.add))
            weights_low(0)
            weights_low(1)
            for b in range(B):
                dve.wait_ge(M["y_psum"], 5 * B)
                dve.tensor_tensor(x_sb[:, b, :], x_sb[:, b, :], ps[:, 7, b * D:(b + 1) * D], ALU.add).then_inc(M["x_updated"], 1)

            def down_low(e):
                dve.wait_ge(M["mo_d_split"], e + 1)
                dve.tensor_tensor(mo_d_lo[e % 2][:, :, :], mo_down[:, e, :, :], mo_d_hi[:, e % 2, :, :].bitcast(F32), ALU.subtract).then_inc(M["mo_d_low"], 1)

            layernorm(5)
            dve.wait_ge(M["mo_x_split"], 1)
            dve.tensor_tensor(mo_x_lo[:, :, :], ps[:, 0, :].rearrange("p (k s) -> p k s", k=KC), mo_x_hi[:, :, :].bitcast(F32), ALU.subtract).then_inc(M["mo_x_split"], 1)

            def router(part):
                if part == 0:
                    dve.wait_ge(M["mo_r_loaded"], 32)
                    dve.wait_ge(M["mo_psum"], 2)
                    chained(dve.tensor_tensor(mo_s[:, :, :], ps[:, 2, 0:B * E].rearrange("p (b e) -> p b e", b=B), mo_bias[:, :].unsqueeze(1).to_broadcast([P, B, E]), ALU.add))
                    chained(dve.tensor_reduce(mo_m[:, 0, :], mo_s[:, :, :], AX.X, ALU.max))
                    dve.tensor_tensor(mo_s[:, :, :], mo_s[:, :, :], mo_m[:, 0, :].unsqueeze(2).to_broadcast([P, B, E]), ALU.subtract).then_inc(M["mo_centred"], 1)
                elif part == 1:
                    dve.wait_ge(M["mo_act"], 2)
                    chained(dve.tensor_reduce(mo_m[:, 1, :], mo_s[:, :, :], AX.X, ALU.add))
                    chained(dve.reciprocal(mo_m[:, 2, :], mo_m[:, 1, :]))
                    chained(dve.tensor_tensor(mo_s[:, :, :], mo_s[:, :, :], mo_m[:, 2, :].unsqueeze(2).to_broadcast([P, B, E]), ALU.mult))
                elif part < 4:
                    b = part - 2
                    mine = mo_s[:, b, :].unsqueeze(2).to_broadcast([P, E, E])
                    other = mo_s[:, b, :].unsqueeze(1).to_broadcast([P, E, E])
                    chained(dve.tensor_tensor(mo_gt[:, b, :, :], other, mine, ALU.is_gt))
                    chained(dve.tensor_tensor(mo_eq[:, b, :, :], other, mine, ALU.is_equal))
                    chained(dve.tensor_tensor(mo_eq[:, b, :, :], mo_eq[:, b, :, :], mo_first[:, :, :], ALU.mult))
                    chained(dve.tensor_tensor(mo_gt[:, b, :, :], mo_gt[:, b, :, :], mo_eq[:, b, :, :], ALU.add))
                    chained(dve.tensor_reduce(mo_rank[:, b, :], mo_gt[:, b, :, :], AX.X, ALU.add))
                else:
                    chained(dve.scalar_tensor_tensor(out=mo_s[:, :, :], in0=mo_rank[:, :, :], scalar=TOP - 0.5, in1=mo_s[:, :, :], op0=ALU.is_lt, op1=ALU.mult))
                    chained(dve.tensor_reduce(mo_m[:, 1, :], mo_s[:, :, :], AX.X, ALU.add))
                    chained(dve.reciprocal(mo_m[:, 2, :], mo_m[:, 1, :]))
                    chained(dve.tensor_tensor(mo_s[:, :, :], mo_s[:, :, :], mo_m[:, 2, :].unsqueeze(2).to_broadcast([P, B, E]), ALU.mult))

            def products(e):
                dve.wait_ge(M["mo_silu"], e + 1)
                if e >= 2:
                    dve.wait_ge(M["mo_a_hi_done"], e - 1)
                dve.tensor_tensor(mo_a[:, e % 2, :, :].rearrange("p i s -> p (i s)"), ps[0:IP, 4 + 2 * (e % 2), :], mo_sg[:, e % 2, :, :].rearrange("p i s -> p (i s)"),
                                  ALU.mult).then_inc(M["mo_a_done"], 1)

            def products_low(e):
                dve.wait_ge(M["mo_a_hi_done"], e + 1)
                dve.tensor_tensor(mo_a_lo[:, e % 3, :, :], mo_a[:, e % 2, :, :], mo_a_hi[:, e % 3, :, :].bitcast(F32), ALU.subtract).then_inc(M["mo_a_lo_done"], 1)

            def add_expert(e):
                dve.wait_ge(M["mo_y_psum"], e + 1)
                if e >= 1:
                    dve.wait_ge(M["mo_y_done"], B * e)
                for b in range(B):
                    ins = dve.scalar_tensor_tensor(out=x_sb[:, b, :], in0=ps[:, Y_BANKS[e % 4], b * D:(b + 1) * D], scalar=mo_s[:, b, e:e + 1], in1=x_sb[:, b, :],
                                                   op0=ALU.mult, op1=ALU.add)
                    ins.then_inc(M["x_updated"] if e == E - 1 else M["mo_y_done"], 1)

            router(0)
            for e in range(E):
                if e + 2 < E:
                    weights_low(e + 2)
                products(e)
                if e >= 1:
                    down_low(e - 1)
                if 1 <= e < 5:
                    router(e)
                elif e in (5, 6):
                    add_expert(2 * (e - 5))
                    add_expert(2 * (e - 5) + 1)
                elif e > 6:
                    add_expert(e - 3)
                products_low(e)
            down_low(E - 1)
            for e in range(E - 3, E):
                add_expert(e)

        @block.tensor
        def _(pe):
            def xn_transposes(k):
                pe.wait_ge(M["xn_ready"], B * (k + 1))
                for kc in range(KC):
                    for b in range(B):
                        last = pe.transpose(ps[:, 0, (kc * B + b) * P:(kc * B + b + 1) * P], xn[:, b, kc * P:(kc + 1) * P], ident[:, :])
                last.then_inc(M["xT_psum"], 1)

            pe.wait_ge(M["ident_ready"], 1)
            xn_transposes(0)

            def context_transposes(j):
                if j >= 4:
                    pe.wait_ge(M["qn_done"], j + 1)
                for t in range(4):
                    last = pe.transpose(ps[:, 4 + j % 4, t * P:(t + 1) * P], ctx_nat[:, 4 * j + t, 0:C], ident[:, :])
                last.then_inc(M["ctxT_psum"], 1)

            def query_part(c):
                if c < 8:
                    b, g = c // NG, c % NG
                    if c == 0:
                        pe.wait_ge(M["wq_loaded"], 16)
                    if c < 4:
                        pe.wait_ge(M["ctxT_lo_done"], c + 1)
                    else:
                        pe.wait_ge(M["qn_done"], c - 3)
                    for kc in range(KC):
                        last = pe.matmul(ps[:, 4 + c % 4, :], xnT[:, kc, b * S:(b + 1) * S],
                                         wq[:, kc, g * 512:(g + 1) * 512], start=(kc == 0), stop=(kc == KC - 1))
                    last.then_inc(M["q_psum"], 1)
                elif c < 12:
                    if c == 8:
                        pe.wait_ge(M["ctx1_loaded"], 16)
                    context_transposes(c - 4)
                elif c < 14:
                    for j in (2 * (c - 12), 2 * (c - 12) + 1):
                        pe.wait_ge(M["ctxT_lo_done"], j + 5)
                        for t in range(4):
                            h = 4 * j + t
                            last = pe.transpose(ps[:, 4 + j, t * P:(t + 1) * P], wk[:, h * P:(h + 1) * P], ident[:, :])
                        last.then_inc(M["wkT_psum"], 1)
                elif c < 18:
                    for j in (2 * (c - 14), 2 * (c - 14) + 1):
                        if j >= 2:
                            pe.wait_ge(M["qT_done"], j - 1)
                        else:
                            pe.wait_ge(M["wkT_done"], H // 4)
                        for t in range(2):
                            for b in range(B):
                                last = pe.transpose(ps[:, 4 + j % 2, (t * B + b) * P:(t * B + b + 1) * P], qn[:, b, 2 * j + t, :], ident[:, :])
                        last.then_inc(M["qT_psum"], 1)
                elif c < 26:
                    j = c - 18
                    pe.wait_ge(M["qT_done"], j + 1)
                    if j >= 2:
                        pe.wait_ge(M["q3_lo_done"], j - 1)
                    for t in range(2):
                        h = 2 * j + t
                        last = pe.matmul(ps[:, 6 + j % 2, t * B * S:(t + 1) * B * S], wkT[:, h, :], qT[:, h, :], start=True, stop=True)
                    last.then_inc(M["q3_psum"], 1)
                elif c == 26:
                    pe.wait_ge(M["gains_done"], 1)
                    pe.transpose(ps[0:1, 4, 0:P], gqk[:, :], ident[:, :]).then_inc(M["small_psum"], 1)
                elif c == 28:
                    pe.wait_ge(M["gains_done"], 2)
                    pe.matmul(ps[:, 5, 0:1], ones[0:1, :], gain_max[:, :], start=True, stop=True).then_inc(M["small_psum"], 1)

            pe.wait_ge(M["ctx_loaded"], 16)
            for j in range(4):
                context_transposes(j)
            pe.wait_ge(M["wk_split"], 1)
            pe.wait_ge(M["xnT_ready"], 1)
            for c in range(B * NC):
                if c % 4 == 0:
                    pe.wait_ge(M["ctxT_lo_done"], c // 4 + 1)
                for g in range(NG):
                    i = c * NG + g
                    if i >= 4:
                        pe.wait_ge(M["k_squared"], i - 3)
                    r = slice(g * 512, (g + 1) * 512)
                    pe.matmul(ps[:, i % 4, :], ctxT_hi[:, c, :], wk_hi[:, r], start=True, stop=False)
                    pe.matmul(ps[:, i % 4, :], ctxT_hi[:, c, :], wk_lo[:, r], start=False, stop=False)
                    pe.matmul(ps[:, i % 4, :], ctxT_lo[:, c, :], wk_hi[:, r], start=False, stop=True).then_inc(M["k_psum"], 1)
                query_part(c)
            pe.wait_ge(M["q3_lo_done"], H // 2)
            pe.wait_ge(M["wabs_done"], 2)
            pe.matmul(ps[:, 7, 0:2], ones[:, :], w_abs[:, :], start=True, stop=True).then_inc(M["small_psum"], 1)
            pe.wait_ge(M["k_squared"], B * NC * NG)

            STEPS = B * NG * (NC // 2)

            def scores(i):
                b, g, c2 = i // (NG * NC // 2), i // (NC // 2) % NG, i % (NC // 2)
                if i >= 2:
                    pe.wait_ge(M["s_scaled"], i - 1)
                for t in range(2):
                    c = b * NC + 2 * c2 + t
                    bank = 2 * (i % 2) + t
                    q_hi = q3_hi[:, b, G * g:G * g + G, :]
                    q_lo = q3_lo[:, b, G * g:G * g + G, :]
                    pe.matmul(ps[:, bank, :], ctxT_hi[:, c, :], q_hi, start=True, stop=False)
                    pe.matmul(ps[:, bank, :], ctxT_hi[:, c, :], q_lo, start=False, stop=False)
                    last = pe.matmul(ps[:, bank, :], ctxT_lo[:, c, :], q_hi, start=False, stop=True)
                last.then_inc(M["s_psum"], 1)

            def weighted_sums(i):
                b, g, c2 = i // (NG * NC // 2), i // (NC // 2) % NG, i % (NC // 2)
                j = b * NG + g
                pe.wait_ge(M["p_done"], i + 1)
                if c2 == 0 and j == 1:
                    pe.wait_ge(M["wq_quant"], 1)
                if c2 == 0 and j >= 2:
                    pe.wait_ge(M["o_done"], j - 1)
                for t in range(2):
                    c = b * NC + 2 * c2 + t
                    for h in range(G):
                        at = ps[:, 4 + 2 * (j % 2) + h // 2, (h % 2) * (C + 2):(h % 2) * (C + 2) + C + 1]
                        first = c2 == 0 and t == 0
                        last = pe.matmul(at, p_sb[:, i % 2, t, h * S:(h + 1) * S], ctx_nat[:, c, 0:C + 1],
                                         start=first and h % 2 == 0, stop=(c2 == NC // 2 - 1 and t == 1), skip_group_check=True)
                last.then_inc(M["pv_chunk"], 1)

            for i in range(STEPS + 1):
                if i < STEPS:
                    scores(i)
                if i >= 1:
                    weighted_sums(i - 1)
            pe.wait_ge(M["o_done"], B * NG)
            pe.wait_ge(M["wv_loaded"], 16)
            pe.wait_ge(M["wo_loaded"], 16)
            for j in range(H // 2):
                if j >= 2:
                    pe.wait_ge(M["oT_done"], j - 1)
                for t in range(2):
                    for b in range(B):
                        last = pe.transpose(ps[:, j % 2, (t * B + b) * P:(t * B + b + 1) * P], o_n[:, b, 2 * j + t, :], ident[:, :])
                last.then_inc(M["oT_psum"], 1)
            for j in range(H // 2):
                pe.wait_ge(M["oT_done"], j + 1)
                if j >= 2:
                    pe.wait_ge(M["aT_done"], j - 1)
                for t in range(2):
                    h = 2 * j + t
                    last = pe.matmul(ps[:, 2 + j % 2, t * B * S:(t + 1) * B * S], wv[:, h, :], oT[:, h, :], start=True, stop=True)
                last.then_inc(M["aT_psum"], 1)
            pe.wait_ge(M["aT_done"], H // 2)
            for b in range(B):
                for h in range(H):
                    last = pe.matmul(ps[:, 4 + b, 0:D], aT[:, h, b * S:(b + 1) * S], wo[:, h, :], start=(h == 0), stop=(h == H - 1))
                last.then_inc(M["y_psum"], 1)

            def weight_transposes(i):
                pe.wait_ge(M["wq_quant"], 4 + 3 * (i // 4))
                pe.wait_ge(M["sa_s_masked"], KC * (i // 4 + 1))
                for t in range(4):
                    if i < 4:
                        src = w1[:, 4 * (i % 2) + t, (i // 2) * P:(i // 2 + 1) * P]
                    else:
                        ic, o = 2 * (i - 4) + t // 2, t % 2
                        src = w2[:, o, ic * P:(ic + 1) * P]
                    last = pe.transpose(ps[:, (4 + i) % 8, t * P:(t + 1) * P], src, ident[:, :])
                last.then_inc(M["wqT_psum"], 1)

            xn_transposes(1)
            pe.wait_ge(M["xnT_ready"], 2)
            pe.wait_ge(M["sa_w_loaded"], 128)
            for t in range(2):
                for j in range(KC):
                    for kc in range(KC):
                        last = pe.matmul(ps[:, 1 + t, j * B * S:(j + 1) * B * S], w_in[:, kc, t * D + j * P:t * D + (j + 1) * P],
                                         xnT[:, kc, :], start=(kc == 0), stop=(kc == KC - 1))
            last.then_inc(M["sa_q_psum"], 1)
            for b in range(B):
                for kc in range(KC):
                    pe.matmul(ps[:, 3, b * D:(b + 1) * D], xnT[:, kc, b * S:(b + 1) * S], w_in[:, kc, 2 * D:3 * D], start=(kc == 0), stop=False)
                last = pe.matmul(ps[:, 3, b * D:(b + 1) * D], ones[0:1, :], b_in_row[:, 2 * D:3 * D], start=False, stop=True)
            last.then_inc(M["sa_v_psum"], 1)
            for b in range(B):
                if b == 1:
                    pe.wait_ge(M["sa_v_done"], 2)
                    pe.wait_ge(M["sa_qkT"], 2 * KC)
                for j in range(KC):
                    i = b * KC + j
                    pe.wait_ge(M["sa_km_done"], i + 1)
                    for t in range(2):
                        last = pe.matmul(ps[:, 4 * (1 - b) + 2 * j + t, :], sa_qT[:, j, b * S:(b + 1) * S],
                                         sa_km[:, i % 2, 4 * t:4 * t + 4, :], start=True, stop=True)
                    last.then_inc(M["sa_s_psum"], 1)
            for i in range(8):
                weight_transposes(i)
            for b in range(B):
                pe.wait_ge(M["sa_p_done"], b + 1)
                pe.wait_ge(M["wqT_done"], 4 * (b + 1))
                for g in range(4):
                    for t in range(4):
                        last = pe.transpose(ps[:, 4 * (1 - b) + g, t * P:(t + 1) * P], sa_s[:, b, 4 * g + t, :], ident[:, :])
                    last.then_inc(M["sa_pT_psum"], 1)
            def context_transposes_2(b, g):
                if b == 0:
                    pe.wait_ge(M["sa_pT_done"], 4 if g == 0 else 8)
                    if g >= 2:
                        pe.wait_ge(M["xb_cT_done"], g - 1)
                elif g == 0:
                    pe.wait_ge(M["xb_od_done"], 1)
                else:
                    pe.wait_ge(M["xb_cT_done"], 4 + g)
                bank = 3 if b == 1 else 7 - 4 * (g % 2)
                for t in range(4):
                    last = pe.transpose(ps[:, bank, t * P:(t + 1) * P], ctx_nat[:, b * NC + 4 * g + t, 0:C], ident[:, :])
                last.then_inc(M["xb_cT_psum"], 1)

            def key_products(first, last):
                if first == 0:
                    pe.wait_ge(M["xb_cT_done"], 4)
                    pe.wait_ge(M["xb_centred"], 5)
                for c in range(first, last):
                    if c >= 2:
                        pe.wait_ge(M["xb_kv_done"], c if c == NC // 2 else c - 1)
                    pe.matmul(ps[:, KEY_BANKS[c], :], xb_cT[0][c // 4][:, c % 4, :], xb_wkv[:, :], start=True, stop=False)
                    for part in range(2):
                        last = pe.matmul(ps[:, KEY_BANKS[c], :], ones[0:1, :].bitcast(F32R), xb_bkv_split[:, part, :], start=False, stop=(part == 1))
                    last.then_inc(M["xb_kv_psum"], 1)

            for g in range(4):
                context_transposes_2(0, g)
            for b in range(B):
                pe.wait_ge(M["sa_pT_done"], 4 * b + 4)
                for h in range(H):
                    last = pe.matmul(ps[:, 4 * (1 - b), h * (HD + 2):h * (HD + 2) + HD + 1], sa_pT[:, b, h, :], sa_v[:, b, h, 0:HD + 1],
                                     start=True, stop=True)
                last.then_inc(M["sa_o_psum"], 1)
            key_products(0, 2)
            for b in range(B):
                pe.wait_ge(M["sa_o_done"], b + 1)
                for kc in range(KC):
                    last = pe.transpose(ps[:, 4 * (1 - b) + 1, kc * S:(kc + 1) * S], sa_o[:, b, kc * P:(kc + 1) * P], ident[:, :])
                last.then_inc(M["sa_oT_psum"], 1)
            for b in range(B):
                pe.wait_ge(M["sa_oT_done"], b + 1)
                y = ps[:, 4 * (1 - b) + 2, 0:D]
                for kc in range(KC):
                    pe.matmul(y, sa_oT[:, kc, b * S:(b + 1) * S], w_out[:, kc, :], start=(kc == 0), stop=False)
                pe.matmul(y, ones[0:1, :], b_out_row[:, :], start=False, stop=True).then_inc(M["y_psum"], 1)
            key_products(2, 8)
            pe.wait_ge(M["ff_q_done"], B)
            for kc in range(KC):
                for b in range(B):
                    last = pe.transpose(ps[:, 0, (kc * B + b) * P:(kc * B + b + 1) * P], ff_q1[:, b, kc * P:(kc + 1) * P], ident[:, :])
            last.then_inc(M["ff_qT_psum"], 1)
            pe.wait_ge(M["ff_qT_done"], 1)
            pe.wait_ge(M["xb_kv_done"], 7)
            pe.wait_ge(M["wqT_done"], 8)
            for b in range(B):
                for t in range(2):
                    for kc in range(KC):
                        last = pe.matmul(ps[:, 4 + 2 * b + t, :], ff_qT1[:, kc, b * S:(b + 1) * S], w1qT[:, kc, t * 512:(t + 1) * 512],
                                         start=(kc == 0), stop=(kc == KC - 1))
                last.then_inc(M["ff_h_psum"], 1)
            key_products(8, NC)
            for b in range(B):
                pe.wait_ge(M["ff_q_done"], B + b + 1)
                for g in range(2):
                    for t in range(4):
                        last = pe.transpose(ps[:, 4 + 2 * b + g, t * P:(t + 1) * P], ff_h[:, b, (4 * g + t) * P:(4 * g + t + 1) * P], ident[:, :])
                    last.then_inc(M["ff_qT_psum"], 1)
            for b in range(B):
                pe.wait_ge(M["ff_qT_done"], 1 + 2 * (b + 1))
                for ic in range(FC):
                    last = pe.matmul(ps[:, 1 + b, 0:D], ff_qT2[:, ic, b * S:(b + 1) * S], w2qT[:, ic, :], start=(ic == 0), stop=(ic == FC - 1))
                last.then_inc(M["y_psum"], 1)

            xn_transposes(3)
            pe.wait_ge(M["xnT_ready"], 3)
            pe.wait_ge(M["xb_w_loaded"], 13 * 16)
            for b in range(B):
                for kc in range(KC):
                    last = pe.matmul(ps[:, 0, b * D:(b + 1) * D], xnT[:, kc, b * S:(b + 1) * S], xb_wq[:, kc, :], start=(kc == 0), stop=(kc == KC - 1))
            last.then_inc(M["xb_q_psum"], 1)

            def last_rows(stage):
                if stage == 0:
                    for b in range(B):
                        last = pe.transpose(ps[:, 3, b * DCA:(b + 1) * DCA], xb_yd[:, b, :], ident[0:DCA, 0:DCA])
                elif stage in (1, 2):
                    b = stage - 1
                    if b == 0:
                        pe.wait_ge(M["xb_last_act"], 1)
                    else:
                        pe.wait_ge(M["xb_kd_read"], 1)
                    last = pe.matmul(ps[:, 3, :], xb_ydT[:, b, :, :].rearrange("p r k -> p (r k)"), xb_wd[:, :], start=True, stop=True)
                elif stage == 6:
                    pe.wait_ge(M["xb_kdm_done"], B)
                    for b in range(B):
                        for kc in range(KC):
                            last = pe.transpose(ps[:, 3, (b * KC + kc) * P:(b * KC + kc + 1) * P], xb_kdm[b][:, kc * P:(kc + 1) * P], ident[:, :])
                elif stage == 7:
                    pe.wait_ge(M["xb_last_act"], 2)
                    for kc in range(KC):
                        for b in range(B):
                            last = pe.transpose(ps[:, 3, (kc * B + b) * S:(kc * B + b + 1) * S], xb_q[:, b, kc * P:(kc + 1) * P], ident[:, :])
                elif stage == 8:
                    pe.wait_ge(M["xb_last_act"], 3)
                    for b in range(B):
                        for kc in range(KC):
                            last = pe.matmul(ps[:, 3, b * D + kc * P:b * D + (kc + 1) * P], xb_qfT[:, kc, b * S:(b + 1) * S], xb_kdT[:, b, kc, :], start=True, stop=True)
                elif stage == 11:
                    pe.wait_ge(M["xb_pd_done"], 1)
                    for kc in range(KC):
                        for b in range(B):
                            last = pe.transpose(ps[:, 3, (kc * B + b) * S:(kc * B + b + 1) * S], xb_pd[:, b, kc * P:(kc + 1) * P], ident[:, :])
                elif stage == 12:
                    pe.wait_ge(M["xb_last_act"], 5)
                    for b in range(B):
                        for kc in range(KC):
                            last = pe.matmul(ps[:, 3, b * D + kc * P:b * D + (kc + 1) * P], xb_pdT[:, kc, b * S:(b + 1) * S],
                                             xb_kdm[b][:, D + kc * P:D + (kc + 1) * P], start=True, stop=True)
                else:
                    return
                last.then_inc(M["xb_last_psum"], 1)

            def k_transposes(n, g):
                pe.wait_ge(M["xb_klo"], n + 1)
                if 4 * n + g >= 2:
                    pe.wait_ge(M["xb_kT_done"], 4 * n + g - 1)
                if g == 2 and n % PAIRS > 0:
                    pe.wait_ge(M["xb_q2_done"], n)
                for t in range(4):
                    last = pe.transpose(ps[:, 4 * (g % 2), t * P:(t + 1) * P],
                                        xb_kn[n % 2][:, 4 * g + t, :, :].bitcast(F32).rearrange("p h w -> p (h w)"), ident[:, :])
                last.then_inc(M["xb_kT_psum"], 1)

            def maxima(n, m):
                pe.wait_ge(M["xb_kT_done"], 4 * n + m // 2 + 1)
                if 8 * n + m >= 2:
                    pe.wait_ge(M["xb_m_done"], 8 * n + m - 1)
                r = slice(W * (m % 2), W * (m % 2) + W)
                pe.matmul(ps[:, 1 + m % 2, :], xb_qT1[r, n % PAIRS, :], xb_kT[r, n % 2, 4 * (m // 2):4 * (m // 2) + 4, :],
                          start=True, stop=True).then_inc(M["xb_m_psum"], 1)

            def q_transpose(n):
                i = n % PAIRS
                pe.wait_ge(M["xb_row_done"], n + 1)
                pe.wait_ge(M["xb_kT_done"], min(4 * n + 5, 4 * PAIRS * (n // PAIRS + 1)))
                pe.transpose(ps[:, 0, 0:S], xb_qn[:, 2 * i:2 * i + 2, :].bitcast(F32).rearrange("p h w -> p (h w)"), ident[:, :]).then_inc(M["xb_q2_psum"], 1)

            def scores_t(n, u):
                m = n * NU + u
                pe.wait_ge(M["xb_q2_done"], n + 1)
                if m >= 2:
                    pe.wait_ge(M["xb_p_done"], m - 1)
                for t in range(2):
                    last = pe.matmul(ps[:, 5 + u % 2, t * 2 * S:(t + 1) * 2 * S], xb_kT[:, n % 2, 2 * u + t, :], xb_qT2[:, n % 2, :],
                                     start=True, stop=True)
                last.then_inc(M["xb_s_psum"], 1)

            def head_sums(n, u):
                m, i = n * NU + u, n % PAIRS
                pe.wait_ge(M["xb_p_done"], m + 1)
                for t in range(2):
                    c = 2 * u + t
                    for h in (2 * i, 2 * i + 1):
                        last = pe.matmul(ps[32 * (h % 4):32 * (h % 4) + 32, 7, (h // 4) * S:(h // 4 + 1) * S], xb_v[0:P - 1, c, h * VW:h * VW + 2 * HD],
                                         xb_p[0:P - 1, m % 2, 2 * t + h % 2, :], start=(c == 0), stop=(c == NC - 1), skip_group_check=True)
                last.then_inc(M["xb_pv_done"], 1)

            def queries_1(b):
                pe.wait_ge(M["xb_qn_done"], b + 1)
                if b == 0:
                    pe.wait_ge(M["xb_kv_done"], NC)
                    pe.wait_ge(M["x_updated"], 3 * B)
                else:
                    pe.wait_ge(M["xb_m_done"], 8 * PAIRS)
                for g in range(2):
                    for t in range(4):
                        j = 4 * g + t
                        last = pe.transpose(ps[:, 1 + g, t * P:(t + 1) * P], xb_qn[:, 2 * j:2 * j + 2, :].bitcast(F32).rearrange("p h w -> p (h w)"), ident[:, :])
                    last.then_inc(M["xb_q1_psum"], 1)

            def second_keys(c):
                if c == 0:
                    pe.wait_ge(M["xb_cT_done"], 8)
                else:
                    pe.wait_ge(M["xb_kv_done"], NC + c)
                pe.matmul(ps[:, 3, 0:D], xb_cT[1][c // 4][:, c % 4, :], xb_wkv[:, :].rearrange("p (h v d) -> p h v d", h=H, v=2)[:, :, 0, :],
                          start=True, stop=True).then_inc(M["xb_kv_psum"], 1)

            def second_values(c):
                if c == 0:
                    pe.wait_ge(M["xb_kv_done"], 2 * NC)
                elif c == 1:
                    pe.wait_ge(M["xb_p_done"], UNITS)
                else:
                    pe.wait_ge(M["xb_kv_done"], 2 * NC + c - 1)
                pe.matmul(ps[:, 3 + 3 * (c % 2), 0:D], xb_cT[1][c // 4][:, c % 4, :], xb_wkv[:, :].rearrange("p (h v d) -> p h v d", h=H, v=2)[:, :, 1, :],
                          start=True, stop=True).then_inc(M["xb_kv_psum"], 1)

            def sums_transposes(b):
                pe.wait_ge(M["xb_oh_done"], b + 1)
                pe.wait_ge(M["xb_p_done"], (b + 1) * UNITS)
                for g in range(4):
                    last = pe.transpose(ps[:, 5, g * S:(g + 1) * S], xb_oh[:, g * S:(g + 1) * S], ident[:, :])
                last.then_inc(M["xb_ohT_psum"], 1)

            queries_1(0)
            pe.wait_ge(M["xb_q1_done"], 2)
            pe.wait_ge(M["xb_const"], 8)
            for slot in range(-6, B * OFFSET + 4):
                if unit_at(slot, -8):
                    if slot == OFFSET + 8:
                        pe.wait_ge(M["xb_kv_done"], 3 * NC)
                        pe.wait_ge(M["xb_o_done"], 1)
                    scores_t(*unit_at(slot, -8))
                if unit_at(slot, 4):
                    if slot == OFFSET - 4:
                        pe.wait_ge(M["xb_q1_done"], 4)
                    maxima(*unit_at(slot, 4))
                if slot % 2 == 0 and unit_at(slot, 6):
                    n, u = unit_at(slot, 6)
                    k_transposes(n, u // 2)
                if slot % 8 == 5 and unit_at(slot, 0):
                    q_transpose(unit_at(slot, 0)[0])
                if unit_at(slot, -9):
                    head_sums(*unit_at(slot, -9))
                if slot in LAST_SLOTS:
                    last_rows(LAST_SLOTS[slot])
                if 41 <= slot < 45:
                    context_transposes_2(1, slot - 41)
                if 45 <= slot < 61:
                    second_keys(slot - 45)
                if slot == 65:
                    queries_1(1)
                for b in range(B):
                    if slot == OFFSET * (b + 1) + 3:
                        sums_transposes(b)
                if OFFSET <= slot < OFFSET + 8:
                    second_values(2 * (slot - OFFSET))
                    second_values(2 * (slot - OFFSET) + 1)
            for b in range(B):
                pe.wait_ge(M["xb_o_done"], b + 1)
                for kc in range(KC):
                    last = pe.transpose(ps[:, 1 + b, kc * S:(kc + 1) * S], xb_o[:, b, kc * P:(kc + 1) * P], ident[:, :])
                last.then_inc(M["xb_oT_psum"], 1)
            for b in range(B):
                pe.wait_ge(M["xb_oT_done"], b + 1)
                for kc in range(KC):
                    pe.matmul(ps[:, 3 + b, 0:D], xb_qfT[:, kc, b * S:(b + 1) * S], xb_wo[:, kc, :], start=(kc == 0), stop=False)
                pe.matmul(ps[:, 3 + b, 0:D], ones[0:1, :], xb_wo_row[:, :], start=False, stop=True).then_inc(M["y_psum"], 1)

            pe.wait_ge(M["sb_dve"], 1)
            for kc in range(KC):
                for b in range(B):
                    last = pe.transpose(ps[:, 0, (kc * B + b) * P:(kc * B + b + 1) * P], sb_h[:, b, kc * P:(kc + 1) * P], ident[:, :])
            last.then_inc(M["sb_psum"], 1)
            pe.wait_ge(M["sb_act"], 1)
            for t in range(2):
                for j in range(KC):
                    for kc in range(KC):
                        last = pe.matmul(ps[:, 1 + t, j * B * S:(j + 1) * B * S], sb_w[:, kc, t * D + j * P:t * D + (j + 1) * P], sb_hT[:, kc, :],
                                         start=(kc == 0), stop=(kc == KC - 1))
            last.then_inc(M["sb_psum"], 1)
            pe.wait_ge(M["x_updated"], 4 * B)
            for b in range(B):
                for kc in range(KC):
                    last = pe.matmul(ps[:, 3, b * D:(b + 1) * D], sb_hT[:, kc, b * S:(b + 1) * S], sb_w[:, kc, 2 * D:3 * D], start=(kc == 0), stop=(kc == KC - 1))
            last.then_inc(M["sb_psum"], 1)
            pe.wait_ge(M["sb_act"], 3)
            for b in range(B):
                for kc in range(KC):
                    last = pe.matmul(ps[:, 4, b * S:(b + 1) * S], sb_qT[:, kc, b * S:(b + 1) * S], sb_kT[:, kc, b * S:(b + 1) * S], start=(kc == 0), stop=(kc == KC - 1))
            last.then_inc(M["sb_psum"], 1)
            pe.wait_ge(M["sb_dve"], 3)
            for b in range(B):
                last = pe.transpose(ps[:, 5, b * S:(b + 1) * S], sb_s[:, b, :], ident[:, :])
            last.then_inc(M["sb_psum"], 1)
            pe.wait_ge(M["sb_act"], 6)
            pe.wait_ge(M["sb_act"], 4)
            for kc in range(KC):
                for b in range(B):
                    last = pe.matmul(ps[:, 6, (kc * B + b) * S:(kc * B + b + 1) * S], sb_v[:, b, kc * P:(kc + 1) * P], sb_pT[:, b, :], start=True, stop=True)
            last.then_inc(M["sb_psum"], 1)
            pe.wait_ge(M["sb_act"], 7)
            for b in range(B):
                for kc in range(KC):
                    last = pe.matmul(ps[:, 7, b * D:(b + 1) * D], sb_oT[:, kc, b * S:(b + 1) * S], sb_wo[:, kc, :], start=(kc == 0), stop=(kc == KC - 1))
                last.then_inc(M["y_psum"], 1)

            pe.wait_ge(M["mo_r_loaded"], 32)
            for kc in range(KC):
                last = pe.transpose(ps[:, 1, kc * E:(kc + 1) * E], mo_r[:, kc * P:(kc + 1) * P], ident[0:E, 0:E])
            last.then_inc(M["mo_psum"], 1)
            xn_transposes(5)
            pe.wait_ge(M["xnT_ready"], 4)
            pe.wait_ge(M["mo_act"], 1)
            for b in range(B):
                for kc in range(KC):
                    last = pe.matmul(ps[:, 2, b * E:(b + 1) * E], xnT[:, kc, b * S:(b + 1) * S], mo_rT[:, kc, :], start=(kc == 0), stop=(kc == KC - 1))
            last.then_inc(M["mo_psum"], 1)
            SPLIT = ((0, 0), (0, 1), (1, 0))

            def gate_and_up(e):
                pe.wait_ge(M["mo_w_low"], 2 * (e + 1))
                if e >= 2:
                    pe.wait_ge(M["mo_a_done"], e - 1)
                w, x = (mo_w_hi, mo_w_lo), (mo_x_hi, mo_x_lo)
                for t in range(2):
                    for ic in range(IC):
                        for kc in range(KC):
                            for k, (p, q) in enumerate(SPLIT):
                                last = pe.matmul(ps[0:IP, 3 + 2 * (e % 2) + t, ic * B * S:(ic + 1) * B * S], w[p][:, e % 3, t, kc, ic * IP:(ic + 1) * IP], x[q][:, kc, :],
                                                 start=(kc == 0 and k == 0), stop=(kc == KC - 1 and k == 2))
                last.then_inc(M["mo_gu_psum"], 1)

            def down(e):
                pe.wait_ge(M["mo_a_lo_done"], e + 1)
                pe.wait_ge(M["mo_d_low"], e + 1)
                if e == 2:
                    pe.wait_ge(M["mo_centred"], 1)
                if e == 1:
                    pe.wait_ge(M["x_updated"], 5 * B)
                if e >= 4:
                    pe.wait_ge(M["mo_y_done"], B * (e - 3))
                a_parts, d_parts = (mo_a_hi, mo_a_lo), (mo_d_hi[:, e % 2, :, :], mo_d_lo[e % 2])
                for b in range(B):
                    for ic in range(IC):
                        for k, (p, q) in enumerate(SPLIT):
                            last = pe.matmul(ps[:, Y_BANKS[e % 4], b * D:(b + 1) * D], a_parts[p][:, e % 3, ic, b * S:(b + 1) * S], d_parts[q][:, ic, :],
                                             start=(ic == 0 and k == 0), stop=(ic == IC - 1 and k == 2))
                last.then_inc(M["mo_y_psum"], 1)

            pe.wait_ge(M["mo_x_split"], 2)
            for e in range(E + 2):
                if e < E:
                    gate_and_up(e)
                if e >= 2:
                    down(e - 2)


def kernel(**inputs):
    import concourse.bacc as bacc
    from concourse.bass_utils import run_bass_kernel_spmd

    nc = bacc.Bacc("TRN2", target_bir_lowering=False, num_devices=1)
    arrays, args = {}, {}
    for name, value in inputs.items():
        value = np.ascontiguousarray(value)
        arrays[f"in_{name}"] = value
        args[name] = nc.dram_tensor(f"in_{name}", value.shape, mybir.dt.from_np(value.dtype), kind="ExternalInput").ap()
    out = nc.dram_tensor("out", inputs["x"].shape, F32, kind="ExternalOutput").ap()
    build(nc, args, out)
    return run_bass_kernel_spmd(nc, [arrays], core_ids=[0]).results[0]["out"]
```
